# Optimizing a Trainium2 kernel written in Bass

```python
import numpy as np
import jax
import jax.numpy as jnp

def _softmax(x, axis=-1):
    return jax.nn.softmax(x, axis=axis)

def _gelu(x):
    return jax.nn.gelu(x, approximate=True)

def _silu(x):
    return jax.nn.silu(x)

def _sigmoid(x):
    return jax.nn.sigmoid(x)

def _layernorm(x, axis=-1, eps=1e-05):
    m = jnp.mean(x, axis=axis, keepdims=True)
    v = jnp.var(x, axis=axis, keepdims=True)
    return (x - m) / jnp.sqrt(v + eps)

def _scatter_add(tgt, idx, src, axis=0):
    return tgt.at[idx].add(src)

def _segment_sum(src, seg, n):
    return jax.ops.segment_sum(src, seg, n)
kernel_name = 'mk_flamingo_gated_d4_seqx_r4_345956'

def setup_inputs(seed: int=0):
    np.random.seed(seed)
    _w = jnp.asarray

    def _rec_inputs():
        import jax
        import jax.numpy as jnp
        _rk = jax.random.key(seed)
        x = -0.000125 + 0.9999 * jax.random.normal(jax.random.fold_in(_rk, 1), (2, 1024, 256), jnp.float32)
        _lenS = 1024 - jax.random.randint(jax.random.fold_in(_rk, 7), (2,), 0, max(1, 1024 // 4) + 1, jnp.int32)
        _lenS2 = 64 - jax.random.randint(jax.random.fold_in(_rk, 8), (2,), 0, max(1, 64 // 4) + 1, jnp.int32)
        _ctx_1024P = jax.random.normal(jax.random.fold_in(_rk, 11), (2, 16, 256), jnp.float32)
        _ctx_1024c = jax.random.dirichlet(jax.random.fold_in(_rk, 511), 0.3 * jnp.ones((16,), jnp.float32), (2, 64))
        _ctx_1024t = jnp.einsum('bsk,bkd->bsd', _ctx_1024c, _ctx_1024P)
        _ctx_1024t = _ctx_1024t * jax.lax.rsqrt(jnp.mean(jnp.square(_ctx_1024t)) + 1e-12) * 0.953939
        ctx_1024 = -1.52775e-05 + 0.999936 * (_ctx_1024t + 0.3 * jax.random.normal(jax.random.fold_in(_rk, 611), (2, 64, 256), jnp.float32))
        _validS = jnp.arange(1024)[None, :] < _lenS[:, None]
        _validS2 = jnp.arange(64)[None, :] < _lenS2[:, None]
        _causal = jnp.tril(jnp.ones((1024, 1024), dtype=bool))
        mask_BxS2_bf1 = jnp.ones((2, 64), dtype=bool)
        mask_SxS2_bk1 = jnp.broadcast_to(_validS2[0:1, :], (1024, 64))
        mask_BxSxS2_ik1 = jnp.where(jnp.broadcast_to(_validS2[:, None, :], (2, 1024, 64)), 1, 0).astype(jnp.int32)
        _g = jax.random.normal(jax.random.fold_in(_rk, 9001), (2, 4), jnp.float32)
        _g = jnp.sign(_g) * jnp.maximum(jnp.abs(_g), 1.0) + (_g == 0) * 1.0
        g_xattn = _g[0]
        g_ffn = _g[1]
        return (x, ctx_1024, mask_BxS2_bf1, mask_SxS2_bk1, mask_BxSxS2_ik1, g_xattn, g_ffn)
    x, ctx_1024, mask_BxS2_bf1, mask_SxS2_bk1, mask_BxSxS2_ik1, g_xattn, g_ffn = _rec_inputs()

    def _L0_xattn_setup():
        import jax, jax.numpy as jnp
        import numpy as np
        DIM = 256
        EPS_DENOM = 1e-06
        EPS_LN = 1e-05

        def _layernorm(x, gamma, beta):
            mu = jnp.mean(x, axis=-1, keepdims=True)
            var = jnp.var(x, axis=-1, keepdims=True)
            return (x - mu) * jax.lax.rsqrt(var + EPS_LN) * gamma + beta
        key = jax.random.key(seed)
        ks = jax.random.split(key, 12)
        B, T, D = (8, 1024, DIM)
        s = 1.0 / np.sqrt(D)
        return {'audio': jax.random.normal(ks[0], (B, T, D), jnp.float32), 'video': jax.random.normal(ks[1], (B, T, D), jnp.float32), 'Wq': jax.random.normal(ks[2], (D, D), jnp.float32) * s, 'bq': jax.random.normal(ks[3], (D,), jnp.float32) * 0.02, 'Wk': jax.random.normal(ks[4], (D, D), jnp.float32) * s, 'bk': jax.random.normal(ks[5], (D,), jnp.float32) * 0.02, 'Wv': jax.random.normal(ks[6], (D, D), jnp.float32) * s, 'bv': jax.random.normal(ks[7], (D,), jnp.float32) * 0.02, 'Wo': jax.random.normal(ks[8], (D, D), jnp.float32) * s, 'bo': jax.random.normal(ks[9], (D,), jnp.float32) * 0.02, 'gamma': jnp.ones((D,), jnp.float32), 'beta': jnp.zeros((D,), jnp.float32)}
    _L0_xattn_all = _L0_xattn_setup()
    _L0_xattn_in = {k: v for k, v in _L0_xattn_all.items() if k in ('Wq', 'bq', 'Wk', 'bk', 'Wv', 'bv', 'Wo', 'bo', 'gamma', 'beta')}
    del _L0_xattn_all

    def _L0_ffn_setup():
        import jax, jax.numpy as jnp
        import numpy as np
        H, E, DFF = (256, 8, 1024)
        key = jax.random.key(seed)
        ks = jax.random.split(key, 7)
        s = lambda *shape: 1.0 / np.sqrt(shape[-2] if len(shape) > 1 else shape[-1])
        x = jax.random.normal(ks[0], (2, 512, H), dtype=jnp.float32)
        Wr = jax.random.normal(ks[1], (H, E), dtype=jnp.float32) * (1.0 / np.sqrt(H))
        br = jnp.zeros((E,), dtype=jnp.float32)
        W1 = jax.random.normal(ks[2], (E, H, DFF), dtype=jnp.float32) * (1.0 / np.sqrt(H))
        b1 = jnp.zeros((E, DFF), dtype=jnp.float32)
        W2 = jax.random.normal(ks[3], (E, DFF, H), dtype=jnp.float32) * (1.0 / np.sqrt(DFF))
        b2 = jnp.zeros((E, H), dtype=jnp.float32)
        return {'x': x, 'Wr': Wr, 'br': br, 'W1': W1, 'b1': b1, 'W2': W2, 'b2': b2}
    _L0_ffn_all = _L0_ffn_setup()
    _L0_ffn_in = {k: v for k, v in _L0_ffn_all.items() if k in ('Wr', 'br', 'W1', 'b1', 'W2', 'b2')}
    del _L0_ffn_all

    def _L1_xattn_setup():
        import jax, jax.numpy as jnp
        import numpy as np
        D_MODEL = 256
        N_HEADS = 16
        HEAD_DIM = D_MODEL // N_HEADS
        key = jax.random.key(seed)
        ks = jax.random.split(key, 11)
        B, Q, K = (4, 512, 512)
        s = 1.0 / np.sqrt(D_MODEL)
        inp = {'q': jax.random.normal(ks[0], (B, Q, D_MODEL), jnp.float32), 'k': jax.random.normal(ks[1], (B, K, D_MODEL), jnp.float32), 'v': jax.random.normal(ks[2], (B, K, D_MODEL), jnp.float32), 'kv_mask': jnp.ones((B, K), dtype=bool), 'Wq': jax.random.normal(ks[3], (D_MODEL, D_MODEL), jnp.float32) * s, 'bq': jnp.zeros((D_MODEL,), jnp.float32), 'Wk': jax.random.normal(ks[4], (D_MODEL, D_MODEL), jnp.float32) * s, 'bk': jnp.zeros((D_MODEL,), jnp.float32), 'Wv': jax.random.normal(ks[5], (D_MODEL, D_MODEL), jnp.float32) * s, 'bv': jnp.zeros((D_MODEL,), jnp.float32), 'Wo': jax.random.normal(ks[6], (D_MODEL, D_MODEL), jnp.float32) * s, 'bo': jnp.zeros((D_MODEL,), jnp.float32)}
        return inp
    _L1_xattn_all = _L1_xattn_setup()
    _L1_xattn_in = {k: v for k, v in _L1_xattn_all.items() if k in ('Wq', 'bq', 'Wk', 'bk', 'Wv', 'bv', 'Wo', 'bo')}
    del _L1_xattn_all

    def _L1_ffn_setup():
        import jax, jax.numpy as jnp
        import numpy as np
        NUM_EXPERTS = 8
        HIDDEN = 256
        FFN = 1024
        BATCH = 2
        SEQ = 512
        key = jax.random.key(seed)
        k_x, k_g, k_u, k_d = jax.random.split(key, 4)
        scale_in = 1.0 / np.sqrt(HIDDEN)
        scale_mid = 1.0 / np.sqrt(FFN)
        return {'hidden_states': jax.random.normal(k_x, (BATCH, SEQ, HIDDEN), dtype=jnp.float32), 'Wg': jax.random.normal(k_g, (NUM_EXPERTS, HIDDEN, FFN), dtype=jnp.float32) * scale_in, 'Wu': jax.random.normal(k_u, (NUM_EXPERTS, HIDDEN, FFN), dtype=jnp.float32) * scale_in, 'Wd': jax.random.normal(k_d, (NUM_EXPERTS, FFN, HIDDEN), dtype=jnp.float32) * scale_mid}
    _L1_ffn_all = _L1_ffn_setup()
    _L1_ffn_in = {k: v for k, v in _L1_ffn_all.items() if k in ('Wg', 'Wu', 'Wd')}
    del _L1_ffn_all

    def _L2_xattn_setup():
        import jax, jax.numpy as jnp
        import numpy as np
        B, S, D, H = (4, 512, 256, 16)
        HD = D // H
        key = jax.random.key(seed)
        ks = jax.random.split(key, 16)
        inv = 1.0 / np.sqrt(D)
        inv_hd = 1.0 / np.sqrt(D)
        inp = {'query': jax.random.normal(ks[0], (B, S, D), jnp.float32), 'key': jax.random.normal(ks[1], (B, S, D), jnp.float32), 'value': jax.random.normal(ks[2], (B, S, D), jnp.float32), 'mask': jnp.triu(jnp.ones((S, S), jnp.bool_), k=1), 'Wq': jax.random.normal(ks[3], (D, D), jnp.float32) * inv, 'Wk': jax.random.normal(ks[4], (D, D), jnp.float32) * inv, 'Wv': jax.random.normal(ks[5], (D, D), jnp.float32) * inv, 'wq_h': jax.random.normal(ks[6], (D, HD), jnp.float32) * inv_hd, 'bq_h': jax.random.normal(ks[7], (HD,), jnp.float32) * inv_hd, 'wk_h': jax.random.normal(ks[8], (D, HD), jnp.float32) * inv_hd, 'bk_h': jax.random.normal(ks[9], (HD,), jnp.float32) * inv_hd, 'wv_h': jax.random.normal(ks[10], (D, HD), jnp.float32) * inv_hd, 'bv_h': jax.random.normal(ks[11], (HD,), jnp.float32) * inv_hd, 'Wo': jax.random.normal(ks[12], (D, D), jnp.float32) * inv}
        return inp
    _L2_xattn_all = _L2_xattn_setup()
    _L2_xattn_in = {k: v for k, v in _L2_xattn_all.items() if k in ('Wq', 'Wk', 'Wv', 'wq_h', 'bq_h', 'wk_h', 'bk_h', 'wv_h', 'bv_h', 'Wo')}
    del _L2_xattn_all

    def _L2_ffn_setup():
        import math
        import jax, jax.numpy as jnp
        import numpy as np
        NUM_EXPERTS = 8
        CAPACITY_FACTOR = 1.5
        key = jax.random.key(seed)
        ks = jax.random.split(key, 4)
        B, T, D, F, E = (4, 512, 256, 1024, NUM_EXPERTS)
        scale = 0.02
        return {'x': jax.random.normal(ks[0], (B, T, D), dtype=jnp.float32), 'router_w': jax.random.normal(ks[1], (E, D), dtype=jnp.float32) * scale, 'w1': jax.random.normal(ks[2], (E, D, F), dtype=jnp.float32) * scale, 'b1': jnp.zeros((E, F), dtype=jnp.float32), 'w2': jax.random.normal(ks[3], (E, F, D), dtype=jnp.float32) * scale, 'b2': jnp.zeros((E, D), dtype=jnp.float32)}
    _L2_ffn_all = _L2_ffn_setup()
    _L2_ffn_in = {k: v for k, v in _L2_ffn_all.items() if k in ('router_w', 'w1', 'b1', 'w2', 'b2')}
    del _L2_ffn_all

    def _L3_xattn_setup():
        import jax, jax.numpy as jnp
        import numpy as np
        B, S, D, H = (2, 512, 256, 16)
        HD = D // H
        key = jax.random.key(seed)
        ks = jax.random.split(key, 12)
        s = 1.0 / np.sqrt(D)
        return {'query': jax.random.normal(ks[0], (B, S, D), jnp.float32), 'key': jax.random.normal(ks[1], (B, S, D), jnp.float32), 'value': jax.random.normal(ks[2], (B, S, D), jnp.float32), 'mask': jax.random.randint(ks[3], (B, S, S), 0, 2, jnp.int32), 'wq_kernel': jax.random.normal(ks[4], (D, D), jnp.float32) * s, 'wq_bias': jnp.zeros((D,), jnp.float32), 'wk_kernel': jax.random.normal(ks[5], (D, D), jnp.float32) * s, 'wk_bias': jnp.zeros((D,), jnp.float32), 'wv_kernel': jax.random.normal(ks[6], (D, D), jnp.float32) * s, 'wv_bias': jnp.zeros((D,), jnp.float32), 'wo_kernel': jax.random.normal(ks[7], (D, D), jnp.float32) * s, 'wo_bias': jnp.zeros((D,), jnp.float32)}
    _L3_xattn_all = _L3_xattn_setup()
    _L3_xattn_in = {k: v for k, v in _L3_xattn_all.items() if k in ('wq_kernel', 'wq_bias', 'wk_kernel', 'wk_bias', 'wv_kernel', 'wv_bias', 'wo_kernel', 'wo_bias')}
    del _L3_xattn_all

    def _L3_ffn_setup():
        import jax, jax.numpy as jnp
        import numpy as np
        D_MODEL = 256
        FF = 1024
        E = 8
        TOP_K = 2
        CAP_FACTOR = 1.25
        B, T = (4, 512)

        def _moe_forward(x, gate_w, gate_b, w1, b1, w2, b2):
            Bb, Tt, d = x.shape
            S = Bb * Tt
            C = int(CAP_FACTOR * S / E)
            xf = x.reshape(S, d)
            logits = xf @ gate_w + gate_b
            probs = jax.nn.softmax(logits, axis=1)
            topk_p, topk_i = jax.lax.top_k(probs, TOP_K)
            topk_pn = topk_p / jnp.sum(topk_p, axis=1, keepdims=True)
            rows = jnp.arange(S)
            w_te = jnp.zeros((S, E), xf.dtype).at[rows[:, None], topk_i].set(topk_pn)
            mask = jnp.zeros((S, E), bool).at[rows[:, None], topk_i].set(True)
            rank = jnp.cumsum(mask.astype(jnp.int32), axis=0)
            slot = jnp.where(mask & (rank <= C), rank - 1, C)
            e_grid = jnp.broadcast_to(jnp.arange(E), (S, E))
            t_grid = jnp.broadcast_to(rows[:, None], (S, E))
            buf = jnp.full((E, C + 1), S, jnp.int32).at[e_grid, slot].set(t_grid)
            idx = buf[:, :C]
            valid = idx < S
            x_pad = jnp.concatenate([xf, jnp.zeros((1, d), xf.dtype)], axis=0)
            xin = x_pad[idx]
            h = jax.nn.relu(jnp.einsum('ecd,edh->ech', xin, w1) + b1[:, None, :])
            out = jnp.einsum('ech,ehd->ecd', h, w2) + b2[:, None, :]
            w_pad = jnp.concatenate([w_te, jnp.zeros((1, E), xf.dtype)], axis=0)
            tok_w = w_pad[idx, jnp.arange(E)[:, None]]
            out = out * jnp.where(valid, tok_w, 0.0)[:, :, None]
            final = jnp.zeros((S + 1, d), xf.dtype).at[idx.reshape(-1)].add(out.reshape(-1, d))[:S]
            return final.reshape(Bb, Tt, d)
        key = jax.random.key(seed)
        ks = jax.random.split(key, 7)
        s = 0.02
        return {'x': jax.random.normal(ks[0], (B, T, D_MODEL), jnp.float32), 'gate_w': jax.random.normal(ks[1], (D_MODEL, E), jnp.float32) * s, 'gate_b': jnp.zeros((E,), jnp.float32), 'w1': jax.random.normal(ks[2], (E, D_MODEL, FF), jnp.float32) * s, 'b1': jnp.zeros((E, FF), jnp.float32), 'w2': jax.random.normal(ks[3], (E, FF, D_MODEL), jnp.float32) * s, 'b2': jnp.zeros((E, D_MODEL), jnp.float32)}
    _L3_ffn_all = _L3_ffn_setup()
    _L3_ffn_in = {k: v for k, v in _L3_ffn_all.items() if k in ('gate_w', 'gate_b', 'w1', 'b1', 'w2', 'b2')}
    del _L3_ffn_all
    return {'x': x, 'ctx_1024': ctx_1024, 'mask_BxS2_bf1': mask_BxS2_bf1, 'mask_SxS2_bk1': mask_SxS2_bk1, 'mask_BxSxS2_ik1': mask_BxSxS2_ik1, 'g_xattn': g_xattn, 'g_ffn': g_ffn, 'L0_xattn_Wq': _L0_xattn_in['Wq'], 'L0_xattn_bq': _L0_xattn_in['bq'], 'L0_xattn_Wk': _L0_xattn_in['Wk'], 'L0_xattn_bk': _L0_xattn_in['bk'], 'L0_xattn_Wv': _L0_xattn_in['Wv'], 'L0_xattn_bv': _L0_xattn_in['bv'], 'L0_xattn_Wo': _L0_xattn_in['Wo'], 'L0_xattn_bo': _L0_xattn_in['bo'], 'L0_xattn_gamma': _L0_xattn_in['gamma'], 'L0_xattn_beta': _L0_xattn_in['beta'], 'L0_ffn_Wr': _L0_ffn_in['Wr'], 'L0_ffn_br': _L0_ffn_in['br'], 'L0_ffn_W1': _L0_ffn_in['W1'], 'L0_ffn_b1': _L0_ffn_in['b1'], 'L0_ffn_W2': _L0_ffn_in['W2'], 'L0_ffn_b2': _L0_ffn_in['b2'], 'L1_xattn_Wq': _L1_xattn_in['Wq'], 'L1_xattn_bq': _L1_xattn_in['bq'], 'L1_xattn_Wk': _L1_xattn_in['Wk'], 'L1_xattn_bk': _L1_xattn_in['bk'], 'L1_xattn_Wv': _L1_xattn_in['Wv'], 'L1_xattn_bv': _L1_xattn_in['bv'], 'L1_xattn_Wo': _L1_xattn_in['Wo'], 'L1_xattn_bo': _L1_xattn_in['bo'], 'L1_ffn_Wg': _L1_ffn_in['Wg'], 'L1_ffn_Wu': _L1_ffn_in['Wu'], 'L1_ffn_Wd': _L1_ffn_in['Wd'], 'L2_xattn_Wq': _L2_xattn_in['Wq'], 'L2_xattn_Wk': _L2_xattn_in['Wk'], 'L2_xattn_Wv': _L2_xattn_in['Wv'], 'L2_xattn_wq_h': _L2_xattn_in['wq_h'], 'L2_xattn_bq_h': _L2_xattn_in['bq_h'], 'L2_xattn_wk_h': _L2_xattn_in['wk_h'], 'L2_xattn_bk_h': _L2_xattn_in['bk_h'], 'L2_xattn_wv_h': _L2_xattn_in['wv_h'], 'L2_xattn_bv_h': _L2_xattn_in['bv_h'], 'L2_xattn_Wo': _L2_xattn_in['Wo'], 'L2_ffn_router_w': _L2_ffn_in['router_w'], 'L2_ffn_w1': _L2_ffn_in['w1'], 'L2_ffn_b1': _L2_ffn_in['b1'], 'L2_ffn_w2': _L2_ffn_in['w2'], 'L2_ffn_b2': _L2_ffn_in['b2'], 'L3_xattn_wq_kernel': _L3_xattn_in['wq_kernel'], 'L3_xattn_wq_bias': _L3_xattn_in['wq_bias'], 'L3_xattn_wk_kernel': _L3_xattn_in['wk_kernel'], 'L3_xattn_wk_bias': _L3_xattn_in['wk_bias'], 'L3_xattn_wv_kernel': _L3_xattn_in['wv_kernel'], 'L3_xattn_wv_bias': _L3_xattn_in['wv_bias'], 'L3_xattn_wo_kernel': _L3_xattn_in['wo_kernel'], 'L3_xattn_wo_bias': _L3_xattn_in['wo_bias'], 'L3_ffn_gate_w': _L3_ffn_in['gate_w'], 'L3_ffn_gate_b': _L3_ffn_in['gate_b'], 'L3_ffn_w1': _L3_ffn_in['w1'], 'L3_ffn_b1': _L3_ffn_in['b1'], 'L3_ffn_w2': _L3_ffn_in['w2'], 'L3_ffn_b2': _L3_ffn_in['b2']}

def reference(x, ctx_1024, mask_BxS2_bf1, mask_SxS2_bk1, mask_BxSxS2_ik1, g_xattn, g_ffn, L0_xattn_Wq, L0_xattn_bq, L0_xattn_Wk, L0_xattn_bk, L0_xattn_Wv, L0_xattn_bv, L0_xattn_Wo, L0_xattn_bo, L0_xattn_gamma, L0_xattn_beta, L0_ffn_Wr, L0_ffn_br, L0_ffn_W1, L0_ffn_b1, L0_ffn_W2, L0_ffn_b2, L1_xattn_Wq, L1_xattn_bq, L1_xattn_Wk, L1_xattn_bk, L1_xattn_Wv, L1_xattn_bv, L1_xattn_Wo, L1_xattn_bo, L1_ffn_Wg, L1_ffn_Wu, L1_ffn_Wd, L2_xattn_Wq, L2_xattn_Wk, L2_xattn_Wv, L2_xattn_wq_h, L2_xattn_bq_h, L2_xattn_wk_h, L2_xattn_bk_h, L2_xattn_wv_h, L2_xattn_bv_h, L2_xattn_Wo, L2_ffn_router_w, L2_ffn_w1, L2_ffn_b1, L2_ffn_w2, L2_ffn_b2, L3_xattn_wq_kernel, L3_xattn_wq_bias, L3_xattn_wk_kernel, L3_xattn_wk_bias, L3_xattn_wv_kernel, L3_xattn_wv_bias, L3_xattn_wo_kernel, L3_xattn_wo_bias, L3_ffn_gate_w, L3_ffn_gate_b, L3_ffn_w1, L3_ffn_b1, L3_ffn_w2, L3_ffn_b2):
    import jax
    import jax.numpy as jnp

    def _L0_xattn_ref(audio, video, Wq, bq, Wk, bk, Wv, bv, Wo, bo, gamma, beta):
        import jax, jax.numpy as jnp
        import numpy as np
        DIM = 256
        EPS_DENOM = 1e-06
        EPS_LN = 1e-05

        def _layernorm(x, gamma, beta):
            mu = jnp.mean(x, axis=-1, keepdims=True)
            var = jnp.var(x, axis=-1, keepdims=True)
            return (x - mu) * jax.lax.rsqrt(var + EPS_LN) * gamma + beta
        Q = audio @ Wq.T + bq
        K = video @ Wk.T + bk
        V = video @ Wv.T + bv
        Q = jax.nn.elu(Q) + 1.0
        K = jax.nn.elu(K) + 1.0
        KV = jnp.einsum('btd,bte->bde', K, V)
        K_sum = K.sum(axis=1)
        attn_num = jnp.einsum('btd,bde->bte', Q, KV)
        attn_denom = Q * K_sum[:, None, :] + EPS_DENOM
        attn_out = attn_num / attn_denom
        attn_out = attn_out @ Wo.T + bo
        return _layernorm(audio + attn_out, gamma, beta)

    def _L0_ffn_ref(x, Wr, br, W1, b1, W2, b2):
        import jax, jax.numpy as jnp
        import numpy as np
        H, E, DFF = (256, 8, 1024)
        B, S, Hd = x.shape
        n_exp = W1.shape[0]
        xt = x.reshape(-1, Hd)
        logits = xt @ Wr + br
        probs = jax.nn.softmax(logits, axis=-1)
        gate = jnp.max(probs, axis=-1)
        idx = jnp.argmax(probs, axis=-1)
        h1 = jnp.maximum(jnp.einsum('th,ehf->etf', xt, W1) + b1[:, None, :], 0.0)
        ye = jnp.einsum('etf,efh->eth', h1, W2) + b2[:, None, :]
        onehot = jax.nn.one_hot(idx, n_exp, dtype=xt.dtype)
        y = jnp.einsum('te,eth->th', onehot, ye) * gate[:, None]
        return y.reshape(B, S, Hd)

    def _L1_xattn_ref(q, k, v, kv_mask, Wq, bq, Wk, bk, Wv, bv, Wo, bo):
        import jax, jax.numpy as jnp
        import numpy as np
        D_MODEL = 256
        N_HEADS = 16
        HEAD_DIM = D_MODEL // N_HEADS
        B, Qlen, _ = q.shape
        Klen = k.shape[1]
        qh = (q @ Wq.T + bq).reshape(B, Qlen, N_HEADS, HEAD_DIM).transpose(0, 2, 1, 3)
        kh = (k @ Wk.T + bk).reshape(B, Klen, N_HEADS, HEAD_DIM).transpose(0, 2, 1, 3)
        vh = (v @ Wv.T + bv).reshape(B, Klen, N_HEADS, HEAD_DIM).transpose(0, 2, 1, 3)
        score = jnp.einsum('bhqd,bhkd->bhqk', qh, kh) / np.sqrt(HEAD_DIM).astype(np.float32)
        score = jnp.where(kv_mask[:, None, None, :], score, jnp.float32(-10000.0))
        attn = jax.nn.softmax(score, axis=-1)
        out = jnp.einsum('bhqk,bhkd->bhqd', attn, vh)
        out = out.transpose(0, 2, 1, 3).reshape(B, Qlen, D_MODEL)
        return out @ Wo.T + bo

    def _L1_ffn_ref(hidden_states, Wg, Wu, Wd):
        import jax, jax.numpy as jnp
        import numpy as np
        NUM_EXPERTS = 8
        HIDDEN = 256
        FFN = 1024
        BATCH = 2
        SEQ = 512
        B, S, H = hidden_states.shape
        x = hidden_states.reshape(-1, H)

        def expert_step(acc, w):
            wg, wu, wd = w
            h = jax.nn.silu(x @ wg) * (x @ wu)
            return (acc + h @ wd, None)
        acc, _ = jax.lax.scan(expert_step, jnp.zeros_like(x), (Wg, Wu, Wd))
        return acc.reshape(B, S, H)

    def _L2_xattn_ref(query, key, value, mask, Wq, Wk, Wv, wq_h, bq_h, wk_h, bk_h, wv_h, bv_h, Wo):
        import jax, jax.numpy as jnp
        import numpy as np
        B, S, D, H = (4, 512, 256, 16)
        HD = D // H
        q = jnp.einsum('bsd,de->bse', query, Wq)
        k = jnp.einsum('bsd,de->bse', key, Wk)
        v = jnp.einsum('bsd,de->bse', value, Wv)
        qh = jnp.einsum('bsd,dh->bsh', q, wq_h) + bq_h
        kh = jnp.einsum('bsd,dh->bsh', k, wk_h) + bk_h
        vh = jnp.einsum('bsd,dh->bsh', v, wv_h) + bv_h
        scores = jnp.einsum('bsh,bth->bst', qh, kh) / jnp.sqrt(jnp.float32(HD))
        scores = jnp.where(mask, jnp.float32(-1000000000.0), scores)
        attn = jax.nn.softmax(scores, axis=-1)
        out_h = jnp.einsum('bst,bth->bsh', attn, vh)
        out = jnp.tile(out_h, (1, 1, H))
        return jnp.einsum('bsd,de->bse', out, Wo)

    def _L2_ffn_ref(x, router_w, w1, b1, w2, b2):
        import math
        import jax, jax.numpy as jnp
        import numpy as np
        NUM_EXPERTS = 8
        CAPACITY_FACTOR = 1.5
        B, T, D = x.shape
        E = router_w.shape[0]
        N = B * T
        C = max(math.ceil(CAPACITY_FACTOR * N / E), 1)
        x_flat = x.reshape(N, D)
        logits = x_flat @ router_w.T
        probs = jax.nn.softmax(logits, axis=-1)
        chosen_e = jnp.argmax(probs, axis=-1)
        chosen_p = jnp.max(probs, axis=-1)
        onehot = jax.nn.one_hot(chosen_e, E, dtype=jnp.float32)
        pos = jnp.take_along_axis(jnp.cumsum(onehot, axis=0), chosen_e[:, None], axis=1)[:, 0] - 1.0
        pos = pos.astype(jnp.int32)
        kept = pos < C
        pos_c = jnp.clip(pos, 0, C - 1)
        buf = jnp.zeros((E, C, D), dtype=x.dtype).at[chosen_e, pos_c].add(x_flat * kept[:, None].astype(x.dtype))
        h = jax.nn.gelu(jnp.einsum('ecd,edf->ecf', buf, w1) + b1[:, None, :], approximate=False)
        eo = jnp.einsum('ecf,efd->ecd', h, w2) + b2[:, None, :]
        y = eo[chosen_e, pos_c] * (chosen_p * kept.astype(x.dtype))[:, None]
        return y.reshape(B, T, D)

    def _L3_xattn_ref(query, key, value, mask, wq_kernel, wq_bias, wk_kernel, wk_bias, wv_kernel, wv_bias, wo_kernel, wo_bias):
        import jax, jax.numpy as jnp
        import numpy as np
        B, S, D, H = (2, 512, 256, 16)
        HD = D // H
        b = query.shape[0]

        def split_heads(x):
            return x.reshape(b, -1, H, HD).transpose(0, 2, 1, 3)
        q = split_heads(query @ wq_kernel + wq_bias)
        k = split_heads(key @ wk_kernel + wk_bias)
        v = split_heads(value @ wv_kernel + wv_bias)
        scores = jnp.einsum('bhqd,bhkd->bhqk', q, k) / jnp.sqrt(jnp.float32(HD))
        m = mask[:, None, :, :]
        scores = jnp.where(m == 0, jnp.float32(-1000000000.0), scores)
        attn = jax.nn.softmax(scores, axis=-1)
        out = jnp.einsum('bhqk,bhkd->bhqd', attn, v)
        out = out.transpose(0, 2, 1, 3).reshape(b, -1, D)
        return out @ wo_kernel + wo_bias

    def _L3_ffn_ref(x, gate_w, gate_b, w1, b1, w2, b2):
        import jax, jax.numpy as jnp
        import numpy as np
        D_MODEL = 256
        FF = 1024
        E = 8
        TOP_K = 2
        CAP_FACTOR = 1.25
        B, T = (4, 512)

        def _moe_forward(x, gate_w, gate_b, w1, b1, w2, b2):
            Bb, Tt, d = x.shape
            S = Bb * Tt
            C = int(CAP_FACTOR * S / E)
            xf = x.reshape(S, d)
            logits = xf @ gate_w + gate_b
            probs = jax.nn.softmax(logits, axis=1)
            topk_p, topk_i = jax.lax.top_k(probs, TOP_K)
            topk_pn = topk_p / jnp.sum(topk_p, axis=1, keepdims=True)
            rows = jnp.arange(S)
            w_te = jnp.zeros((S, E), xf.dtype).at[rows[:, None], topk_i].set(topk_pn)
            mask = jnp.zeros((S, E), bool).at[rows[:, None], topk_i].set(True)
            rank = jnp.cumsum(mask.astype(jnp.int32), axis=0)
            slot = jnp.where(mask & (rank <= C), rank - 1, C)
            e_grid = jnp.broadcast_to(jnp.arange(E), (S, E))
            t_grid = jnp.broadcast_to(rows[:, None], (S, E))
            buf = jnp.full((E, C + 1), S, jnp.int32).at[e_grid, slot].set(t_grid)
            idx = buf[:, :C]
            valid = idx < S
            x_pad = jnp.concatenate([xf, jnp.zeros((1, d), xf.dtype)], axis=0)
            xin = x_pad[idx]
            h = jax.nn.relu(jnp.einsum('ecd,edh->ech', xin, w1) + b1[:, None, :])
            out = jnp.einsum('ech,ehd->ecd', h, w2) + b2[:, None, :]
            w_pad = jnp.concatenate([w_te, jnp.zeros((1, E), xf.dtype)], axis=0)
            tok_w = w_pad[idx, jnp.arange(E)[:, None]]
            out = out * jnp.where(valid, tok_w, 0.0)[:, :, None]
            final = jnp.zeros((S + 1, d), xf.dtype).at[idx.reshape(-1)].add(out.reshape(-1, d))[:S]
            return final.reshape(Bb, Tt, d)
        return _moe_forward(x, gate_w, gate_b, w1, b1, w2, b2)
    x = x + jnp.tanh(g_xattn[0]) * _L0_xattn_ref(_layernorm(x, axis=-1), ctx_1024, L0_xattn_Wq, L0_xattn_bq, L0_xattn_Wk, L0_xattn_bk, L0_xattn_Wv, L0_xattn_bv, L0_xattn_Wo, L0_xattn_bo, L0_xattn_gamma, L0_xattn_beta)
    x = x + jnp.tanh(g_ffn[0]) * _L0_ffn_ref(_layernorm(x, axis=-1), L0_ffn_Wr, L0_ffn_br, L0_ffn_W1, L0_ffn_b1, L0_ffn_W2, L0_ffn_b2)
    x = x + jnp.tanh(g_xattn[1]) * _L1_xattn_ref(_layernorm(x, axis=-1), ctx_1024, ctx_1024, mask_BxS2_bf1, L1_xattn_Wq, L1_xattn_bq, L1_xattn_Wk, L1_xattn_bk, L1_xattn_Wv, L1_xattn_bv, L1_xattn_Wo, L1_xattn_bo)
    x = x + jnp.tanh(g_ffn[1]) * _L1_ffn_ref(_layernorm(x, axis=-1), L1_ffn_Wg, L1_ffn_Wu, L1_ffn_Wd)
    x = x + jnp.tanh(g_xattn[2]) * _L2_xattn_ref(_layernorm(x, axis=-1), ctx_1024, ctx_1024, mask_SxS2_bk1, L2_xattn_Wq, L2_xattn_Wk, L2_xattn_Wv, L2_xattn_wq_h, L2_xattn_bq_h, L2_xattn_wk_h, L2_xattn_bk_h, L2_xattn_wv_h, L2_xattn_bv_h, L2_xattn_Wo)
    x = x + jnp.tanh(g_ffn[2]) * _L2_ffn_ref(_layernorm(x, axis=-1), L2_ffn_router_w, L2_ffn_w1, L2_ffn_b1, L2_ffn_w2, L2_ffn_b2)
    x = x + jnp.tanh(g_xattn[3]) * _L3_xattn_ref(_layernorm(x, axis=-1), ctx_1024, ctx_1024, mask_BxSxS2_ik1, L3_xattn_wq_kernel, L3_xattn_wq_bias, L3_xattn_wk_kernel, L3_xattn_wk_bias, L3_xattn_wv_kernel, L3_xattn_wv_bias, L3_xattn_wo_kernel, L3_xattn_wo_bias)
    x = x + jnp.tanh(g_ffn[3]) * _L3_ffn_ref(_layernorm(x, axis=-1), L3_ffn_gate_w, L3_ffn_gate_b, L3_ffn_w1, L3_ffn_b1, L3_ffn_w2, L3_ffn_b2)
    return x

_drawn_inputs = setup_inputs


def setup_inputs(seed=0):
    import zlib

    import numpy as np

    out = dict(_drawn_inputs(seed))
    spreads = {'L0_xattn_gamma': (1.0, 0.2),
     'L0_xattn_beta': (0.0, 0.1),
     'L0_ffn_br': (0.0, 0.1),
     'L0_ffn_b1': (0.0, 0.416),
     'L0_ffn_b2': (0.0, 0.295),
     'L1_xattn_bq': (0.0, 0.414),
     'L1_xattn_bk': (0.0, 2.0),
     'L1_xattn_bv': (0.0, 0.1),
     'L1_xattn_bo': (0.0, 0.1),
     'L2_ffn_b1': (0.0, 0.8),
     'L2_ffn_b2': (0.0, 0.8),
     'L3_xattn_wq_bias': (0.0, 0.791),
     'L3_xattn_wk_bias': (0.0, 2.0),
     'L3_xattn_wv_bias': (0.0, 0.341),
     'L3_xattn_wo_bias': (0.0, 0.324),
     'L3_ffn_gate_b': (0.0, 0.302),
     'L3_ffn_b1': (0.0, 0.8),
     'L3_ffn_b2': (0.0, 0.392)}
    factors = {'L0_xattn_bq': 2.81,
     'L0_xattn_bk': 3.745,
     'L0_xattn_bo': 109.741,
     'L2_xattn_bq_h': 5.141,
     'L2_xattn_bk_h': 200.0,
     'L2_ffn_router_w': 5.448,
     'L2_ffn_w1': 7.134,
     'L2_ffn_w2': 6.745,
     'L3_ffn_w1': 3.891}
    for name, (base, spread) in spreads.items():
        noise = np.random.default_rng([zlib.crc32(name.encode()), seed]).standard_normal(out[name].shape)
        drawn = base * np.exp(spread * noise) if base else spread * noise
        out[name] = jnp.asarray(drawn.astype(out[name].dtype))
    for name, factor in factors.items():
        out[name] = (out[name] * factor).astype(out[name].dtype)
    return out
```

```python
from contextlib import ExitStack

import numpy as np

import concourse.bass as bass
from concourse import mybir

ALU = mybir.AluOpType
ACT = mybir.ActivationFunctionType
AX = mybir.AxisListType
F32 = mybir.dt.float32
F32R = mybir.dt.float32r
BF16 = mybir.dt.bfloat16
U8 = mybir.dt.uint8
I32 = mybir.dt.int32
U32 = mybir.dt.uint32

P = 128
B, SEQ, D = 2, 1024, 256
S2 = 64
T = B * SEQ
NT = T // P
TB = NT // B
KD = D // P
GROUP = 4
GT = GROUP * P
NG = NT // GROUP
H, HD = 16, 16
HC = P // HD
PAIRS = H // 2
VC = 2 * HD + 2
E = 8
F = 1024
FC = F // P
LN_EPS = 1e-5
BIG = 3.0e38
MASKED = {1: -10000.0, 2: -1.0e9, 3: -1.0e9}

HALF = F // 2
FH = HALF // P
UNITS = 2 * E
SLOTS = 3 * P
CAP = {0: 256, 2: 384, 3: 320}
ITEMS = {0: T // 256 + E - 1, 2: E, 3: E}
IR = {0: 256, 2: 384, 3: 384}
TOPK = {0: 1, 2: 1, 3: 2}
ROWS = 32 * P
FAR = float(1 << 20)
PIECE = 1024


def build(nc, a, out, subs):
    with ExitStack() as ctx:
        def sb(name, shape, dt=F32, stack=ctx):
            return stack.enter_context(nc.sbuf_tensor(name, shape, dt))

        def sem(name):
            return ctx.enter_context(nc.semaphore(name))

        xs = sb("xs", [P, NT, D])
        lnx = sb("lnx", [P, NT, D])
        xT = sb("xT", [P, KD, T])
        ident = sb("ident", [P, P])
        ones = sb("ones", [P, 1])
        eps = sb("eps", [P, 1])
        hmask = sb("hmask", [P, HC])
        zero = sb("zero", [P, 1])
        primer = sb("primer", [P, 8])
        gates = sb("gates", [P, 8])
        gates_raw = sb("gates_raw", [P, 8])
        ctx_sb = sb("ctx_sb", [P, D])
        ctxT = sb("ctxT", [P, KD, P])
        bn = sb("bn", [P, NT, 6])
        st_sum, st_dif, st_m2, st_sq, st_var, st_std, st_rstd, st_mean = (
            sb(n, [P, NT]) for n in ("st_sum", "st_dif", "st_m2", "st_sq", "st_var", "st_std", "st_rstd", "st_mean"))
        wat = sb("wat", [P, 4, KD, D])
        wraw = sb("wraw", [P, 4, PIECE])
        whi = sb("whi", [P, 2, 4, PIECE], F32R)
        wlo = sb("wlo", [P, 2, 4, PIECE], F32R)
        ps = ctx.enter_context(nc.psum_tensor("ps", [P, 8, 512], F32))

        wr = sb("wr", [P, 4, KD, E])
        rb = sb("rb", [P, 4, E])
        b1c = sb("b1c", [P, 4, E * FC])
        b2c = sb("b2c", [P, 4, E * KD])
        tri = sb("tri", [P, P], BF16)
        ones_b = sb("ones_b", [P, P], BF16)
        mask_b = sb("mask_b", [P, NT, E], BF16)
        desc = sb("desc", [P, E])
        first_row = sb("first_row", [P, E])
        r_p, r_e, r_key, r_oh1, r_oh2, r_keep, r_pos = (
            sb(n, [P, NT, E]) for n in ("r_p", "r_e", "r_key", "r_oh1", "r_oh2", "r_keep", "r_pos"))
        r_grid = sb("r_grid", [P, NT, E])
        r_count, r_items, r_upto = (sb(n, [P, E]) for n in ("r_count", "r_items", "r_upto"))
        steps = sb("steps", [P, E])
        item_no = sb("item_no", [P, NT])
        item_expert = sb("item_expert", [P, NT], I32)
        r_m, r_s, r_k = (sb(n, [P, NT]) for n in ("r_m", "r_s", "r_k"))
        r_top, r_slot, r_kept, r_w = (sb(n, [P, 2, NT]) for n in ("r_top", "r_slot", "r_kept", "r_w"))
        sidx = sb("sidx", [P, 2, NT], U32)
        gidx = sb("gidx", [P, 2, NT], U32)
        xbuf = nc.dram_tensor("xbuf", (ROWS, D), F32, kind="Internal").ap()
        ybuf = nc.dram_tensor("ybuf", (ROWS, D), F32, kind="Internal").ap()
        xflat = xT[:, :, :].rearrange("p k t -> p (k t)")
        y_t = xflat[:, 0:KD * SLOTS].rearrange("p (k t) -> p k t", k=KD)
        y_row = xflat[:, 768:2304].rearrange("p (s j d) -> p s j d", s=2, j=3)
        x_row = xflat[:, 2304:3840].rearrange("p (s j d) -> p s j d", s=2, j=3)
        y_second = xflat.rearrange("p (t d) -> p t d", t=NT)

        with ExitStack() as attn_mem:
            def asb(name, shape, dt=F32):
                return sb(name, shape, dt, attn_mem)
            brow = asb("brow", [P, 5, D])
            bcol = asb("bcol", [P, 4])
            ctxD = asb("ctxD", [P, KD, B, 2, S2])
            bmask = asb("bmask", [P, NT, S2])
            mask8 = asb("mask8", [P, TB, S2], U8)
            mask32 = asb("mask32", [P, NT, S2], I32)
            sc = asb("sc", [P, 2, H, S2])
            smax = asb("smax", [P, 2, H])
            pt = asb("pt", [P, PAIRS, P])
            rsum = asb("rsum", [P, PAIRS, 2])
            oh = asb("oh", [P, D])
            ot = asb("ot", [P, KD, P])
            mha_mem = attn_mem.enter_context(ExitStack())
            kblk = sb("kblk", [P, B, KD, HC, S2], stack=mha_mem)
            vblk = sb("vblk", [P, B, PAIRS, VC], stack=mha_mem)
            kt = sb("kt", [P, KD, P], stack=mha_mem)
            qt = sb("qt", [P, 2, KD, P], stack=mha_mem)
            mha_mem.close()
            a2_mem = attn_mem.enter_context(ExitStack())
            wh = sb("wh", [P, 3, KD, HD], stack=a2_mem)
            wqkv = sb("wqkv", [P, 3, KD, HD], stack=a2_mem)
            wo8 = sb("wo8", [P, D], stack=a2_mem)
            bh = sb("bh", [HD, 2], stack=a2_mem)
            bvh = sb("bvh", [P, HD], stack=a2_mem)
            khT = sb("khT", [HD, B, S2], stack=a2_mem)
            vh = sb("vh", [P, B, HD + 1], stack=a2_mem)
            qhT = sb("qhT", [HD, T], stack=a2_mem)
            oh8 = sb("oh8", [P, NT, HC, HD], stack=a2_mem)
            rs2 = sb("rs2", [P, 2, PAIRS], stack=a2_mem)
            ot8 = sb("ot8", [P, 2, P], stack=a2_mem)
        with ExitStack() as a0_mem:
            def asb(name, shape, dt=F32):
                return sb(name, shape, dt, a0_mem)
            brow0 = asb("brow0", [P, 5, D])
            bcol0 = asb("bcol0", [P, KD])
            k0 = asb("k0", [P, D])
            k0_min = asb("k0_min", [P, D])
            v0 = asb("v0", [P, D])
            kv0 = asb("kv0", [P, B, KD, D])
            ksum0 = asb("ksum0", [P, B, KD])
            q_min = asb("q_min", [P, KD, GT])
            q_relu = asb("q_relu", [P, KD, GT])
            q_den = asb("q_den", [P, KD, GT])
            q_o = asb("q_o", [P, KD, GT])
        xTh = sb("xTh", [P, KD, T], F32R)
        xTl = sb("xTl", [P, KD, T], F32R)
        h_act = sb("h_act", [P, 2, GT])
        h_32 = sb("h_32", [P, 2, GT])
        h_hi = sb("h_hi", [P, FH, GT], F32R)
        h_lo = sb("h_lo", [P, FH, GT], F32R)

        in_x, in_ctx, in_gate = sem("in_x"), sem("in_ctx"), sem("in_gate")
        in_wat, in_bias, in_mask = sem("in_wat"), sem("in_bias"), sem("in_mask")
        const_done, gates_done = sem("const_done"), sem("gates_done")
        ctx_tr, ctxT_done = sem("ctx_tr"), sem("ctxT_done")
        bn_done, var_done, std_done, ln_done = sem("bn_done"), sem("var_done"), sem("std_done"), sem("ln_done")
        tr_done, xt_done, xl_done = sem("tr_done"), sem("xt_done"), sem("xl_done")
        x_done, link_s, out_done = sem("x_done"), sem("link_s"), sem("out_done")
        a0_kv, a0_kmin, a0_kexp, a0_k, a0_kvcopy = (
            sem(f"a0_{n}") for n in ("kv", "kmin", "kexp", "k", "kvcopy"))
        a0_q, a0_qmin, a0_qexp, a0_den, a0_num, a0_o, a0_proj, a0_res, a0_bo, a0_gam, a0_nrm, a0_beta = (
            sem(f"a0_{n}") for n in
            ("q", "qmin", "qexp", "den", "num", "o", "proj", "res", "bo", "gam", "nrm", "beta"))
        w_in = [sem(f"w_in{q}") for q in range(4)]
        w_hi, w_lo, w_used = sem("w_hi"), sem("w_lo"), sem("w_used")
        f_up, f_act, f_h, f_hi, f_lo, f_used, f_yevac, f_back = (
            sem(f"f_{n}") for n in ("up", "act", "h", "hi", "lo", "used", "yevac", "back"))
        m_kv, m_kt, m_kblk, m_q, m_qt, m_s, m_min, m_max, m_sub, m_exp = (
            sem(f"m_{n}") for n in ("kv", "kt", "kblk", "q", "qt", "s", "min", "max", "sub", "exp"))
        m_ptr, m_pta, m_ptd, m_av, m_rs, m_oh, m_otr, m_ot, m_proj, m_bo = (
            sem(f"m_{n}") for n in ("ptr", "pta", "ptd", "av", "rs", "oh", "otr", "ot", "proj", "bo"))
        m_tab = sem("m_tab")
        in_moe, zeroed = sem("in_moe"), sem("zeroed")
        r_logits, r_sub, r_exp, r_mask, r_rank, r_idx = (sem(f"r_{n}") for n in ("logits", "sub", "exp", "mask", "rank", "idx"))
        scattered, x_tr, x_hi, x_lo, y_out, y_tr, y_copied = (
            sem(n) for n in ("scattered", "x_tr", "x_hi", "x_lo", "y_out", "y_tr", "y_copied"))
        m_act, y_half = sem("m_act"), sem("y_half")
        x_in = [sem("x_in0"), sem("x_in1")]
        y_st = [sem("y_st0"), sem("y_st1")]
        fetched = [sem(f"fetched{g}") for g in range(NG)]
        a2_pe, a2_act, a2_dve, a2_pool, in_a2 = (sem(f"a2_{n}") for n in ("pe", "act", "dve", "pool", "in"))

        def row(v, n):
            return v.rearrange("(o n) -> o n", o=1).to_broadcast([P, n])

        def col(v):
            return v

        block = ctx.enter_context(nc.Block())
        x_dram = a["x"].rearrange("b (t p) d -> p (b t) d", p=P)
        BIAS = {0: 96, 1: 64, 3: 64}
        bias_at = {0: 96, 1: 160, 3: 224}
        COUNTS = {f"ffn{l}": (4 * ITEMS[l], ITEMS[l], ITEMS[l] * FC, ITEMS[l]) for l in ITEMS}
        COUNTS["ffn1"] = (3 * UNITS, UNITS, UNITS * NG * FH, 0)
        PIECES, UNITS_BEFORE, CHUNKS, EXPERTS = {}, {}, {}, {}
        at = [0, 0, 0, 0]
        for name in subs:
            if name in COUNTS:
                PIECES[name], UNITS_BEFORE[name], CHUNKS[name], EXPERTS[name] = at
                at = [x + y for x, y in zip(at, COUNTS[name])]
        LOADS, at = {}, [0, 0, 0, 0]
        for name in subs:
            if name in COUNTS:
                LOADS[name] = list(at)
                at = [x + COUNTS[name][1] * (q < 3 or name != "ffn1") for q, x in enumerate(at)]
        MOE = [l for l in (0, 2, 3) if f"ffn{l}" in subs]
        SENT, FETCHED, MC, ROW_LOADS = {}, {}, {}, {}
        for l in MOE:
            before = [b for b in MOE if b < l]
            MC[f"ffn{l}"] = sum(ITEMS[b] * FC for b in before)
            SENT[l] = NT * sum(TOPK[b] for b in before + [l])
            FETCHED[l] = GROUP * sum(TOPK[b] for b in before + [l])
            ROW_LOADS[l] = [sum((ITEMS[b] + 1 - s) // 2 for b in before) for s in range(2)]
        PRIMED = 4
        WAT = {layer: i + 1 for i, layer in enumerate(l for l in (0, 1, 2, 3) if f"attn{l}" in subs)}
        MASKS = {layer: i + 1 for i, layer in enumerate(l for l in (1, 2, 3) if f"attn{l}" in subs)}
        N = {name: i for i, name in enumerate(subs)}

        @block.sync
        def _(sp):
            for g in range(NG):
                sp.dma_start(xs[:, g * GROUP:(g + 1) * GROUP, :], x_dram[:, g * GROUP:(g + 1) * GROUP, :]).then_inc(in_x, 16)
            sp.dma_start(ctx_sb[:, :], a["ctx_1024"].rearrange("b s d -> (b s) d")).then_inc(in_ctx, 16)
            sp.dma_start(gates_raw[:, 0:4], row(a["g_xattn"], 4)).then_inc(in_gate, 16)
            sp.dma_start(gates_raw[:, 4:8], row(a["g_ffn"], 4)).then_inc(in_gate, 16)

            def load_moe():
                for l in (0, 2, 3):
                    sp.dma_start(wr[:, l, :, :], a[f"router{l}"].rearrange("(k p) e -> p k e", p=P)).then_inc(in_moe, 16)
                    sp.dma_start(b1c[:, l, :], a[f"b1_{l}"]).then_inc(in_moe, 16)
                    sp.dma_start(b2c[:, l, :], a[f"b2_{l}"]).then_inc(in_moe, 16)
                sp.dma_start(rb[:, 0, :], row(a["L0_ffn_br"], E)).then_inc(in_moe, 16)
                sp.dma_start(rb[:, 3, :], row(a["L3_ffn_gate_b"], E)).then_inc(in_moe, 16)
                sp.wait_ge(zeroed, 1)
                for h in range(2):
                    sp.dma_start(xbuf.rearrange("(h p c) d -> h p (c d)", h=2, p=P)[h], xflat).then_inc(zeroed, 16)

            def expert_weights(layer, e, u):
                w1, w2 = a[f"L{layer}_w1"], a[f"L{layer}_w2"]
                for q in range(4):
                    sp.wait_ge(w_lo, PIECES[f"ffn{layer}"] + 4 * u + q + 1)
                    if q < 2:
                        sp.dma_start(wraw[:, q, :], w1.rearrange("e (k p) f -> e k p f", p=P)[e, q]).then_inc(w_in[q], 16)
                    else:
                        sp.dma_start(wraw[:, q, :].rearrange("p (c d) -> p c d", c=4),
                                     w2.rearrange("e (h c p) d -> e h p c d", h=2, p=P)[e, q - 2]).then_inc(w_in[q], 16)

            def moe(layer):
                name = f"ffn{layer}"
                nth = MOE.index(layer)
                items = ITEMS[layer]
                xrows = xbuf[0:items * IR[layer], :].rearrange("(e j p) d -> e p j d", e=items, p=P)
                yrows = ybuf[0:items * IR[layer], :].rearrange("(e j p) d -> e p j d", e=items, p=P)
                tiles = IR[layer] // P

                def store(e, s):
                    sp.wait_ge(y_copied, EXPERTS[name] + e + 1)
                    sp.dma_start(yrows[e], y_row[:, s, 0:tiles, :]).then_inc(y_st[s], 16)

                def weights(e):
                    if layer == 0:
                        expert_weights(layer, sp.value_load(item_expert[0:1, bass.ds(e, 1)], min_val=0, max_val=E - 1), e)
                    else:
                        expert_weights(layer, e, e)

                def step(e, s):
                    sp.wait_ge(x_tr, EXPERTS[name] + e + 1)
                    sp.dma_start(x_row[:, s, 0:tiles, :], xrows[e + 2]).then_inc(x_in[s], 16)
                    weights(e + 2)
                if layer == 0:
                    sp.wait_ge(r_idx, 1)
                    weights(1)
                sp.wait_ge(scattered, 16 * SENT[layer])
                for s in range(2):
                    sp.dma_start(x_row[:, s, 0:tiles, :], xrows[s]).then_inc(x_in[s], 16)
                even = (items - 2) // 2 * 2
                with sp.Fori(0, even - 1, 2) as e:
                    for s in range(2):
                        step(e + s, s)
                        store(e + s, s)
                for e in range(even, items):
                    if e + 2 < items:
                        step(e, e % 2)
                    store(e, e % 2)

            def load_wat(n):
                if n > 0:
                    before = max(l for l in range(n) if f"attn{l}" in N)
                    sp.wait_ge(x_done, NT * (N[f"attn{before}"] + 1))
                for i in range(4):
                    sp.dma_start(wat[:, i, :, :], a[f"attn{n}"][i].rearrange("(k p) e -> p k e", p=P)).then_inc(in_wat, 16)

            load_wat(0)
            load_moe()
            for i, n in enumerate(("bk", "bv", "bo", "gamma", "beta")):
                sp.dma_start(brow0[:, i, :], row(a["L0_xattn_" + n], D)).then_inc(in_bias, 16)
            sp.dma_start(bcol0[:, :], col(a["L0_xattn_bq"])).then_inc(in_bias, 16)

            def load_vectors(layer, n):
                sp.wait_ge(x_done, NT * n)
                for i, v in enumerate(("bv", "bo")):
                    sp.dma_start(brow[:, i, :], row(a[f"L{layer}_{v}"], D)).then_inc(in_bias, 16)
                for i, v in enumerate(("bq", "bk")):
                    sp.dma_start(bcol[:, KD * i:KD * (i + 1)], a[f"L{layer}_{v}"]).then_inc(in_bias, 16)
                if layer == 1:
                    sp.dma_start(mask8[:, 0:B, :], a["mask_BxS2_bf1"].rearrange("(o b) s -> o b s", o=1).to_broadcast([P, B, S2])).then_inc(in_mask, 16)
                else:
                    sp.dma_start(mask32[:, :, :], a["mask_BxSxS2_ik1"].rearrange("b (t p) s -> p (b t) s", p=P)).then_inc(in_mask, 16)

            def stream_ffn1():
                with sp.Fori(0, E) as e:
                    for half in range(2):
                        for q, src in enumerate((a["L1_ffn_Wg"], a["L1_ffn_Wu"], a["L1_ffn_Wd"])):
                            sp.wait_ge(w_lo, PIECES["ffn1"] + 6 * e + 3 * half + q + 2)
                            if q < 2:
                                sp.dma_start(wraw[:, q, :].rearrange("p (k f) -> p k f", k=KD),
                                             src.rearrange("e (k p) (h f) -> e h p k f", p=P, h=2)[e, half]).then_inc(w_in[q], 16)
                            else:
                                sp.dma_start(wraw[:, q, :].rearrange("p (c d) -> p c d", c=FH),
                                             src.rearrange("e (h c p) d -> e h p c d", h=2, p=P)[e, half]).then_inc(w_in[q], 16)

            def load_attn2(n):
                sp.wait_ge(x_done, NT * n)
                sp.dma_start(wh[:, :, :, :], a["attn2_heads"].rearrange("i (k p) j -> p i k j", p=P)).then_inc(in_a2, 16)
                sp.dma_start(bh[:, :], a["attn2_bias"]).then_inc(in_a2, 16)
                sp.dma_start(bvh[:, :], row(a["L2_xattn_bv_h"], HD)).then_inc(in_a2, 16)
                sp.dma_start(mask8[:, :, :], a["mask_SxS2_bk1"].rearrange("(t p) s -> p t s", p=P)).then_inc(in_mask, 16)

            if "ffn0" in N:
                expert_weights(0, 0, 0)
            if "attn1" in N:
                load_wat(1)
            if "ffn0" in N:
                moe(0)
            if "attn1" in N:
                load_vectors(1, N["attn1"])
            if "ffn1" in N:
                stream_ffn1()
            if "attn2" in N:
                load_wat(2)
                load_attn2(N["attn2"])
            for layer in (2, 3):
                if layer == 3 and "attn3" in N:
                    load_vectors(3, N["attn3"])
                if f"ffn{layer}" in N:
                    sp.wait_ge(w_lo, PRIMED + PIECES[f"ffn{layer}"])
                    for e in range(2):
                        expert_weights(layer, e, e)
                if layer == 2 and "attn3" in N:
                    load_wat(3)
                if f"ffn{layer}" in N:
                    moe(layer)

            sp.wait_ge(x_done, NT * len(subs))
            sp.dma_start(out.rearrange("b (t p) d -> p (b t) d", p=P), xs[:, :, :]).then_inc(out_done, 16)
            sp.wait_ge(out_done, 16)

        @block.gpsimd
        def _(pool):
            pool.memset(ident[:, :], 0.0).then_inc(const_done, 1)
            pool.memset(ones[:, :], 1.0).then_inc(const_done, 1)
            pool.memset(eps[:, :], LN_EPS).then_inc(const_done, 1)
            pool.memset(zero[:, :], 0.0).then_inc(const_done, 1)
            pool.memset(hmask[:, :], 0.25).then_inc(const_done, 1)
            pool.wait_ge(const_done, 5)
            pool.affine_select(out=ident[:, :], in_=ident[:, :], compare_op=ALU.not_equal, fill=1.0,
                               base=0, pattern=[[-1, P]], channel_multiplier=1).then_inc(const_done, 1)
            pool.affine_select(out=hmask[:, :], in_=hmask[:, :], compare_op=ALU.is_ge, fill=0.0,
                               base=0, pattern=[[-HD, HC]], channel_multiplier=1).then_inc(const_done, 1)
            pool.wait_ge(const_done, 7)
            pool.affine_select(out=hmask[:, :], in_=hmask[:, :], compare_op=ALU.is_ge, fill=0.0,
                               base=HD - 1, pattern=[[HD, HC]], channel_multiplier=-1).then_inc(const_done, 1)

            pool.memset(xflat, 0.0).then_inc(zeroed, 1)
            pool.memset(ones_b[:, :], 1.0).then_inc(const_done, 1)
            pool.memset(tri[:, :], 1.0).then_inc(const_done, 1)
            pool.iota(desc[:, :], pattern=[[-1, E]], base=E, channel_multiplier=0, allow_small_or_imprecise_dtypes=True).then_inc(const_done, 1)
            pool.iota(first_row[:, :], pattern=[[SLOTS, E]], base=-1, channel_multiplier=0, allow_small_or_imprecise_dtypes=True).then_inc(const_done, 1)
            pool.iota(steps[:, :], pattern=[[IR[0], E]], base=0, channel_multiplier=0, allow_small_or_imprecise_dtypes=True).then_inc(const_done, 1)
            pool.iota(item_no[:, :], pattern=[[1, NT]], base=0, channel_multiplier=0, allow_small_or_imprecise_dtypes=True).then_inc(const_done, 1)
            pool.wait_ge(const_done, 14)
            pool.memset(steps[:, 0:1], -1.0).then_inc(const_done, 1)
            pool.affine_select(out=tri[:, :], in_=tri[:, :], compare_op=ALU.is_ge, fill=0.0,
                               base=0, pattern=[[1, P]], channel_multiplier=-1).then_inc(const_done, 1)
            pool.memset(primer[:, 5:6], 0.0).then_inc(y_out, PRIMED)
            for s in range(2):
                pool.memset(primer[:, 3 + s:4 + s], 0.0).then_inc(y_st[s], 16)
            pool.memset(primer[:, 0:1], 0.0).then_inc(w_lo, PRIMED)
            pool.memset(primer[:, 1:2], 0.0).then_inc(w_used, 2)
            pool.memset(primer[:, 2:3], 0.0).then_inc(f_used, 1)

            pool.wait_ge(in_bias, bias_at[0])
            pool.wait_ge(gates_done, 1)
            pool.tensor_scalar(brow0[:, 3:5, :], brow0[:, 3:5, :], gates[:, 0:1], None, ALU.mult).then_inc(a0_beta, 1)
            pool.wait_ge(tr_done, NG)
            with pool.Fori(0, NT) as i:
                pool.tensor_tensor(lnx[:, i, :], lnx[:, i, :], brow0[:, 2, :], ALU.add).then_inc(a0_bo, 1)
            pool.wait_ge(a0_beta, 1)
            with pool.Fori(0, NT) as i:
                pool.tensor_tensor(xs[:, i, :], xs[:, i, :], brow0[:, 4, :], ALU.add).then_inc(a0_bo, 1)
            with pool.Fori(0, NT) as i:
                pool.wait_ge(a0_nrm, i + 1)
                pool.tensor_tensor(lnx[:, i, :], lnx[:, i, :], brow0[:, 3, :], ALU.mult).then_inc(a0_gam, 1)


            def mha(layer, m, n):
                pool.wait_ge(x_done, NT * n)
                for r in range(2):
                    pool.tensor_copy(ctxD[:, :, :, r, :], ctxT[:, :, :].rearrange("p k (b s) -> p k b s", b=B)).then_inc(m_tab, 1)
                pool.memset(vblk[:, :, :, :], 0.0).then_inc(m_tab, 1)
                pool.wait_ge(m_tab, 5 * m + 3)
                for r in range(2):
                    pool.memset(vblk[r * S2:(r + 1) * S2, :, :, 2 * HD + r:2 * HD + r + 1], 1.0).then_inc(m_tab, 1)
                pool.wait_ge(m_tab, 5 * m + 5)
                pool.wait_ge(in_bias, bias_at[layer])
                pool.tensor_scalar(brow[:, 2, :], brow[:, 1, :], gates[:, layer:layer + 1], None, ALU.mult).then_inc(m_bo, 1)
                pool.wait_ge(m_bo, (NT + 1) * m + 1)
                pool.wait_ge(ln_done, NT * (n + 1))
                with pool.Fori(0, NT) as i:
                    pool.tensor_tensor(xs[:, i, :], xs[:, i, :], brow[:, 2, :], ALU.add).then_inc(m_bo, 1)
                with pool.Fori(0, NT, 2) as i:
                    for j in range(2):
                        pool.wait_ge(m_max, NT * m + i + j + 1)
                        pool.tensor_tensor(sc[:, j, :, :], sc[:, j, :, :], smax[:, j, :].unsqueeze(2).to_broadcast([P, H, S2]),
                                           ALU.subtract).then_inc(m_sub, 1)

            def split(layer, ppu, first=0, end=None):
                def unit(u, s):
                    pool.wait_ge(w_used, UNITS_BEFORE[layer] + u + 1)
                    for q in range(ppu):
                        done = PIECES[layer] + u * ppu + q + 1
                        pool.wait_ge(w_in[q], 16 * (LOADS[layer][q] + u + 1))
                        pool.tensor_tensor(whi[:, s, q, :], wraw[:, q, :], zero[:, :].to_broadcast([P, PIECE]), ALU.add).then_inc(w_hi, 1)
                        pool.wait_ge(w_hi, done)
                        pool.tensor_tensor(wlo[:, s, q, :], wraw[:, q, :], whi[:, s, q, :].bitcast(F32), ALU.subtract).then_inc(w_lo, 1)
                end = end or COUNTS[layer][1]
                with pool.Fori(first, end - (end - first) % 2, 2) as u:
                    for s in range(2):
                        unit(u + s, s)
                if (end - first) % 2:
                    unit(end - 1, (end - 1) % 2)

            def moe(layer):
                name = f"ffn{layer}"
                split(name, 4, 0, 2)
                pool.wait_ge(zeroed, 1 + 16 * 2)
                pool.wait_ge(r_idx, MOE.index(layer) + 1)
                for c in range(TOPK[layer]):
                    for i in range(NT):
                        pool.indirect_dma_start(out=xbuf, out_offset=bass.IndirectOffsetOnAxis(ap=sidx[:, c, i:i + 1], axis=0),
                                                in_=lnx[:, i, :], in_offset=None, bounds_check=ROWS - 1, oob_is_err=False).then_inc(scattered, 16)
                split(name, 4, 2)
                for s in range(2):
                    pool.wait_ge(y_st[s], 16 + 16 * (ROW_LOADS[layer][s] + (ITEMS[layer] + 1 - s) // 2))
                rows = ITEMS[layer] * IR[layer]
                for g in range(NG):
                    for c in range(TOPK[layer]):
                        for i in range(g * GROUP, (g + 1) * GROUP):
                            dst = lnx if c == 0 else y_second
                            pool.indirect_dma_start(out=dst[:, i, :], out_offset=None, in_=ybuf[0:rows, :],
                                                    in_offset=bass.IndirectOffsetOnAxis(ap=gidx[:, c, i:i + 1], axis=0),
                                                    bounds_check=rows - 1, oob_is_err=False).then_inc(fetched[g], 16)

            if "ffn0" in N:
                moe(0)
            if "attn1" in N:
                mha(1, 0, N["attn1"])
            if "ffn1" in N:
                pool.wait_ge(x_done, NT * N["ffn1"])
                pool.memset(xT[:, :, :], 0.0).then_inc(f_yevac, 1)
                split("ffn1", 3)

            if "attn2" in N:
                pool.wait_ge(x_done, NT * N["attn2"])
                for r in range(2):
                    pool.tensor_copy(ctxD[:, :, :, r, :], ctxT[:, :, :].rearrange("p k (b s) -> p k b s", b=B)).then_inc(a2_pool, 1)
                pool.memset(vh[:, :, HD:HD + 1], 1.0).then_inc(a2_pool, 1)
            if "ffn2" in N:
                moe(2)
            if "attn3" in N:
                mha(3, 1, N["attn3"])
            if "ffn3" in N:
                moe(3)

        @block.tensor
        def _(pe):
            def mm(out_, lhsT, rhs, start, stop):
                return pe.matmul(out_, lhsT, rhs, start=start, stop=stop)

            def turn_norm(n, split=False):
                for g in range(NG):
                    pe.wait_ge(ln_done, NT * n + GROUP * (g + 1))
                    if g >= 2:
                        pe.wait_ge(xt_done, NG * n + g - 1)
                        if split:
                            pe.wait_ge(xl_done, g - 1)
                    for t in range(GROUP):
                        for k in range(KD):
                            last = pe.transpose(ps[:, (g % 2) * 2 + k, t * P:(t + 1) * P],
                                                lnx[:, g * GROUP + t, k * P:(k + 1) * P], ident[:, :])
                    last.then_inc(tr_done, 1)

            pe.wait_ge(const_done, 8)
            pe.wait_ge(in_ctx, 16)
            for k in range(KD):
                last = pe.transpose(ps[:, 7, k * P:(k + 1) * P], ctx_sb[:, k * P:(k + 1) * P], ident[:, :])
            last.then_inc(ctx_tr, 1)

            def attn0():
                pe.wait_ge(ctxT_done, 1)
                pe.wait_ge(in_wat, 64)
                for i in (0, 1):
                    for k in range(KD):
                        last = mm(ps[:, 4 + i, 0:D], ctxT[:, k, :], wat[:, 1 + i, k, :], k == 0, k == KD - 1)
                last.then_inc(a0_kv, 1)
                turn_norm(0)
                pe.wait_ge(a0_k, 2)
                for b in range(B):
                    r = slice(b * S2, (b + 1) * S2)
                    for k in range(KD):
                        mm(ps[:, 6 + b, k * D:(k + 1) * D], k0[r, k * P:(k + 1) * P], v0[r, :], True, True)
                        last = mm(ps[:, 4 + b, k:k + 1], k0[r, k * P:(k + 1) * P], ones[r, :], True, True)
                last.then_inc(a0_num, 1)
                pe.wait_ge(xt_done, NG)
                pe.wait_ge(a0_kvcopy, 1)
                with pe.Fori(0, NG // B) as j:
                    for b in range(B):
                        s = j * B + b
                        blk = bass.ts(j + b * (NG // B), GT)
                        pe.wait_ge(a0_den, s + 1)
                        for c in range(KD):
                            for k in range(KD):
                                last = mm(ps[:, c, :], wat[:, 0, k, c * P:(c + 1) * P], xT[:, k, blk], k == 0, k == KD - 1)
                        last.then_inc(a0_q, 1)
                        pe.wait_ge(a0_qexp, 3 * s + 3)
                        pe.wait_ge(a0_den, s + 2)
                        for c in range(KD):
                            for k in range(KD):
                                last = mm(ps[:, 2 + c, :], kv0[:, b, k, c * P:(c + 1) * P], q_relu[:, k, :], k == 0, k == KD - 1)
                        last.then_inc(a0_num, 1)
                        pe.wait_ge(a0_o, s + 1)
                        for t in range(GROUP):
                            for c in range(KD):
                                last = mm(ps[:, 4 + t // 2, (t % 2) * D:(t % 2 + 1) * D], q_o[:, c, t * P:(t + 1) * P],
                                          wat[:, 3, c, :], c == 0, c == KD - 1)
                        last.then_inc(a0_proj, 1)
            attn0()

            def mha(layer, m, n):
                pe.wait_ge(in_wat, 64 * WAT[layer])
                pe.wait_ge(m_tab, 5 * m + 2)
                pe.wait_ge(x_done, NT * n)
                for c in range(KD):
                    for k in range(KD):
                        mm(ps[:, 4, c * P:(c + 1) * P], wat[:, 1, k, c * P:(c + 1) * P], ctxT[:, k, :], k == 0, k == KD - 1)
                for b in range(B):
                    for k in range(KD):
                        last = mm(ps[:, 5, b * D:(b + 1) * D], ctxD[:, k, b, :, :], wat[:, 2, k, :], k == 0, k == KD - 1)
                last.then_inc(m_kv, 1)
                turn_norm(n)
                pe.wait_ge(xt_done, NG * (n + 1))
                pe.wait_ge(m_kblk, 8 * (m + 1))
                pe.wait_ge(m_tab, 5 * (m + 1))
                base = NT * m

                def query(i):
                    for c in range(KD):
                        for k in range(KD):
                            last = mm(ps[:, 0, c * P:(c + 1) * P], wat[:, 0, k, c * P:(c + 1) * P], xT[:, k, bass.ts(i, P)], k == 0, k == KD - 1)
                    last.then_inc(m_q, 1)

                def scores(i, first=False):
                    pe.wait_ge(m_qt, 2 * (base + i + 1))
                    if not first:
                        pe.wait_ge(m_min, base + i)
                    for c in range(KD):
                        last = mm(ps[:, 1 + c, :], qt[:, 0, c, :], kblk[:, i // TB, c, :, :], True, True)
                    last.then_inc(m_s, 1)

                def turn_probs(i, j):
                    pe.wait_ge(m_exp, base + i + 1)
                    for q in range(PAIRS):
                        last = pe.transpose(ps[:, 3 + q // 4, (q % 4) * P:(q % 4 + 1) * P], sc[:, j, 2 * q:2 * q + 2, :], ident[:, :])
                    last.then_inc(m_ptr, 1)

                def values(i):
                    pe.wait_ge(m_pta, base + i + 1)
                    pe.wait_ge(m_ptd, base + i + 1)
                    for q in range(PAIRS):
                        last = mm(ps[:, 5, q * VC:(q + 1) * VC], pt[:, q, :], vblk[:, i // TB, q, :], True, True)
                    last.then_inc(m_av, 1)

                def output(i):
                    pe.wait_ge(m_oh, base + i + 1)
                    for c in range(KD):
                        last = pe.transpose(ps[:, 6, c * P:(c + 1) * P], oh[:, c * P:(c + 1) * P], ident[:, :])
                    last.then_inc(m_otr, 1)
                    pe.wait_ge(m_ot, base + i + 1)
                    pe.wait_ge(x_done, NT * n + i)
                    for c in range(KD):
                        last = mm(ps[:, 7, 0:D], ot[:, c, :], wat[:, 3, c, :], c == 0, c == KD - 1)
                    last.then_inc(m_proj, 1)

                query(0)
                scores(0, True)

                def step(i, j):
                    query(i + 1)
                    turn_probs(i, j)
                    scores(i + 1)
                    values(i)
                    output(i)
                with pe.Fori(0, NT - 2, 2) as i:
                    step(i, 0)
                    step(i + 1, 1)
                step(NT - 2, 0)
                turn_probs(NT - 1, 1)
                values(NT - 1)
                output(NT - 1)

            def ffn1(n):
                shared = CHUNKS["ffn1"]
                turn_norm(n, split=True)
                pe.wait_ge(xt_done, NG * (n + 1))
                pe.wait_ge(xl_done, NG)

                def up(c, s, f, blk, start=False, left=False):
                    if not (start and f < 2):
                        pe.wait_ge(f_h, c - 1)
                    tok = bass.ts(blk, GT)
                    for q in range(2):
                        for k in range(KD):
                            w = slice(k * HALF + f * P, k * HALF + (f + 1) * P)
                            o = ps[:, (f % 2) * 2 + q, :]
                            first = mm(o, whi[:, s, q, w], xTh[:, k, tok], k == 0, False)
                            if left and q == k == 0:
                                first.then_inc(w_used, 1)
                            mm(o, whi[:, s, q, w], xTl[:, k, tok], False, False)
                            last = mm(o, wlo[:, s, q, w], xTh[:, k, tok], False, k == KD - 1)
                    last.then_inc(f_up, 1)

                def down(c, s, f):
                    pe.wait_ge(f_lo, shared + c + 1)
                    if f == 0:
                        pe.wait_ge(f_yevac, c // FH + 1)
                    for d in range(KD):
                        w = slice(f * D + d * P, f * D + (d + 1) * P)
                        o = ps[:, 4 + d, :]
                        mm(o, whi[:, s, 2, w], h_hi[:, f, :], f == 0, False)
                        mm(o, whi[:, s, 2, w], h_lo[:, f, :], False, False)
                        last = mm(o, wlo[:, s, 2, w], h_hi[:, f, :], False, f == FH - 1)
                    last.then_inc(f_used, 1)

                def unit(u, s, start=False):
                    pe.wait_ge(w_lo, PRIMED + PIECES["ffn1"] + 3 * (u + 1))
                    c0 = u * (NG * FH)
                    for f in range(FH):
                        up(c0 + f, s, f, 0, start, left=f == 2 and not start)
                        if f >= 2:
                            down(c0 + f - 2, s, f - 2)
                        elif not start:
                            down(c0 + f - 2, 1 - s, f + 2)
                    with pe.Fori(1, NG) as blk:
                        for f in range(FH):
                            c = c0 + blk * FH + f
                            up(c, s, f, blk)
                            down(c - 2, s, (f + 2) % FH)

                unit(0, 0, start=True)
                with pe.Fori(1, UNITS - 1, 2) as u:
                    unit(u, 1)
                    unit(u + 1, 0)
                unit(UNITS - 1, 1)
                last_c = UNITS * NG * FH
                down(last_c - 2, 1, FH - 2)
                down(last_c - 1, 1, FH - 1)
                pe.wait_ge(f_yevac, UNITS * NG + 1)
                for i in range(NT):
                    if i >= 4:
                        pe.wait_ge(x_done, NT * n + i - 3)
                    for d in range(KD):
                        last = pe.transpose(ps[:, i % 4, d * P:(d + 1) * P], xT[:, d, i * P:(i + 1) * P], ident[:, :])
                        if i == d == 0:
                            last.then_inc(w_used, 1)
                    last.then_inc(f_back, 1)

            def moe(layer, n):
                name = f"ffn{layer}"
                nth, cap, items, tiles = MOE.index(layer), CAP[layer], ITEMS[layer], IR[layer] // P
                pe.wait_ge(in_moe, 16 * 11)
                turn_norm(n)
                for i in range(NT):
                    pe.wait_ge(xt_done, NG * n + i // GROUP + 1)
                    for k in range(KD):
                        last = mm(ps[:, 4, i * E:(i + 1) * E], xT[:, k, i * P:(i + 1) * P], wr[:, layer, k, :], k == 0, k == KD - 1)
                last.then_inc(r_logits, 1)
                pe.wait_ge(r_mask, nth + 1)
                if layer == 0:
                    for i in range(NT):
                        pe.matmul(ps[:, 6, 0:E], ones_b[:, :], mask_b[:, i, :], start=(i == 0), stop=(i == NT - 1))
                rank = ps[:, 5, 0:NT * E].rearrange("p (t e) -> p t e", t=NT)
                pe.matmul(rank, tri[:, :], mask_b[:, :, :], start=True, stop=False, skip_group_check=True)
                for i in range(NT - 1):
                    last = pe.matmul(rank[:, i + 1:NT, :], ones_b[:, :], mask_b[:, i:i + 1, :].to_broadcast([P, NT - 1 - i, E]),
                                     start=False, stop=(i == NT - 2), skip_group_check=True)
                last.then_inc(r_rank, 1)

                def turn_rows(e, s):
                    pe.wait_ge(x_in[s], 16 * (ROW_LOADS[layer][s] + 1) + 8 * (e - s))
                    for k in range(KD):
                        for j in range(tiles):
                            last = pe.transpose(ps[:, 6 + k, j * P:(j + 1) * P], x_row[:, s, j, k * P:(k + 1) * P], ident[:, :])
                    last.then_inc(x_tr, 1)

                def up(e, s, f, start=False, left=False):
                    c = CHUNKS[name] + e * FC + f
                    if f == 0:
                        pe.wait_ge(w_lo, PRIMED + PIECES[name] + 4 * (e + 1))
                        pe.wait_ge(x_lo, EXPERTS[name] + e + 1)
                    if not start or f >= 2:
                        pe.wait_ge(m_act, MC[name] + e * FC + f - 1)
                    w = slice(f * P, (f + 1) * P)
                    tok = slice(s * GT * 2, s * GT * 2 + cap)
                    o = ps[:, f % 2, 0:cap]
                    for k in range(KD):
                        first = mm(o, whi[:, s, k, w], xTh[:, k, tok], k == 0, False)
                        if left and k == 0:
                            first.then_inc(w_used, 1)
                        mm(o, whi[:, s, k, w], xTl[:, k, tok], False, False)
                        last = mm(o, wlo[:, s, k, w], xTh[:, k, tok], False, k == KD - 1)
                    last.then_inc(f_up, 1)

                def down(e, s, f):
                    c = CHUNKS[name] + e * FC + f
                    pe.wait_ge(f_lo, c + 1)
                    if f == 0:
                        pe.wait_ge(y_out, PRIMED + EXPERTS[name] + e - 1)
                    for d in range(KD):
                        w = slice((f % 4) * D + d * P, (f % 4) * D + (d + 1) * P)
                        q = 2 + f // 4
                        o = ps[:, 2 + 2 * s + d, 0:cap]
                        mm(o, whi[:, s, q, w], h_hi[:, f % 4, 0:cap], f == 0, False)
                        mm(o, whi[:, s, q, w], h_lo[:, f % 4, 0:cap], False, False)
                        last = mm(o, wlo[:, s, q, w], h_hi[:, f % 4, 0:cap], False, f == FC - 1)
                    last.then_inc(f_used, 1)

                def turn_back(e, s, final=False):
                    pe.wait_ge(y_out, PRIMED + EXPERTS[name] + e + 1)
                    for j in range(tiles):
                        for k in range(KD):
                            o = ps[:, 6 + j // 2, (j % 2) * D + k * P:(j % 2) * D + (k + 1) * P]
                            last = pe.transpose(o, y_t[:, k, j * P:(j + 1) * P], ident[:, :])
                            if final and j == k == 0:
                                last.then_inc(w_used, 1)
                    last.then_inc(y_tr, 1)

                def expert(e, s, start=False, end=False):
                    for f in range(FC):
                        up(e, s, f, start, left=f == 2 and not start)
                        if f >= 2:
                            down(e, s, f - 2)
                        elif not start:
                            down(e - 1, 1 - s, f + 6)
                        if f == 3 and not start:
                            turn_back(e - 1, 1 - s)
                        if f == 5 and not end:
                            if not start:
                                pe.wait_ge(y_copied, EXPERTS[name] + e)
                            turn_rows(e + 1, 1 - s)

                turn_rows(0, 0)
                expert(0, 0, start=True)
                pairs_end = items - 1 - items % 2 * 2
                with pe.Fori(1, pairs_end, 2) as e:
                    expert(e, 1)
                    expert(e + 1, 0)
                for e in range(pairs_end + items % 2, items):
                    expert(e, e % 2, end=e == items - 1)
                last_slot = (items - 1) % 2
                for f in (FC - 2, FC - 1):
                    down(items - 1, last_slot, f)
                turn_back(items - 1, last_slot, final=True)

            if "ffn0" in N:
                moe(0, N["ffn0"])
            if "attn1" in N:
                mha(1, 0, N["attn1"])
            if "ffn1" in N:
                ffn1(N["ffn1"])

            def attn2(n):
                pe.wait_ge(in_wat, 64 * WAT[2])
                pe.wait_ge(in_a2, 48)
                for i in range(3):
                    for c in range(KD):
                        for k in range(KD):
                            last = mm(ps[:, 4, (i * KD + c) * HD:(i * KD + c + 1) * HD], wat[:, i, k, c * P:(c + 1) * P],
                                      wh[:, i, k, :], k == 0, k == KD - 1)
                last.then_inc(a2_pe, 1)
                turn_norm(n)
                pe.wait_ge(a2_dve, 2)
                pe.wait_ge(a2_pool, 2)
                for k in range(KD):
                    mm(ps[0:HD, 5, 0:P], wqkv[:, 1, k, :], ctxT[:, k, :], k == 0, k == KD - 1)
                for b in range(B):
                    for k in range(KD):
                        last = mm(ps[:, 6, b * HD:(b + 1) * HD], ctxD[:, k, b, :, :], wqkv[:, 2, k, :], k == 0, k == KD - 1)
                last.then_inc(a2_pe, 1)
                pe.wait_ge(xt_done, NG * (n + 1))
                for g in range(NG):
                    for k in range(KD):
                        last = mm(ps[0:HD, g, :], wqkv[:, 0, k, :], xT[:, k, g * GT:(g + 1) * GT], k == 0, k == KD - 1)
                    last.then_inc(a2_pe, 1)
                pe.wait_ge(a2_act, 1 + NG)
                pe.wait_ge(a2_dve, 5)
                for i in range(NT):
                    last = mm(ps[:, 4 + i // TB, (i % TB) * S2:(i % TB + 1) * S2], qhT[:, i * P:(i + 1) * P], khT[:, i // TB, :], True, True)
                last.then_inc(a2_pe, 1)
                pe.wait_ge(a2_act, 2 + NG)
                for q in range(PAIRS):
                    last = pe.transpose(ps[:, 6 + q // 4, (q % 4) * P:(q % 4 + 1) * P], sc[:, 0, 2 * q:2 * q + 2, :], ident[:, :])
                last.then_inc(a2_pe, 1)
                pe.wait_ge(a2_act, 3 + NG)
                pe.wait_ge(a2_dve, 10)
                for q in range(PAIRS):
                    for r in range(2):
                        h = slice(r * S2, (r + 1) * S2)
                        last = mm(ps[:, r, q * (HD + 1):(q + 1) * (HD + 1)], pt[h, q, :], vh[h, 2 * q // TB, :], True, True)
                last.then_inc(a2_pe, 1)
                pe.wait_ge(a2_dve, 13)
                for i in range(NT + 1):
                    if i < NT:
                        if i >= 2:
                            pe.wait_ge(a2_act, 3 + NG + i - 1)
                        pe.transpose(ps[:, 2 + i % 2, 0:P], oh8[:, i, :, :], ident[:, :]).then_inc(a2_pe, 1)
                    if i > 0:
                        pe.wait_ge(a2_act, 3 + NG + i)
                        if i > 2:
                            pe.wait_ge(x_done, NT * n + i - 2)
                        mm(ps[:, 4 + (i - 1) % 2, 0:D], ot8[:, (i - 1) % 2, :], wo8[:, :], True, True).then_inc(a2_pe, 1)

            if "attn2" in N:
                attn2(N["attn2"])
            if "ffn2" in N:
                moe(2, N["ffn2"])
            if "attn3" in N:
                mha(3, 1, N["attn3"])
            if "ffn3" in N:
                moe(3, N["ffn3"])

        @block.scalar
        def _(act):
            act.wait_ge(in_gate, 32)
            act.activation(gates[:, :], gates_raw[:, :], ACT.Tanh).then_inc(gates_done, 1)
            act.wait_ge(ctx_tr, 1)
            act.activation(ctxT[:, :, :], ps[:, 7, 0:D].rearrange("p (k s) -> p k s", k=KD), ACT.Copy).then_inc(ctxT_done, 1)

            def std(n):
                act.wait_ge(var_done, n + 1)
                act.activation(st_std[:, :], st_var[:, :], ACT.Sqrt, bias=eps[:, :]).then_inc(std_done, 1)

            def copy_turned(n, dst):
                act.wait_ge(zeroed, 1 + 16 * 2)
                for g in range(NG):
                    act.wait_ge(tr_done, NG * n + g + 1)
                    act.activation(dst[:, :, g * GT:(g + 1) * GT], ps[:, (g % 2) * 2:(g % 2) * 2 + 2, :], ACT.Copy).then_inc(xt_done, 1)

            act.wait_ge(const_done, 8)
            act.wait_ge(a0_kmin, 1)
            act.activation(k0_min[:, :], k0_min[:, :], ACT.Exp).then_inc(a0_kexp, 1)
            std(0)
            copy_turned(0, xT)
            with act.Fori(0, NG // B) as j:
                for b in range(B):
                    s = j * B + b
                    act.wait_ge(a0_q, s + 1)
                    act.wait_ge(a0_num, s + 1)
                    for c in range(KD):
                        act.wait_ge(a0_qmin, 2 * s + c + 1)
                        act.activation(q_relu[:, c, :], ps[:, c, :], ACT.Relu, bias=bcol0[:, c:c + 1]).then_inc(a0_qexp, 1)
                    act.activation(q_min[:, :, :], q_min[:, :, :], ACT.Exp).then_inc(a0_qexp, 1)
            std(1)

            def mha(layer, m, n):
                act.wait_ge(m_kv, m + 1)
                act.wait_ge(in_bias, bias_at[layer])
                for c in range(KD):
                    act.activation(kt[:, c, :], ps[:, 4, c * P:(c + 1) * P], ACT.Identity, bias=bcol[:, KD + c:KD + c + 1]).then_inc(m_kt, 1)
                std(n + 1)
                copy_turned(n, xT)
                base = NT * m

                def query(i):
                    act.wait_ge(m_q, base + i + 1)
                    for c in range(KD):
                        act.activation(qt[:, 0, c, :], ps[:, 0, c * P:(c + 1) * P], ACT.Identity, bias=bcol[:, c:c + 1]).then_inc(m_qt, 1)

                def exps(i, j):
                    act.wait_ge(m_sub, base + i + 1)
                    act.activation(sc[:, j, :, :], sc[:, j, :, :], ACT.Exp).then_inc(m_exp, 1)

                def probs(i):
                    act.wait_ge(m_ptr, base + i + 1)
                    act.activation(pt[:, 0:4, :], ps[:, 3, :].rearrange("p (q t) -> p q t", q=4), ACT.Copy).then_inc(m_pta, 1)

                def heads(i):
                    act.wait_ge(m_otr, base + i + 1)
                    act.activation(ot[:, :, :], ps[:, 6, 0:D].rearrange("p (c t) -> p c t", c=KD), ACT.Copy).then_inc(m_ot, 1)

                def step(i, j):
                    query(i + 1)
                    probs(i)
                    heads(i)
                    exps(i + 1, 1 - j)
                query(0)
                exps(0, 0)
                with act.Fori(0, NT - 2, 2) as i:
                    step(i, 0)
                    step(i + 1, 1)
                step(NT - 2, 0)
                probs(NT - 1)
                heads(NT - 1)

            def ffn1(n):
                shared = CHUNKS["ffn1"]
                std(n + 1)
                copy_turned(n, xTh)

                def silu(c, f):
                    act.wait_ge(f_up, shared + c + 1)
                    act.activation(h_act[:, f % 2, :], ps[:, (f % 2) * 2, :], ACT.Silu).then_inc(f_act, 1)

                def upper(c, f):
                    act.wait_ge(f_h, c + 1)
                    act.wait_ge(f_used, shared + c - FH + 2)
                    act.activation(h_hi[:, f, :], h_32[:, f % 2, :], ACT.Copy).then_inc(f_hi, 1)

                for f in range(FH):
                    silu(f, f)
                    if f > 0:
                        act.wait_ge(f_h, f)
                        act.activation(h_hi[:, f - 1, :], h_32[:, (f - 1) % 2, :], ACT.Copy).then_inc(f_hi, 1)
                with act.Fori(1, UNITS * NG) as blk:
                    for f in range(FH):
                        silu(blk * FH + f, f)
                        upper(blk * FH + f - 1, (f - 1) % FH)
                upper(UNITS * NG * FH - 1, FH - 1)

            def moe(layer, n):
                name = f"ffn{layer}"
                nth, cap, items, tiles = MOE.index(layer), CAP[layer], ITEMS[layer], IR[layer] // P
                func = {0: ACT.Relu, 2: ACT.Gelu, 3: ACT.Relu}[layer]
                std(n + 1)
                copy_turned(n, xT)
                act.wait_ge(r_sub, nth + 1)
                act.activation(r_e[:, :, :], r_p[:, :, :], ACT.Exp).then_inc(r_exp, 1)

                def rows_upper(e, s):
                    act.wait_ge(x_tr, EXPERTS[name] + e + 1)
                    act.activation(xTh[:, :, s * GT * 2:s * GT * 2 + cap], ps[:, 6:8, 0:cap], ACT.Copy).then_inc(x_hi, 1)

                def hidden(e, f, ex, start=False):
                    c = CHUNKS[name] + e * FC + f
                    act.wait_ge(f_up, c + 1)
                    if not start or f >= 2:
                        act.wait_ge(f_hi, c - 1)
                        act.wait_ge(f_lo, c - 1)
                    act.activation(h_32[:, f % 2, 0:cap], ps[:, f % 2, 0:cap], func, bias=b1c[:, layer, bass.ds(ex * FC + f, 1)]).then_inc(m_act, 1)

                def upper(e, f, start=False):
                    c = CHUNKS[name] + e * FC + f
                    act.wait_ge(m_act, MC[name] + e * FC + f + 1)
                    if not (start and f < 3):
                        act.wait_ge(f_used, c - FH + 2)
                    act.activation(h_hi[:, f % 4, 0:cap], h_32[:, f % 2, 0:cap], ACT.Copy).then_inc(f_hi, 1)

                def expert(e, s, start=False, end=False):
                    ex = act.value_load(item_expert[0:1, bass.ds(e, 1)], min_val=0, max_val=E - 1) if layer == 0 else e
                    for f in range(FC):
                        hidden(e, f, ex, start)
                        if f > 0:
                            upper(e, f - 1, start)
                        elif not start:
                            upper(e - 1, FC - 1)
                        if f == 5 and not end:
                            rows_upper(e + 1, 1 - s)
                if layer == 0:
                    act.wait_ge(r_idx, 1)
                rows_upper(0, 0)
                expert(0, 0, start=True)
                pairs_end = items - 1 - items % 2 * 2
                with act.Fori(1, pairs_end, 2) as e:
                    expert(e, 1)
                    expert(e + 1, 0)
                for e in range(pairs_end + items % 2, items):
                    expert(e, e % 2, end=e == items - 1)
                last_slot = (items - 1) % 2
                upper(items - 1, FC - 1)

            if "ffn0" in N:
                moe(0, N["ffn0"])
            if "attn1" in N:
                mha(1, 0, N["attn1"])
            if "ffn1" in N:
                ffn1(N["ffn1"])

            def attn2(n):
                act.wait_ge(a2_pe, 1)
                act.activation(wqkv[:, :, :, :], ps[:, 4, 0:3 * KD * HD].rearrange("p (i k j) -> p i k j", i=3, k=KD), ACT.Copy).then_inc(a2_act, 1)
                std(n + 1)
                copy_turned(n, xT)
                for g in range(NG):
                    act.wait_ge(a2_pe, 3 + g)
                    act.activation(qhT[:, g * GT:(g + 1) * GT], ps[0:HD, g, :], ACT.Identity, bias=bh[:, 0:1]).then_inc(a2_act, 1)
                act.wait_ge(a2_dve, 9)
                act.activation(sc[:, 0, :, :], sc[:, 0, :, :], ACT.Exp).then_inc(a2_act, 1)
                act.wait_ge(a2_pe, 8)
                act.activation(pt[:, 0:4, :], ps[:, 6, :].rearrange("p (q t) -> p q t", q=4), ACT.Copy).then_inc(a2_act, 1)
                for i in range(NT):
                    act.wait_ge(a2_pe, 9 + (2 * i if i else 1))
                    act.activation(ot8[:, i % 2, :], ps[:, 2 + i % 2, 0:P], ACT.Copy).then_inc(a2_act, 1)

            if "attn2" in N:
                attn2(N["attn2"])
            if "ffn2" in N:
                moe(2, N["ffn2"])
            if "attn3" in N:
                mha(3, 1, N["attn3"])
            if "ffn3" in N:
                moe(3, N["ffn3"])

        @block.vector
        def _(dve):
            links = [0]

            def link(ins):
                links[0] += 1
                ins.then_inc(link_s, 1)
                dve.wait_ge(link_s, links[0])

            def stats(n, src):
                with dve.Fori(0, NT) as i:
                    dve.bn_stats(bn[:, i, :], src[:, i, :]).then_inc(bn_done, 1)
                dve.wait_ge(bn_done, NT * (n + 1))
                dve.tensor_tensor(st_sum[:, :], bn[:, :, 1], bn[:, :, 4], ALU.add).then_inc(link_s, 1)
                dve.tensor_tensor(st_dif[:, :], bn[:, :, 1], bn[:, :, 4], ALU.subtract).then_inc(link_s, 1)
                links[0] += 2
                link(dve.tensor_tensor(st_m2[:, :], bn[:, :, 2], bn[:, :, 5], ALU.add))
                dve.tensor_scalar(st_mean[:, :], st_sum[:, :], 0.5, None, ALU.mult).then_inc(link_s, 1)
                links[0] += 1
                link(dve.scalar_tensor_tensor(out=st_sq[:, :], in0=st_dif[:, :], scalar=0.25, in1=st_dif[:, :], op0=ALU.mult, op1=ALU.mult))
                dve.scalar_tensor_tensor(out=st_var[:, :], in0=st_m2[:, :], scalar=1.0 / D, in1=st_sq[:, :],
                                         op0=ALU.mult, op1=ALU.add).then_inc(var_done, 1)
                dve.wait_ge(std_done, n + 1)
                link(dve.reciprocal(st_rstd[:, :], st_std[:, :]))

            def norm(n):
                if n > 0:
                    dve.wait_ge(x_done, NT * n)
                stats(n + (n > 0), xs)
                with dve.Fori(0, NT) as i:
                    dve.tensor_scalar(lnx[:, i, :], xs[:, i, :], st_mean[:, bass.ds(i, 1)], st_rstd[:, bass.ds(i, 1)],
                                      ALU.subtract, ALU.mult).then_inc(ln_done, 1)

            dve.wait_ge(a0_kv, 1)
            dve.wait_ge(in_bias, bias_at[0])
            link(dve.tensor_tensor(k0[:, :], ps[:, 4, 0:D], brow0[:, 0, :], ALU.add))
            dve.tensor_scalar(k0_min[:, :], k0[:, :], 0.0, None, ALU.min).then_inc(a0_kmin, 1)
            dve.tensor_tensor(v0[:, :], ps[:, 5, 0:D], brow0[:, 1, :], ALU.add).then_inc(a0_k, 1)
            dve.wait_ge(a0_kexp, 1)
            dve.scalar_tensor_tensor(out=k0[:, :], in0=k0[:, :], scalar=0.0, in1=k0_min[:, :], op0=ALU.max, op1=ALU.add).then_inc(a0_k, 1)
            dve.wait_ge(in_x, 16 * NG)
            norm(0)
            dve.wait_ge(a0_num, 1)
            dve.tensor_copy(kv0[:, :, :, :], ps[:, 6:8, :].rearrange("p b (k e) -> p b k e", k=KD)).then_inc(a0_kvcopy, 1)
            dve.tensor_copy(ksum0[:, :, :], ps[:, 4:6, 0:KD]).then_inc(a0_den, 1)
            dve.wait_ge(a0_den, 1)
            dve.wait_ge(a0_bo, NT)
            with dve.Fori(0, NG // B) as j:
                for b in range(B):
                    s = j * B + b
                    dve.wait_ge(a0_q, s + 1)
                    for c in range(KD):
                        dve.tensor_scalar(q_min[:, c, :], ps[:, c, :], bcol0[:, c:c + 1], 0.0, ALU.add, ALU.min).then_inc(a0_qmin, 1)
                    dve.wait_ge(a0_qexp, 3 * s + 3)
                    dve.tensor_tensor(q_relu[:, :, :], q_relu[:, :, :], q_min[:, :, :], ALU.add).then_inc(a0_den, 1)
                    dve.wait_ge(a0_den, s + 2)
                    for c in range(KD):
                        dve.tensor_scalar(q_den[:, c, :], q_relu[:, c, :], ksum0[:, b, c:c + 1], 1e-6, ALU.mult, ALU.add).then_inc(a0_res, 1)
                    dve.wait_ge(a0_res, (s + 1) * 8 - 6)
                    dve.reciprocal(q_den[:, :, :], q_den[:, :, :]).then_inc(a0_res, 1)
                    dve.wait_ge(a0_res, (s + 1) * 8 - 5)
                    dve.wait_ge(a0_num, s + 2)
                    dve.tensor_tensor(q_o[:, :, :], ps[:, 2:4, :], q_den[:, :, :], ALU.mult).then_inc(a0_o, 1)
                    dve.wait_ge(a0_proj, s + 1)
                    for t in range(GROUP):
                        tile = (j + b * (NG // B)) * GROUP + t
                        ins = dve.tensor_tensor(lnx[:, tile, :], lnx[:, tile, :], ps[:, 4 + t // 2, (t % 2) * D:(t % 2 + 1) * D], ALU.add)
                        ins.then_inc(a0_res, 2 if t == GROUP - 1 else 1)
            dve.wait_ge(a0_res, 8 * NG)
            stats(1, lnx)
            with dve.Fori(0, NT) as i:
                dve.tensor_scalar(lnx[:, i, :], lnx[:, i, :], st_mean[:, bass.ds(i, 1)], st_rstd[:, bass.ds(i, 1)],
                                  ALU.subtract, ALU.mult).then_inc(a0_nrm, 1)
            dve.wait_ge(a0_bo, 2 * NT)
            with dve.Fori(0, NT) as i:
                dve.wait_ge(a0_gam, i + 1)
                dve.tensor_tensor(xs[:, i, :], xs[:, i, :], lnx[:, i, :], ALU.add).then_inc(x_done, 1)

            def mha(layer, m, n):
                dve.wait_ge(in_mask, 16 * MASKS[layer])
                if layer == 1:
                    nb = B
                    src = mask8[:, 0:B, :]
                else:
                    nb = NT
                    src = mask32[:, :, :]
                link(dve.tensor_scalar(bmask[:, 0:nb, :], src, 0.0, BIG, ALU.not_equal, ALU.mult))
                link(dve.tensor_scalar(bmask[:, 0:nb, :], bmask[:, 0:nb, :], MASKED[layer], None, ALU.add))
                dve.wait_ge(m_kt, KD * (m + 1))
                for b in range(B):
                    for c in range(KD):
                        dve.tensor_tensor(kblk[:, b, c, :, :], kt[:, c, b * S2:(b + 1) * S2].unsqueeze(1).to_broadcast([P, HC, S2]),
                                          hmask[:, :].unsqueeze(2).to_broadcast([P, HC, S2]), ALU.mult).then_inc(m_kblk, 1)
                dve.wait_ge(m_kv, m + 1)
                dve.wait_ge(m_tab, 5 * m + 3)
                dve.wait_ge(in_bias, bias_at[layer])
                for b in range(B):
                    for r in range(2):
                        h = slice(r * S2, (r + 1) * S2)
                        dve.tensor_tensor(vblk[h, b, :, r * HD:(r + 1) * HD],
                                          ps[h, 5, b * D:(b + 1) * D].rearrange("p (q r d) -> p q r d", r=2, d=HD)[:, :, r, :],
                                          brow[h, 0, :].rearrange("p (q r d) -> p q r d", r=2, d=HD)[:, :, r, :],
                                          ALU.add).then_inc(m_kblk, 1)
                norm(n)
                base = NT * m

                def bound(i, j):
                    dve.wait_ge(m_s, base + i + 1)
                    row_ = i // TB if layer == 1 else i
                    dve.tensor_tensor(sc[:, j, :, :], ps[:, 1:3, :].rearrange("p c (h s) -> p (c h) s", h=HC),
                                      bmask[:, bass.ds(row_, 1), :].to_broadcast([P, H, S2]), ALU.min).then_inc(m_min, 1)

                def maxima(i, j):
                    dve.wait_ge(m_min, base + i + 1)
                    dve.tensor_reduce(smax[:, j, :], sc[:, j, :, :], AX.X, ALU.max).then_inc(m_max, 1)

                def probs(i):
                    dve.wait_ge(m_ptr, base + i + 1)
                    dve.tensor_copy(pt[:, 4:8, :], ps[:, 4, :].rearrange("p (q t) -> p q t", q=4)).then_inc(m_ptd, 1)

                def heads(i):
                    av = ps[:, 5, 0:PAIRS * VC].rearrange("p (q v) -> p q v", q=PAIRS)
                    dve.wait_ge(m_av, base + i + 1)
                    dve.reciprocal(rsum[:, :, :], av[:, :, 2 * HD:VC]).then_inc(m_rs, 1)
                    dve.wait_ge(m_rs, base + i + 1)
                    dve.tensor_tensor(oh[:, :].rearrange("p (q r d) -> p q r d", r=2, d=HD),
                                      av[:, :, 0:2 * HD].rearrange("p q (r d) -> p q r d", r=2),
                                      rsum[:, :, :].unsqueeze(3).to_broadcast([P, PAIRS, 2, HD]), ALU.mult).then_inc(m_oh, 1)

                def residual(i):
                    dve.wait_ge(m_proj, base + i + 1)
                    dve.scalar_tensor_tensor(out=xs[:, i, :], in0=ps[:, 7, 0:D], scalar=gates[:, layer:layer + 1], in1=xs[:, i, :],
                                             op0=ALU.mult, op1=ALU.add).then_inc(x_done, 1)

                def step(i, j):
                    probs(i)
                    bound(i + 1, 1 - j)
                    heads(i)
                    maxima(i + 1, 1 - j)
                    residual(i)
                bound(0, 0)
                maxima(0, 0)
                dve.wait_ge(m_bo, (NT + 1) * (m + 1))
                with dve.Fori(0, NT - 2, 2) as i:
                    step(i, 0)
                    step(i + 1, 1)
                step(NT - 2, 0)
                probs(NT - 1)
                heads(NT - 1)
                residual(NT - 1)

            def ffn1(n):
                shared = CHUNKS["ffn1"]
                norm(n)
                for g in range(NG):
                    dve.wait_ge(xt_done, NG * n + g + 1)
                    tok = slice(g * GT, (g + 1) * GT)
                    dve.tensor_tensor(xTl[:, :, tok], ps[:, (g % 2) * 2:(g % 2) * 2 + 2, :], xTh[:, :, tok].bitcast(F32),
                                      ALU.subtract).then_inc(xl_done, 1)

                def product(c, f, start=False):
                    dve.wait_ge(f_act, c + 1)
                    if not start:
                        dve.wait_ge(f_hi, shared + c - 1)
                        dve.wait_ge(f_lo, shared + c - 1)
                    dve.tensor_tensor(h_32[:, f % 2, :], h_act[:, f % 2, :], ps[:, (f % 2) * 2 + 1, :], ALU.mult).then_inc(f_h, 1)

                def lower(c, f):
                    dve.wait_ge(f_hi, shared + c + 1)
                    dve.tensor_tensor(h_lo[:, f, :], h_32[:, f % 2, :], h_hi[:, f, :].bitcast(F32), ALU.subtract).then_inc(f_lo, 1)

                def add_up(blk):
                    dve.wait_ge(f_used, shared + blk * FH + FH + 1)
                    dve.wait_ge(f_yevac, blk + 1)
                    tok = bass.ts(blk % NG, GT)
                    dve.tensor_tensor(xT[:, :, tok], xT[:, :, tok], ps[:, 4:6, :], ALU.add).then_inc(f_yevac, 1)

                for f in range(FH):
                    product(f, f, start=f < 2)
                    if f > 0:
                        lower(f - 1, f - 1)
                with dve.Fori(1, UNITS * NG) as blk:
                    for f in range(FH):
                        product(blk * FH + f, f)
                        lower(blk * FH + f - 1, (f - 1) % FH)
                        if f == 1:
                            add_up(blk - 1)
                lower(UNITS * NG * FH - 1, FH - 1)
                add_up(UNITS * NG - 1)
                for i in range(NT):
                    dve.wait_ge(f_back, i + 1)
                    dve.scalar_tensor_tensor(out=xs[:, i, :], in0=ps[:, i % 4, 0:D], scalar=gates[:, 5:6], in1=xs[:, i, :],
                                             op0=ALU.mult, op1=ALU.add).then_inc(x_done, 1)

            def per_token(v, k=E):
                return v.unsqueeze(2).to_broadcast([P, NT, k])

            def per_expert(v):
                return v.unsqueeze(1).to_broadcast([P, NT, E])

            def choose(top, oh):
                link(dve.tensor_reduce(top, r_p[:, :, :], AX.X, ALU.max))
                link(dve.tensor_tensor(r_key[:, :, :], r_p[:, :, :], per_token(top), ALU.is_equal))
                link(dve.tensor_tensor(r_key[:, :, :], r_key[:, :, :], per_expert(desc[:, :]), ALU.mult))
                link(dve.tensor_reduce(r_k[:, :], r_key[:, :, :], AX.X, ALU.max))
                link(dve.tensor_tensor(oh, r_key[:, :, :], per_token(r_k[:, :]), ALU.is_equal))

            def first_rows_of_items():
                def pair(u, v, op):
                    return dve.tensor_tensor(r_grid[:, :, :], u.unsqueeze(2).to_broadcast([P, NT, E]), v.unsqueeze(1).to_broadcast([P, NT, E]), op)

                def square(u, v, op):
                    return dve.tensor_tensor(r_grid[:, 0:E, :], u.unsqueeze(2).to_broadcast([P, E, E]), v.unsqueeze(1).to_broadcast([P, E, E]), op)
                link(dve.tensor_copy(r_count[:, :], ps[:, 6, 0:E]))
                link(square(r_count[:, :], steps[:, :], ALU.is_gt))
                link(dve.tensor_reduce(r_items[:, :], r_grid[:, 0:E, :], AX.X, ALU.add))
                link(square(desc[:, :], desc[:, :], ALU.is_le))
                link(dve.tensor_tensor(r_grid[:, 0:E, :], r_grid[:, 0:E, :], r_items[:, :].unsqueeze(1).to_broadcast([P, E, E]), ALU.mult))
                link(dve.tensor_reduce(r_upto[:, :], r_grid[:, 0:E, :], AX.X, ALU.add))
                link(pair(item_no[:, :], r_upto[:, :], ALU.is_ge))
                link(dve.tensor_reduce(r_m[:, :], r_grid[:, :, :], AX.X, ALU.add))
                link(dve.tensor_scalar(item_expert[:, :], r_m[:, :], float(E - 1), None, ALU.min))
                link(dve.tensor_tensor(r_count[:, :], r_upto[:, :], r_items[:, :], ALU.subtract))
                link(dve.tensor_scalar(r_count[:, :], r_count[:, :], float(IR[0]), -1.0, ALU.mult, ALU.add))
                return r_count[:, :]

            def route(layer, nth):
                logits = ps[:, 4, 0:NT * E].rearrange("p (t e) -> p t e", t=NT)
                dve.wait_ge(r_logits, nth + 1)
                if layer == 2:
                    link(dve.tensor_copy(r_p[:, :, :], logits))
                else:
                    link(dve.tensor_tensor(r_p[:, :, :], logits, per_expert(rb[:, layer, :]), ALU.add))
                link(dve.tensor_reduce(r_m[:, :], r_p[:, :, :], AX.X, ALU.max))
                dve.tensor_tensor(r_p[:, :, :], r_p[:, :, :], per_token(r_m[:, :]), ALU.subtract).then_inc(r_sub, 1)
                dve.wait_ge(r_exp, nth + 1)
                link(dve.tensor_reduce(r_s[:, :], r_e[:, :, :], AX.X, ALU.add))
                link(dve.reciprocal(r_s[:, :], r_s[:, :]))
                link(dve.tensor_tensor(r_p[:, :, :], r_e[:, :, :], per_token(r_s[:, :]), ALU.mult))
                choose(r_top[:, 0, :], r_oh1[:, :, :])
                if TOPK[layer] == 2:
                    link(dve.scalar_tensor_tensor(out=r_p[:, :, :], in0=r_oh1[:, :, :], scalar=-2.0, in1=r_p[:, :, :], op0=ALU.mult, op1=ALU.add))
                    choose(r_top[:, 1, :], r_oh2[:, :, :])
                    dve.tensor_tensor(mask_b[:, :, :], r_oh1[:, :, :], r_oh2[:, :, :], ALU.add).then_inc(r_mask, 1)
                    link(dve.tensor_tensor(r_s[:, :], r_top[:, 0, :], r_top[:, 1, :], ALU.add))
                    link(dve.reciprocal(r_s[:, :], r_s[:, :]))
                    link(dve.tensor_tensor(r_top[:, :, :], r_top[:, :, :], r_s[:, :].unsqueeze(1).to_broadcast([P, 2, NT]), ALU.mult))
                else:
                    dve.tensor_copy(mask_b[:, :, :], r_oh1[:, :, :]).then_inc(r_mask, 1)
                rank = ps[:, 5, 0:NT * E].rearrange("p (t e) -> p t e", t=NT)
                dve.wait_ge(r_rank, nth + 1)
                first = first_row[:, 0:E]
                if layer == 0:
                    first = first_rows_of_items()
                link(dve.tensor_tensor(r_pos[:, :, :], rank, per_expert(first), ALU.add))
                link(dve.tensor_scalar(r_keep[:, :, :], rank, float(CAP[layer] if layer else T), None, ALU.is_le))
                for c, oh in enumerate((r_oh1, r_oh2)[:TOPK[layer]]):
                    link(dve.tensor_tensor(oh[:, :, :], oh[:, :, :], r_keep[:, :, :], ALU.mult))
                    link(dve.tensor_reduce(r_kept[:, c, :], oh[:, :, :], AX.X, ALU.add))
                    link(dve.tensor_tensor(oh[:, :, :], oh[:, :, :], r_pos[:, :, :], ALU.mult))
                    link(dve.tensor_reduce(r_slot[:, c, :], oh[:, :, :], AX.X, ALU.add))
                k = slice(0, TOPK[layer])
                link(dve.tensor_copy(gidx[:, k, :], r_slot[:, k, :]))
                link(dve.scalar_tensor_tensor(out=r_slot[:, k, :], in0=r_kept[:, k, :], scalar=-FAR, in1=r_slot[:, k, :], op0=ALU.mult, op1=ALU.add))
                dve.tensor_scalar(sidx[:, k, :], r_slot[:, k, :], FAR, None, ALU.add).then_inc(r_idx, 1)
                link(dve.scalar_tensor_tensor(out=r_w[:, k, :], in0=r_top[:, k, :], scalar=gates[:, 4 + layer:5 + layer],
                                              in1=r_kept[:, k, :], op0=ALU.mult, op1=ALU.mult))

            def moe(layer, n):
                name = f"ffn{layer}"
                nth, cap, items, tiles = MOE.index(layer), CAP[layer], ITEMS[layer], IR[layer] // P
                norm(n)
                route(layer, nth)
                if cap < IR[layer]:
                    link(dve.memset(y_t[:, :, cap:SLOTS], 0.0))

                def rows_lower(e, s):
                    dve.wait_ge(x_hi, EXPERTS[name] + e + 1)
                    tok = slice(s * GT * 2, s * GT * 2 + cap)
                    dve.tensor_tensor(xTl[:, :, tok], ps[:, 6:8, 0:cap], xTh[:, :, tok].bitcast(F32), ALU.subtract).then_inc(x_lo, 1)

                def lower(e, f):
                    dve.wait_ge(f_hi, CHUNKS[name] + e * FC + f + 1)
                    dve.tensor_tensor(h_lo[:, f % 4, 0:cap], h_32[:, f % 2, 0:cap], h_hi[:, f % 4, 0:cap].bitcast(F32), ALU.subtract).then_inc(f_lo, 1)

                def output(e, s):
                    dve.wait_ge(f_used, CHUNKS[name] + (e + 1) * FC + 1)
                    ex = dve.value_load(item_expert[0:1, bass.ds(e, 1)], min_val=0, max_val=E - 1) if layer == 0 else e
                    dve.tensor_tensor(y_t[:, :, 0:cap], ps[:, 2 + 2 * s:4 + 2 * s, 0:cap],
                                      b2c[:, layer, bass.ds(ex * KD, KD)].unsqueeze(2).to_broadcast([P, KD, cap]), ALU.add).then_inc(y_out, 1)

                def output_rows(e, s):
                    dve.wait_ge(y_tr, EXPERTS[name] + e + 1)
                    dve.wait_ge(y_st[s], 16 * (ROW_LOADS[layer][s] + 1) + 8 * (e - s))
                    two = ps[:, 6, :].rearrange("p (j d) -> p j d", j=2)
                    dve.tensor_copy(y_row[:, s, 0:tiles - 1, :], two[:, 0:tiles - 1, :]).then_inc(y_half, 1)
                    dve.wait_ge(y_half, EXPERTS[name] + e + 1)
                    dve.tensor_copy(y_row[:, s, tiles - 1, :], ps[:, 7, 0:D] if tiles == 3 else two[:, 1, :]).then_inc(y_copied, 1)

                def expert(e, s, start=False, end=False):
                    for f in range(FC):
                        if f > 0:
                            lower(e, f - 1)
                        elif not start:
                            lower(e - 1, FC - 1)
                        if f == 2 and not start:
                            output(e - 1, 1 - s)
                        if f == 4 and not start:
                            output_rows(e - 1, 1 - s)
                        if f == 6 and not end:
                            rows_lower(e + 1, 1 - s)
                rows_lower(0, 0)
                expert(0, 0, start=True)
                pairs_end = items - 1 - items % 2 * 2
                with dve.Fori(1, pairs_end, 2) as e:
                    expert(e, 1)
                    expert(e + 1, 0)
                for e in range(pairs_end + items % 2, items):
                    expert(e, e % 2, end=e == items - 1)
                last_slot = (items - 1) % 2
                lower(items - 1, FC - 1)
                output(items - 1, last_slot)
                output_rows(items - 1, last_slot)
                for g in range(NG):
                    dve.wait_ge(fetched[g], 16 * FETCHED[layer])
                    for i in range(g * GROUP, (g + 1) * GROUP):
                        ins = dve.scalar_tensor_tensor(out=xs[:, i, :], in0=lnx[:, i, :], scalar=r_w[:, 0, i:i + 1], in1=xs[:, i, :],
                                                       op0=ALU.mult, op1=ALU.add)
                        if TOPK[layer] == 2:
                            link(ins)
                            ins = dve.scalar_tensor_tensor(out=xs[:, i, :], in0=y_second[:, i, :], scalar=r_w[:, 1, i:i + 1], in1=xs[:, i, :],
                                                           op0=ALU.mult, op1=ALU.add)
                        ins.then_inc(x_done, 1)

            if "ffn0" in N:
                moe(0, N["ffn0"])
            if "attn1" in N:
                mha(1, 0, N["attn1"])
            if "ffn1" in N:
                ffn1(N["ffn1"])

            def attn2(n):
                dve.wait_ge(in_wat, 64 * WAT[2])
                dve.wait_ge(in_mask, 16 * MASKS[2])
                dve.tensor_tensor(wo8[:, :], wat[:, 3, 0, :], wat[:, 3, 1, :], ALU.add).then_inc(a2_dve, 1)
                link(dve.tensor_scalar(bmask[:, 0:TB, :], mask8[:, :, :], 0.0, BIG, ALU.is_equal, ALU.mult))
                dve.wait_ge(a2_act, 1)
                dve.tensor_scalar(bmask[:, 0:TB, :], bmask[:, 0:TB, :], MASKED[2], None, ALU.add).then_inc(a2_dve, 1)
                norm(n)
                dve.wait_ge(in_a2, 48)
                dve.wait_ge(a2_pool, 3)
                dve.wait_ge(a2_pe, 2)
                dve.tensor_scalar(khT[:, :, :], ps[0:HD, 5, 0:P].rearrange("p (b s) -> p b s", b=B), bh[:, 1:2], 0.25, ALU.add, ALU.mult).then_inc(a2_dve, 1)
                for b in range(B):
                    dve.tensor_tensor(vh[:, b, 0:HD], ps[:, 6, b * HD:(b + 1) * HD], bvh[:, :], ALU.add).then_inc(a2_dve, 1)
                dve.wait_ge(a2_pe, 7)
                dve.wait_ge(a2_dve, 2)
                for b in range(B):
                    dve.tensor_tensor(sc[:, 0, b * TB:(b + 1) * TB, :], ps[:, 4 + b, :].rearrange("p (t s) -> p t s", t=TB),
                                      bmask[:, 0:TB, :], ALU.min).then_inc(a2_dve, 1)
                dve.wait_ge(a2_dve, 7)
                dve.tensor_reduce(smax[:, 0, :], sc[:, 0, :, :], AX.X, ALU.max).then_inc(a2_dve, 1)
                dve.wait_ge(a2_dve, 8)
                dve.tensor_tensor(sc[:, 0, :, :], sc[:, 0, :, :], smax[:, 0, :].unsqueeze(2).to_broadcast([P, H, S2]), ALU.subtract).then_inc(a2_dve, 1)
                dve.wait_ge(a2_pe, 8)
                dve.tensor_copy(pt[:, 4:8, :], ps[:, 7, :].rearrange("p (q t) -> p q t", q=4)).then_inc(a2_dve, 1)
                dve.wait_ge(a2_pe, 9)
                av = ps[:, 0:2, 0:PAIRS * (HD + 1)].rearrange("p r (q v) -> p r q v", q=PAIRS)
                dve.reciprocal(rs2[:, :, :], av[:, :, :, HD]).then_inc(a2_dve, 1)
                dve.wait_ge(a2_dve, 11)
                for r in range(2):
                    dve.tensor_tensor(oh8[:, :, :, :].rearrange("p (q r) h j -> p q r h j", r=2)[:, :, r, :, :],
                                      av[:, r, :, 0:HD].unsqueeze(2).to_broadcast([P, PAIRS, HC, HD]),
                                      rs2[:, r, :].unsqueeze(2).unsqueeze(3).to_broadcast([P, PAIRS, HC, HD]), ALU.mult).then_inc(a2_dve, 1)
                for i in range(NT):
                    dve.wait_ge(a2_pe, 9 + (2 * i + 3 if i < NT - 1 else 2 * NT))
                    dve.scalar_tensor_tensor(out=xs[:, i, :], in0=ps[:, 4 + i % 2, 0:D], scalar=gates[:, 2:3], in1=xs[:, i, :],
                                             op0=ALU.mult, op1=ALU.add).then_inc(x_done, 1)

            if "attn2" in N:
                attn2(N["attn2"])
            if "ffn2" in N:
                moe(2, N["ffn2"])
            if "attn3" in N:
                mha(3, 1, N["attn3"])
            if "ffn3" in N:
                moe(3, N["ffn3"])


ATTN = {0: [f"L0_xattn_W{n}" for n in "qkvo"], 1: [f"L1_xattn_W{n}" for n in "qkvo"], 3: [f"L3_xattn_w{n}_kernel" for n in "qkvo"]}
INS = ["x", "ctx_1024", "mask_BxS2_bf1", "mask_SxS2_bk1", "mask_BxSxS2_ik1", "g_xattn", "g_ffn",
       "L0_xattn_bk", "L0_xattn_bv", "L0_xattn_bo", "L0_xattn_gamma", "L0_xattn_beta",
       "L2_xattn_bv_h", "L0_ffn_br", "L3_ffn_gate_b", "L1_ffn_Wg", "L1_ffn_Wu", "L1_ffn_Wd"]
SUBS = ["attn0", "ffn0", "attn1", "ffn1", "attn2", "ffn2", "attn3", "ffn3"]


def kernel(**inputs):
    import concourse.bacc as bacc
    from concourse.bass_utils import run_bass_kernel_spmd as run

    def arr(n):
        return np.ascontiguousarray(inputs[n])

    def cols(n):
        return np.ascontiguousarray(arr(n).reshape(-1, P).T)

    arrays = {n: arr(n) for n in INS}
    arrays["L0_xattn_bq"] = cols("L0_xattn_bq")
    for layer, names in ((1, "L1_xattn_b{}"), (3, "L3_xattn_w{}_bias")):
        for n in "vo":
            arrays[f"L{layer}_b{n}"] = arr(names.format(n))
        for n in "qk":
            arrays[f"L{layer}_b{n}"] = cols(names.format(n))
    for layer in (0, 1):
        arrays[f"attn{layer}"] = np.stack([arr(n).T for n in ATTN[layer]])
    arrays["attn2"] = np.stack([arr(f"L2_xattn_W{n}").T for n in "qkv"] + [arr("L2_xattn_Wo")])
    arrays["attn2_heads"] = np.stack([arr(f"L2_xattn_w{n}_h") for n in "qkv"])
    arrays["attn2_bias"] = np.stack([arr(f"L2_xattn_b{n}_h") for n in "qk"], axis=1)
    for layer, (router, w, b) in {0: ("L0_ffn_Wr", "W", "b"), 2: ("L2_ffn_router_w", "w", "b"), 3: ("L3_ffn_gate_w", "w", "b")}.items():
        arrays[f"router{layer}"] = arr(router).T if layer == 2 else arr(router)
        arrays[f"router{layer}"] = np.ascontiguousarray(arrays[f"router{layer}"])
        for i in "12":
            arrays[f"L{layer}_w{i}"] = arr(f"L{layer}_ffn_{w}{i}")
            arrays[f"b{i}_{layer}"] = cols(f"L{layer}_ffn_b{i}")
    arrays["attn3"] = np.stack([arr(n) for n in ATTN[3]])
    nc = bacc.Bacc("TRN2", target_bir_lowering=False, num_devices=1)
    a = {n: nc.dram_tensor(f"in_{n}", v.shape, mybir.dt.from_np(v.dtype), kind="ExternalInput").ap() for n, v in arrays.items()}
    arrays = {f"in_{n}": v for n, v in arrays.items()}
    out = nc.dram_tensor("out", (B, SEQ, D), F32, kind="ExternalOutput").ap()
    build(nc, a, out, SUBS)
    r = run(nc, [arrays], core_ids=[0])
    return r.results[0]["out"]
```

```python
from contextlib import ExitStack

import numpy as np

import concourse.bass as bass
from concourse import mybir

ALU = mybir.AluOpType
ACT = mybir.ActivationFunctionType
AX = mybir.AxisListType
F32 = mybir.dt.float32
F32R = mybir.dt.float32r
BF16 = mybir.dt.bfloat16
U8 = mybir.dt.uint8
I32 = mybir.dt.int32
U32 = mybir.dt.uint32

P = 128
B, SEQ, D = 2, 1024, 256
S2 = 64
T = B * SEQ
NT = T // P
TB = NT // B
KD = D // P
GROUP = 4
GT = GROUP * P
NG = NT // GROUP
H, HD = 16, 16
HC = P // HD
PAIRS = H // 2
VC = 2 * HD + 2
E = 8
F = 1024
FC = F // P
LN_EPS = 1e-5
BIG = 3.0e38
MASKED = {1: -10000.0, 2: -1.0e9, 3: -1.0e9}

HALF = F // 2
FH = HALF // P
UNITS = 2 * E
SLOTS = 3 * P
CAP = {0: 256, 2: 384, 3: 320}
ITEMS = {0: T // 256 + E - 1, 2: E, 3: E}
IR = {0: 256, 2: 384, 3: 384}
TOPK = {0: 1, 2: 1, 3: 2}
LAG = 3
ROWS = 32 * P
FAR = float(1 << 20)
PIECE = 1024


def build(nc, a, out, subs):
    with ExitStack() as ctx:
        def sb(name, shape, dt=F32, stack=ctx):
            return stack.enter_context(nc.sbuf_tensor(name, shape, dt))

        def sem(name):
            return ctx.enter_context(nc.semaphore(name))

        xs = sb("xs", [P, NT, D])
        lnx = sb("lnx", [P, NT, D])
        xT = sb("xT", [P, KD, T])
        ident = sb("ident", [P, P])
        ones = sb("ones", [P, 1])
        eps = sb("eps", [P, 1])
        hmask = sb("hmask", [P, HC])
        zero = sb("zero", [P, 1])
        primer = sb("primer", [P, 8])
        gates = sb("gates", [P, 8])
        gates_raw = sb("gates_raw", [P, 8])
        ctx_sb = sb("ctx_sb", [P, D])
        ctxT = sb("ctxT", [P, KD, P])
        bn = sb("bn", [P, NT, 6])
        st_sum, st_dif, st_m2, st_sq, st_var, st_std, st_rstd, st_mean = (
            sb(n, [P, NT]) for n in ("st_sum", "st_dif", "st_m2", "st_sq", "st_var", "st_std", "st_rstd", "st_mean"))
        wat = sb("wat", [P, 4, KD, D])
        wraw = sb("wraw", [P, 4, PIECE])
        whi = sb("whi", [P, 2, 4, PIECE], F32R)
        wlo = sb("wlo", [P, 2, 4, PIECE], F32R)
        ps = ctx.enter_context(nc.psum_tensor("ps", [P, 8, 512], F32))

        wr = sb("wr", [P, 4, KD, E])
        rb = sb("rb", [P, 4, E])
        b1c = sb("b1c", [P, 4, E * FC])
        b2c = sb("b2c", [P, 4, E * KD])
        tri = sb("tri", [P, P], BF16)
        ones_b = sb("ones_b", [P, P], BF16)
        mask_b = sb("mask_b", [P, NT, E], BF16)
        desc = sb("desc", [P, E])
        first_row = sb("first_row", [P, E])
        r_p, r_e, r_key, r_oh1, r_oh2, r_keep, r_pos = (
            sb(n, [P, NT, E]) for n in ("r_p", "r_e", "r_key", "r_oh1", "r_oh2", "r_keep", "r_pos"))
        r_grid = sb("r_grid", [P, NT, E])
        r_count, r_items, r_upto = (sb(n, [P, E]) for n in ("r_count", "r_items", "r_upto"))
        steps = sb("steps", [P, E])
        item_no = sb("item_no", [P, NT])
        item_expert = sb("item_expert", [P, NT], I32)
        r_m, r_s, r_k = (sb(n, [P, NT]) for n in ("r_m", "r_s", "r_k"))
        r_top, r_slot, r_kept, r_w = (sb(n, [P, 2, NT]) for n in ("r_top", "r_slot", "r_kept", "r_w"))
        sidx = sb("sidx", [P, 2, NT], U32)
        gidx = sb("gidx", [P, 2, NT], U32)
        xbuf = nc.dram_tensor("xbuf", (ROWS, D), F32, kind="Internal").ap()
        ybuf = nc.dram_tensor("ybuf", (ROWS, D), F32, kind="Internal").ap()
        xflat = xT[:, :, :].rearrange("p k t -> p (k t)")
        y_t = xflat[:, 0:KD * SLOTS].rearrange("p (k t) -> p k t", k=KD)
        y_row = xflat[:, 768:2304].rearrange("p (s j d) -> p s j d", s=2, j=3)
        x_row = xflat[:, 2304:3840].rearrange("p (s j d) -> p s j d", s=2, j=3)
        y_second = xflat.rearrange("p (t d) -> p t d", t=NT)

        with ExitStack() as attn_mem:
            def asb(name, shape, dt=F32):
                return sb(name, shape, dt, attn_mem)
            brow = asb("brow", [P, 5, D])
            bcol = asb("bcol", [P, 4])
            ctxD = asb("ctxD", [P, KD, B, 2, S2])
            bmask = asb("bmask", [P, NT, S2])
            mask8 = asb("mask8", [P, TB, S2], U8)
            mask32 = asb("mask32", [P, NT, S2], I32)
            sc = asb("sc", [P, 2, H, S2])
            smax = asb("smax", [P, 2, H])
            pt = asb("pt", [P, PAIRS, P])
            rsum = asb("rsum", [P, PAIRS, 2])
            oh = asb("oh", [P, D])
            ot = asb("ot", [P, KD, P])
            mha_mem = attn_mem.enter_context(ExitStack())
            kblk = sb("kblk", [P, B, KD, HC, S2], stack=mha_mem)
            vblk = sb("vblk", [P, B, PAIRS, VC], stack=mha_mem)
            kt = sb("kt", [P, KD, P], stack=mha_mem)
            qt = sb("qt", [P, 2, KD, P], stack=mha_mem)
            mha_mem.close()
            a2_mem = attn_mem.enter_context(ExitStack())
            wh = sb("wh", [P, 3, KD, HD], stack=a2_mem)
            wqkv = sb("wqkv", [P, 3, KD, HD], stack=a2_mem)
            wo8 = sb("wo8", [P, D], stack=a2_mem)
            bh = sb("bh", [HD, 2], stack=a2_mem)
            bvh = sb("bvh", [P, HD], stack=a2_mem)
            khT = sb("khT", [HD, B, S2], stack=a2_mem)
            vh = sb("vh", [P, B, HD + 1], stack=a2_mem)
            qhT = sb("qhT", [HD, T], stack=a2_mem)
            oh8 = sb("oh8", [P, NT, HC, HD], stack=a2_mem)
            rs2 = sb("rs2", [P, 2, PAIRS], stack=a2_mem)
            ot8 = sb("ot8", [P, 2, P], stack=a2_mem)
        with ExitStack() as a0_mem:
            def asb(name, shape, dt=F32):
                return sb(name, shape, dt, a0_mem)
            brow0 = asb("brow0", [P, 5, D])
            bcol0 = asb("bcol0", [P, KD])
            k0 = asb("k0", [P, D])
            k0_min = asb("k0_min", [P, D])
            v0 = asb("v0", [P, D])
            kv0 = asb("kv0", [P, B, KD, D])
            ksum0 = asb("ksum0", [P, B, KD])
            q_min = asb("q_min", [P, KD, GT])
            q_relu = asb("q_relu", [P, KD, GT])
            q_den = asb("q_den", [P, KD, GT])
            q_o = asb("q_o", [P, KD, GT])
        xTh = sb("xTh", [P, KD, T], F32R)
        xTl = sb("xTl", [P, KD, T], F32R)
        h_act = sb("h_act", [P, 2, GT])
        h_32 = sb("h_32", [P, 2, GT])
        h_hi = sb("h_hi", [P, FH, GT], F32R)
        h_lo = sb("h_lo", [P, FH, GT], F32R)

        in_ctx, in_gate = sem("in_ctx"), sem("in_gate")
        in_x = [sem(f"in_x{g}") for g in range(NG)]
        in_wat, in_bias, in_mask = sem("in_wat"), sem("in_bias"), sem("in_mask")
        const_done, gates_done = sem("const_done"), sem("gates_done")
        ctx_tr, ctxT_done = sem("ctx_tr"), sem("ctxT_done")
        bn_done, var_done, std_done, ln_done = sem("bn_done"), sem("var_done"), sem("std_done"), sem("ln_done")
        tr_done, xt_done, xl_done = sem("tr_done"), sem("xt_done"), sem("xl_done")
        x_done, link_s, out_done = sem("x_done"), sem("link_s"), sem("out_done")
        a0_kv, a0_kmin, a0_kexp, a0_k, a0_kvcopy = (
            sem(f"a0_{n}") for n in ("kv", "kmin", "kexp", "k", "kvcopy"))
        a0_q, a0_qmin, a0_qexp, a0_den, a0_num, a0_o, a0_proj, a0_res, a0_bo, a0_gam, a0_nrm, a0_beta = (
            sem(f"a0_{n}") for n in
            ("q", "qmin", "qexp", "den", "num", "o", "proj", "res", "bo", "gam", "nrm", "beta"))
        w_in = [sem(f"w_in{q}") for q in range(4)]
        w_hi, w_lo, w_used = sem("w_hi"), sem("w_lo"), sem("w_used")
        f_up, f_act, f_h, f_hi, f_lo, f_used, f_yevac, f_back = (
            sem(f"f_{n}") for n in ("up", "act", "h", "hi", "lo", "used", "yevac", "back"))
        m_kv, m_kt, m_kblk, m_q, m_qt, m_s, m_min, m_max, m_sub, m_exp = (
            sem(f"m_{n}") for n in ("kv", "kt", "kblk", "q", "qt", "s", "min", "max", "sub", "exp"))
        m_ptr, m_pta, m_ptd, m_av, m_rs, m_oh, m_otr, m_ot, m_proj, m_bo = (
            sem(f"m_{n}") for n in ("ptr", "pta", "ptd", "av", "rs", "oh", "otr", "ot", "proj", "bo"))
        m_tab = sem("m_tab")
        in_moe, zeroed = sem("in_moe"), sem("zeroed")
        r_logits, r_sub, r_exp, r_mask, r_rank, r_idx = (sem(f"r_{n}") for n in ("logits", "sub", "exp", "mask", "rank", "idx"))
        scattered, x_tr, x_hi, x_lo, y_out, y_tr, y_copied = (
            sem(n) for n in ("scattered", "x_tr", "x_hi", "x_lo", "y_out", "y_tr", "y_copied"))
        m_act, y_half = sem("m_act"), sem("y_half")
        x_in = [sem("x_in0"), sem("x_in1")]
        y_st = [sem("y_st0"), sem("y_st1")]
        fetched = [sem(f"fetched{g}") for g in range(NG)]
        a2_pe, a2_act, a2_dve, a2_pool, in_a2 = (sem(f"a2_{n}") for n in ("pe", "act", "dve", "pool", "in"))

        def row(v, n):
            return v.rearrange("(o n) -> o n", o=1).to_broadcast([P, n])

        def col(v):
            return v

        block = ctx.enter_context(nc.Block())
        x_dram = a["x"].rearrange("b (t p) d -> p (b t) d", p=P)
        BIAS = {0: 96, 1: 64, 3: 64}
        bias_at = {0: 96, 1: 160, 3: 224}
        COUNTS = {f"ffn{l}": (4 * ITEMS[l], ITEMS[l], ITEMS[l] * FC, ITEMS[l]) for l in ITEMS}
        COUNTS["ffn1"] = (3 * UNITS, UNITS, UNITS * NG * FH, 0)
        PIECES, CHUNKS, EXPERTS = {}, {}, {}
        at = [0, 0, 0, 0]
        for name in subs:
            if name in COUNTS:
                PIECES[name], _, CHUNKS[name], EXPERTS[name] = at
                at = [x + y for x, y in zip(at, COUNTS[name])]
        LOADS, at = {}, [0, 0, 0, 0]
        for name in subs:
            if name in COUNTS:
                LOADS[name] = list(at)
                at = [x + COUNTS[name][1] * (q < 3 or name != "ffn1") for q, x in enumerate(at)]
        MOE = [l for l in (0, 2, 3) if f"ffn{l}" in subs]
        SENT, FETCHED, MC, ROW_LOADS = {}, {}, {}, {}
        for l in MOE:
            before = [b for b in MOE if b < l]
            MC[f"ffn{l}"] = sum(ITEMS[b] * FC for b in before)
            SENT[l] = NT * sum(TOPK[b] for b in before + [l])
            FETCHED[l] = GROUP * sum(TOPK[b] for b in before + [l])
            ROW_LOADS[l] = [sum((ITEMS[b] + 1 - s) // 2 for b in before) for s in range(2)]
        PRIMED = 4
        WAT = {layer: i + 1 for i, layer in enumerate(l for l in (0, 1, 2, 3) if f"attn{l}" in subs)}
        MASKS = {layer: i + 1 for i, layer in enumerate(l for l in (1, 2, 3) if f"attn{l}" in subs)}
        N = {name: i for i, name in enumerate(subs)}

        @block.sync
        def _(sp):
            for g in range(NG):
                sp.dma_start(xs[:, g * GROUP:(g + 1) * GROUP, :], x_dram[:, g * GROUP:(g + 1) * GROUP, :]).then_inc(in_x[g], 16)
                if g == 0:
                    sp.dma_start(ctx_sb[:, :], a["ctx_1024"].rearrange("b s d -> (b s) d")).then_inc(in_ctx, 16)
            sp.dma_start(gates_raw[:, 0:4], row(a["g_xattn"], 4)).then_inc(in_gate, 16)
            sp.dma_start(gates_raw[:, 4:8], row(a["g_ffn"], 4)).then_inc(in_gate, 16)

            def load_moe():
                for l in (0, 2, 3):
                    sp.dma_start(wr[:, l, :, :], a[f"router{l}"].rearrange("(k p) e -> p k e", p=P)).then_inc(in_moe, 16)
                    sp.dma_start(b1c[:, l, :], a[f"b1_{l}"]).then_inc(in_moe, 16)
                    sp.dma_start(b2c[:, l, :], a[f"b2_{l}"]).then_inc(in_moe, 16)
                sp.dma_start(rb[:, 0, :], row(a["L0_ffn_br"], E)).then_inc(in_moe, 16)
                sp.dma_start(rb[:, 3, :], row(a["L3_ffn_gate_b"], E)).then_inc(in_moe, 16)
                sp.wait_ge(zeroed, 1)
                for h in range(2):
                    sp.dma_start(xbuf.rearrange("(h p c) d -> h p (c d)", h=2, p=P)[h], wraw[:, :, :].rearrange("p q c -> p (q c)")).then_inc(zeroed, 16)

            def expert_weights(layer, e, u, pieces=range(4)):
                w1, w2 = a[f"L{layer}_w1"], a[f"L{layer}_w2"]
                for q in pieces:
                    sp.wait_ge(w_lo, PIECES[f"ffn{layer}"] + 4 * u + q + 1)
                    if q < 2:
                        sp.dma_start(wraw[:, q, :], w1.rearrange("e (k p) f -> e k p f", p=P)[e, q]).then_inc(w_in[q], 16)
                    else:
                        sp.dma_start(wraw[:, q, :].rearrange("p (c d) -> p c d", c=4),
                                     w2.rearrange("e (h c p) d -> e h p c d", h=2, p=P)[e, q - 2]).then_inc(w_in[q], 16)

            def moe(layer):
                name = f"ffn{layer}"
                nth = MOE.index(layer)
                items = ITEMS[layer]
                xrows = xbuf[0:items * IR[layer], :].rearrange("(e j p) d -> e p j d", e=items, p=P)
                yrows = ybuf[0:items * IR[layer], :].rearrange("(e j p) d -> e p j d", e=items, p=P)
                tiles = IR[layer] // P

                def store(e, s):
                    sp.wait_ge(y_copied, EXPERTS[name] + e + 1)
                    sp.dma_start(yrows[e], y_row[:, s, 0:tiles, :]).then_inc(y_st[s], 16)

                def rows(e, s):
                    if not isinstance(e, int) or e >= 2:
                        sp.wait_ge(x_tr, EXPERTS[name] + e - 1)
                    sp.dma_start(x_row[:, s, 0:tiles, :], xrows[e]).then_inc(x_in[s], 16)

                def expert_of(e):
                    return sp.value_load(item_expert[0:1, bass.ds(e, 1)], min_val=0, max_val=E - 1) if layer == 0 else e

                def step(e, s, stores=True, weights=True, loads=True):
                    if weights:
                        ex = expert_of(e + 2)
                        expert_weights(layer, ex, e + 2, (0, 1))
                    if stores:
                        store(e - 1, 1 - s)
                    if weights:
                        expert_weights(layer, ex, e + 2, (2, 3))
                    if loads:
                        rows(e + 3, 1 - s)
                if layer == 0:
                    sp.wait_ge(r_idx, 1)
                    expert_weights(0, expert_of(1), 1)
                sp.wait_ge(scattered, 16 * SENT[layer])
                for e in range(3):
                    rows(e, e % 2)
                step(0, 0, stores=False)
                pairs = (items - 4) // 2 * 2
                with sp.Fori(1, pairs, 2) as e:
                    step(e, 1)
                    step(e + 1, 0)
                for e in range(pairs + 1, items + 1):
                    step(e, e % 2, weights=e + 2 < items, loads=e + 3 < items)

            def load_wat(n):
                if n > 0:
                    before = max(l for l in range(n) if f"attn{l}" in N)
                    sp.wait_ge(x_done, NT * (N[f"attn{before}"] + 1))
                for i in range(4):
                    sp.dma_start(wat[:, i, :, :], a[f"attn{n}"][i].rearrange("(k p) e -> p k e", p=P)).then_inc(in_wat, 16)

            load_wat(0)
            for i, n in enumerate(("bk", "bv", "bo", "gamma", "beta")):
                sp.dma_start(brow0[:, i, :], row(a["L0_xattn_" + n], D)).then_inc(in_bias, 16)
            sp.dma_start(bcol0[:, :], col(a["L0_xattn_bq"])).then_inc(in_bias, 16)
            load_moe()

            def load_vectors(layer, n):
                sp.wait_ge(x_done, NT * n)
                for i, v in enumerate(("bv", "bo")):
                    sp.dma_start(brow[:, i, :], row(a[f"L{layer}_{v}"], D)).then_inc(in_bias, 16)
                for i, v in enumerate(("bq", "bk")):
                    sp.dma_start(bcol[:, KD * i:KD * (i + 1)], a[f"L{layer}_{v}"]).then_inc(in_bias, 16)
                if layer == 1:
                    sp.dma_start(mask8[:, 0:B, :], a["mask_BxS2_bf1"].rearrange("(o b) s -> o b s", o=1).to_broadcast([P, B, S2])).then_inc(in_mask, 16)
                else:
                    sp.dma_start(mask32[:, :, :], a["mask_BxSxS2_ik1"].rearrange("b (t p) s -> p (b t) s", p=P)).then_inc(in_mask, 16)

            def stream_ffn1():
                with sp.Fori(0, E) as e:
                    for half in range(2):
                        for q, src in enumerate((a["L1_ffn_Wg"], a["L1_ffn_Wu"], a["L1_ffn_Wd"])):
                            sp.wait_ge(w_lo, PIECES["ffn1"] + 6 * e + 3 * half + q + 2)
                            if q < 2:
                                sp.dma_start(wraw[:, q, :].rearrange("p (k f) -> p k f", k=KD),
                                             src.rearrange("e (k p) (h f) -> e h p k f", p=P, h=2)[e, half]).then_inc(w_in[q], 16)
                            else:
                                sp.dma_start(wraw[:, q, :].rearrange("p (c d) -> p c d", c=FH),
                                             src.rearrange("e (h c p) d -> e h p c d", h=2, p=P)[e, half]).then_inc(w_in[q], 16)

            def load_attn2(n):
                sp.wait_ge(x_done, NT * n)
                sp.dma_start(wh[:, :, :, :], a["attn2_heads"].rearrange("i (k p) j -> p i k j", p=P)).then_inc(in_a2, 16)
                sp.dma_start(bh[:, :], a["attn2_bias"]).then_inc(in_a2, 16)
                sp.dma_start(bvh[:, :], row(a["L2_xattn_bv_h"], HD)).then_inc(in_a2, 16)
                sp.dma_start(mask8[:, :, :], a["mask_SxS2_bk1"].rearrange("(t p) s -> p t s", p=P)).then_inc(in_mask, 16)

            sp.wait_ge(zeroed, 1 + 16 * 2)
            if "ffn0" in N:
                expert_weights(0, 0, 0)
            if "attn1" in N:
                load_wat(1)
            if "ffn0" in N:
                moe(0)
            if "attn1" in N:
                load_vectors(1, N["attn1"])
            if "ffn1" in N:
                stream_ffn1()
            if "attn2" in N:
                load_wat(2)
                load_attn2(N["attn2"])
            for layer in (2, 3):
                if layer == 3 and "attn3" in N:
                    load_vectors(3, N["attn3"])
                if f"ffn{layer}" in N:
                    sp.wait_ge(w_lo, PRIMED + PIECES[f"ffn{layer}"])
                    for e in range(2):
                        expert_weights(layer, e, e)
                if layer == 2 and "attn3" in N:
                    load_wat(3)
                if f"ffn{layer}" in N:
                    moe(layer)

            out_dram = out.rearrange("b (t p) d -> p (b t) d", p=P)
            for g in range(NG):
                sp.wait_ge(x_done, NT * (len(subs) - 1) + (g + 1) * GROUP)
                sp.dma_start(out_dram[:, g * GROUP:(g + 1) * GROUP, :], xs[:, g * GROUP:(g + 1) * GROUP, :]).then_inc(out_done, 16)
            sp.wait_ge(out_done, 16 * NG)

        @block.gpsimd
        def _(pool):
            pool.memset(ident[:, :], 0.0).then_inc(const_done, 1)
            pool.memset(ones[:, :], 1.0).then_inc(const_done, 1)
            pool.memset(eps[:, :], LN_EPS).then_inc(const_done, 1)
            pool.memset(zero[:, :], 0.0).then_inc(const_done, 1)
            pool.memset(hmask[:, :], 0.25).then_inc(const_done, 1)
            pool.wait_ge(const_done, 5)
            pool.affine_select(out=ident[:, :], in_=ident[:, :], compare_op=ALU.not_equal, fill=1.0,
                               base=0, pattern=[[-1, P]], channel_multiplier=1).then_inc(const_done, 1)
            pool.affine_select(out=hmask[:, :], in_=hmask[:, :], compare_op=ALU.is_ge, fill=0.0,
                               base=0, pattern=[[-HD, HC]], channel_multiplier=1).then_inc(const_done, 1)
            pool.wait_ge(const_done, 7)
            pool.affine_select(out=hmask[:, :], in_=hmask[:, :], compare_op=ALU.is_ge, fill=0.0,
                               base=HD - 1, pattern=[[HD, HC]], channel_multiplier=-1).then_inc(const_done, 1)

            pool.memset(wraw[:, :, :], 0.0).then_inc(zeroed, 1)
            pool.memset(ones_b[:, :], 1.0).then_inc(const_done, 1)
            pool.memset(tri[:, :], 1.0).then_inc(const_done, 1)
            pool.iota(desc[:, :], pattern=[[-1, E]], base=E, channel_multiplier=0, allow_small_or_imprecise_dtypes=True).then_inc(const_done, 1)
            pool.iota(first_row[:, :], pattern=[[SLOTS, E]], base=-1, channel_multiplier=0, allow_small_or_imprecise_dtypes=True).then_inc(const_done, 1)
            pool.iota(steps[:, :], pattern=[[IR[0], E]], base=0, channel_multiplier=0, allow_small_or_imprecise_dtypes=True).then_inc(const_done, 1)
            pool.iota(item_no[:, :], pattern=[[1, NT]], base=0, channel_multiplier=0, allow_small_or_imprecise_dtypes=True).then_inc(const_done, 1)
            pool.wait_ge(const_done, 14)
            pool.memset(steps[:, 0:1], -1.0).then_inc(const_done, 1)
            pool.affine_select(out=tri[:, :], in_=tri[:, :], compare_op=ALU.is_ge, fill=0.0,
                               base=0, pattern=[[1, P]], channel_multiplier=-1).then_inc(const_done, 1)
            pool.memset(primer[:, 5:6], 0.0).then_inc(y_out, PRIMED)
            for s in range(2):
                pool.memset(primer[:, 3 + s:4 + s], 0.0).then_inc(y_st[s], 16)
            pool.memset(primer[:, 0:1], 0.0).then_inc(w_lo, PRIMED)
            pool.memset(primer[:, 1:2], 0.0).then_inc(w_used, 2)
            pool.memset(primer[:, 2:3], 0.0).then_inc(f_used, 1)
            pool.memset(primer[:, 6:7], 0.0).then_inc(f_yevac, 1)

            pool.wait_ge(in_bias, bias_at[0])
            pool.wait_ge(gates_done, 1)
            pool.tensor_scalar(brow0[:, 3:5, :], brow0[:, 3:5, :], gates[:, 0:1], None, ALU.mult).then_inc(a0_beta, 1)
            pool.wait_ge(tr_done, NG)
            for i in range(NT):
                pool.tensor_tensor(lnx[:, i, :], lnx[:, i, :], brow0[:, 2, :], ALU.add).then_inc(a0_bo, 1)
            pool.wait_ge(a0_beta, 1)
            for i in range(NT):
                pool.tensor_tensor(xs[:, i, :], xs[:, i, :], brow0[:, 4, :], ALU.add).then_inc(a0_bo, 1)
            for i in range(NT):
                pool.wait_ge(a0_nrm, i + 1)
                pool.tensor_tensor(lnx[:, i, :], lnx[:, i, :], brow0[:, 3, :], ALU.mult).then_inc(a0_gam, 1)


            def mha(layer, m, n):
                pool.wait_ge(x_done, NT * n)
                for r in range(2):
                    pool.tensor_copy(ctxD[:, :, :, r, :], ctxT[:, :, :].rearrange("p k (b s) -> p k b s", b=B)).then_inc(m_tab, 1)
                pool.memset(vblk[:, :, :, :], 0.0).then_inc(m_tab, 1)
                pool.wait_ge(m_tab, 5 * m + 3)
                for r in range(2):
                    pool.memset(vblk[r * S2:(r + 1) * S2, :, :, 2 * HD + r:2 * HD + r + 1], 1.0).then_inc(m_tab, 1)
                pool.wait_ge(m_tab, 5 * m + 5)
                pool.wait_ge(in_bias, bias_at[layer])
                pool.tensor_scalar(brow[:, 2, :], brow[:, 1, :], gates[:, layer:layer + 1], None, ALU.mult).then_inc(m_bo, 1)
                pool.wait_ge(m_bo, (NT + 1) * m + 1)
                pool.wait_ge(ln_done, NT * (n + 1))
                for i in range(NT):
                    pool.tensor_tensor(xs[:, i, :], xs[:, i, :], brow[:, 2, :], ALU.add).then_inc(m_bo, 1)
                with pool.Fori(0, NT, 2) as i:
                    for j in range(2):
                        pool.wait_ge(m_max, NT * m + i + j + 1)
                        pool.tensor_tensor(sc[:, j, :, :], sc[:, j, :, :], smax[:, j, :].unsqueeze(2).to_broadcast([P, H, S2]),
                                           ALU.subtract).then_inc(m_sub, 1)

            def split(layer, ppu):
                def unit(u, s):
                    pool.wait_ge(w_used, u + 1)
                    for q in range(ppu):
                        done = PIECES[layer] + u * ppu + q + 1
                        pool.wait_ge(w_in[q], 16 * (LOADS[layer][q] + u + 1))
                        pool.tensor_tensor(whi[:, s, q, :], wraw[:, q, :], zero[:, :].to_broadcast([P, PIECE]), ALU.add).then_inc(w_hi, 1)
                        pool.wait_ge(w_hi, done)
                        pool.tensor_tensor(wlo[:, s, q, :], wraw[:, q, :], whi[:, s, q, :].bitcast(F32), ALU.subtract).then_inc(w_lo, 1)
                with pool.Fori(0, COUNTS[layer][1], 2) as u:
                    for s in range(2):
                        unit(u + s, s)

            def moe(layer):
                name = f"ffn{layer}"

                def lower(u, s):
                    for q in range(4):
                        pool.wait_ge(w_hi, PIECES[name] + 4 * u + q + 1)
                        pool.tensor_tensor(wlo[:, s, q, :], wraw[:, q, :], whi[:, s, q, :].bitcast(F32), ALU.subtract).then_inc(w_lo, 1)
                lower(0, 0)
                pool.wait_ge(zeroed, 1 + 16 * 2)
                pool.wait_ge(r_idx, MOE.index(layer) + 1)
                for c in range(TOPK[layer]):
                    for i in range(NT):
                        pool.indirect_dma_start(out=xbuf, out_offset=bass.IndirectOffsetOnAxis(ap=sidx[:, c, i:i + 1], axis=0),
                                                in_=lnx[:, i, :], in_offset=None, bounds_check=ROWS - 1, oob_is_err=False).then_inc(scattered, 16)
                last = (ITEMS[layer] - 1) // 2 * 2
                with pool.Fori(1, last, 2) as u:
                    lower(u, 1)
                    lower(u + 1, 0)
                for u in range(last + 1, ITEMS[layer]):
                    lower(u, 1)
                for s in range(2):
                    pool.wait_ge(y_st[s], 16 + 16 * (ROW_LOADS[layer][s] + (ITEMS[layer] + 1 - s) // 2))
                rows = ITEMS[layer] * IR[layer]
                for g in range(NG):
                    for c in range(TOPK[layer]):
                        for i in range(g * GROUP, (g + 1) * GROUP):
                            dst = lnx if c == 0 else y_second
                            pool.indirect_dma_start(out=dst[:, i, :], out_offset=None, in_=ybuf[0:rows, :],
                                                    in_offset=bass.IndirectOffsetOnAxis(ap=gidx[:, c, i:i + 1], axis=0),
                                                    bounds_check=rows - 1, oob_is_err=False).then_inc(fetched[g], 16)

            if "ffn0" in N:
                moe(0)
            if "attn1" in N:
                mha(1, 0, N["attn1"])
            if "ffn1" in N:
                split("ffn1", 3)

            if "attn2" in N:
                pool.wait_ge(x_done, NT * N["attn2"])
                for r in range(2):
                    pool.tensor_copy(ctxD[:, :, :, r, :], ctxT[:, :, :].rearrange("p k (b s) -> p k b s", b=B)).then_inc(a2_pool, 1)
                pool.memset(vh[:, :, HD:HD + 1], 1.0).then_inc(a2_pool, 1)
            if "ffn2" in N:
                moe(2)
            if "attn3" in N:
                mha(3, 1, N["attn3"])
            if "ffn3" in N:
                moe(3)

        @block.tensor
        def _(pe):
            def mm(out_, lhsT, rhs, start, stop):
                return pe.matmul(out_, lhsT, rhs, start=start, stop=stop)

            def turn_norm(n, wide=False, after=None):
                for g in range(NG):
                    pe.wait_ge(ln_done, NT * n + GROUP * (g + 1))
                    if g >= 2 and not wide:
                        pe.wait_ge(xt_done, NG * n + g - 1)
                    for t in range(GROUP):
                        for k in range(KD):
                            last = pe.transpose(ps[:, (g if wide else g % 2) * 2 + k, t * P:(t + 1) * P],
                                                lnx[:, g * GROUP + t, k * P:(k + 1) * P], ident[:, :])
                    last.then_inc(tr_done, 1)
                    if after and g >= 1:
                        after(g - 1)
                if after:
                    after(NG - 1)

            pe.wait_ge(const_done, 8)
            pe.wait_ge(in_ctx, 16)
            for k in range(KD):
                last = pe.transpose(ps[:, 7, k * P:(k + 1) * P], ctx_sb[:, k * P:(k + 1) * P], ident[:, :])
            last.then_inc(ctx_tr, 1)

            def attn0():
                turn_norm(0)
                pe.wait_ge(ctxT_done, 1)
                pe.wait_ge(in_wat, 64)
                for i in (0, 1):
                    for k in range(KD):
                        last = mm(ps[:, 4 + i, 0:D], ctxT[:, k, :], wat[:, 1 + i, k, :], k == 0, k == KD - 1)
                last.then_inc(a0_kv, 1)
                pe.wait_ge(xt_done, NG)

                def query(s):
                    j, b = divmod(s, B)
                    blk = slice((j + b * (NG // B)) * GT, (j + b * (NG // B) + 1) * GT)
                    for c in range(KD):
                        for k in range(KD):
                            last = mm(ps[:, c, :], wat[:, 0, k, c * P:(c + 1) * P], xT[:, k, blk], k == 0, k == KD - 1)
                    last.then_inc(a0_q, 1)
                query(0)
                pe.wait_ge(a0_k, 2)
                for b in range(B):
                    r = slice(b * S2, (b + 1) * S2)
                    for k in range(KD):
                        mm(ps[:, 6 + b, k * D:(k + 1) * D], k0[r, k * P:(k + 1) * P], v0[r, :], True, True)
                        last = mm(ps[:, 4 + b, k:k + 1], k0[r, k * P:(k + 1) * P], ones[r, :], True, True)
                last.then_inc(a0_num, 1)
                pe.wait_ge(a0_kvcopy, 1)
                for s in range(NG):
                    b = s % B
                    pe.wait_ge(a0_qexp, 3 * s + 3)
                    pe.wait_ge(a0_den, s + 2)
                    for c in range(KD):
                        for k in range(KD):
                            last = mm(ps[:, 2 + c, :], kv0[:, b, k, c * P:(c + 1) * P], q_relu[:, k, :], k == 0, k == KD - 1)
                    last.then_inc(a0_num, 1)
                    if s + 1 < NG:
                        query(s + 1)
                    pe.wait_ge(a0_o, s + 1)
                    if s > 0:
                        pe.wait_ge(a0_res, 8 * s)
                    for t in range(GROUP):
                        for c in range(KD):
                            last = mm(ps[:, 4 + t // 2, (t % 2) * D:(t % 2 + 1) * D], q_o[:, c, t * P:(t + 1) * P],
                                      wat[:, 3, c, :], c == 0, c == KD - 1)
                    last.then_inc(a0_proj, 1)
            attn0()

            def mha(layer, m, n):
                pe.wait_ge(in_wat, 64 * WAT[layer])
                pe.wait_ge(m_tab, 5 * m + 2)
                pe.wait_ge(x_done, NT * n)
                for c in range(KD):
                    for k in range(KD):
                        mm(ps[:, 4, c * P:(c + 1) * P], wat[:, 1, k, c * P:(c + 1) * P], ctxT[:, k, :], k == 0, k == KD - 1)
                for b in range(B):
                    for k in range(KD):
                        last = mm(ps[:, 5, b * D:(b + 1) * D], ctxD[:, k, b, :, :], wat[:, 2, k, :], k == 0, k == KD - 1)
                last.then_inc(m_kv, 1)
                turn_norm(n)
                pe.wait_ge(xt_done, NG * (n + 1))
                pe.wait_ge(m_kblk, 8 * (m + 1))
                pe.wait_ge(m_tab, 5 * (m + 1))
                base = NT * m

                def query(i):
                    for c in range(KD):
                        for k in range(KD):
                            last = mm(ps[:, 0, c * P:(c + 1) * P], wat[:, 0, k, c * P:(c + 1) * P], xT[:, k, bass.ts(i, P)], k == 0, k == KD - 1)
                    last.then_inc(m_q, 1)

                def scores(i, first=False):
                    pe.wait_ge(m_qt, 2 * (base + i + 1))
                    if not first:
                        pe.wait_ge(m_min, base + i)
                    for c in range(KD):
                        last = mm(ps[:, 1 + c, :], qt[:, 0, c, :], kblk[:, i // TB, c, :, :], True, True)
                    last.then_inc(m_s, 1)

                def turn_probs(i, j):
                    pe.wait_ge(m_exp, base + i + 1)
                    for q in range(PAIRS):
                        last = pe.transpose(ps[:, 3 + q // 4, (q % 4) * P:(q % 4 + 1) * P], sc[:, j, 2 * q:2 * q + 2, :], ident[:, :])
                    last.then_inc(m_ptr, 1)

                def values(i):
                    pe.wait_ge(m_pta, base + i + 1)
                    pe.wait_ge(m_ptd, base + i + 1)
                    for q in range(PAIRS):
                        last = mm(ps[:, 5, q * VC:(q + 1) * VC], pt[:, q, :], vblk[:, i // TB, q, :], True, True)
                    last.then_inc(m_av, 1)

                def turn_heads(i):
                    pe.wait_ge(m_oh, base + i + 1)
                    for c in range(KD):
                        last = pe.transpose(ps[:, 6, c * P:(c + 1) * P], oh[:, c * P:(c + 1) * P], ident[:, :])
                    last.then_inc(m_otr, 1)

                def output(i):
                    pe.wait_ge(m_ot, base + i + 1)
                    if n > 0 or not isinstance(i, int) or i > 0:
                        pe.wait_ge(x_done, NT * n + i)
                    for c in range(KD):
                        last = mm(ps[:, 7, 0:D], ot[:, c, :], wat[:, 3, c, :], c == 0, c == KD - 1)
                    last.then_inc(m_proj, 1)

                def step(i, j, first=False, ahead=True):
                    if ahead:
                        query(i + 2)
                    turn_probs(i, j)
                    if not first:
                        turn_heads(i - 1)
                    if ahead:
                        scores(i + 2)
                    if not first:
                        output(i - 1)
                    values(i)
                query(0)
                scores(0, True)
                query(1)
                scores(1)
                step(0, 0, first=True)
                with pe.Fori(1, NT - 4, 2) as i:
                    step(i, 1)
                    step(i + 1, 0)
                step(NT - 3, 1)
                step(NT - 2, 0, ahead=False)
                step(NT - 1, 1, ahead=False)
                turn_heads(NT - 1)
                output(NT - 1)

            def ffn1(n):
                shared = CHUNKS["ffn1"]
                turn_norm(n, wide=True)
                pe.wait_ge(xt_done, NG * n + 3)
                pe.wait_ge(xl_done, 3)

                def up(c, s, f, blk, start=False, left=False):
                    if not (start and f < 2):
                        pe.wait_ge(f_h, c - 1)
                    tok = bass.ts(blk, GT)
                    for q in range(2):
                        for k in range(KD):
                            w = slice(k * HALF + f * P, k * HALF + (f + 1) * P)
                            o = ps[:, (f % 2) * 2 + q, :]
                            first = mm(o, whi[:, s, q, w], xTh[:, k, tok], k == 0, False)
                            if left and q == k == 0:
                                first.then_inc(w_used, 1)
                            mm(o, whi[:, s, q, w], xTl[:, k, tok], False, False)
                            last = mm(o, wlo[:, s, q, w], xTh[:, k, tok], False, k == KD - 1)
                    last.then_inc(f_up, 1)

                def down(c, s, f):
                    pe.wait_ge(f_lo, shared + c + 1)
                    if f == 0:
                        pe.wait_ge(f_yevac, c // FH + 1)
                    for d in range(KD):
                        w = slice(f * D + d * P, f * D + (d + 1) * P)
                        o = ps[:, 4 + d, :]
                        mm(o, whi[:, s, 2, w], h_hi[:, f, :], f == 0, False)
                        mm(o, whi[:, s, 2, w], h_lo[:, f, :], False, False)
                        last = mm(o, wlo[:, s, 2, w], h_hi[:, f, :], False, f == FH - 1)
                    last.then_inc(f_used, 1)

                def unit(u, s, start=False):
                    pe.wait_ge(w_lo, PRIMED + PIECES["ffn1"] + 3 * u + 2)
                    c0 = u * (NG * FH)
                    for f in range(FH):
                        up(c0 + f, s, f, 0, start, left=f == 2 and not start)
                        if f == 2:
                            pe.wait_ge(w_lo, PRIMED + PIECES["ffn1"] + 3 * (u + 1))
                        if f >= 2:
                            down(c0 + f - 2, s, f - 2)
                        elif not start:
                            down(c0 + f - 2, 1 - s, f + 2)
                    if start:
                        pe.wait_ge(xt_done, NG * (n + 1))
                        pe.wait_ge(xl_done, NG)
                    with pe.Fori(1, NG) as blk:
                        for f in range(FH):
                            c = c0 + blk * FH + f
                            up(c, s, f, blk)
                            down(c - 2, s, (f + 2) % FH)

                unit(0, 0, start=True)
                with pe.Fori(1, UNITS - 1, 2) as u:
                    unit(u, 1)
                    unit(u + 1, 0)
                unit(UNITS - 1, 1)
                last_c = UNITS * NG * FH
                down(last_c - 2, 1, FH - 2)
                down(last_c - 1, 1, FH - 1)
                pe.wait_ge(f_yevac, UNITS * NG + 1)
                for i in range(NT):
                    if i >= 4:
                        pe.wait_ge(x_done, NT * n + i - 3)
                    for d in range(KD):
                        last = pe.transpose(ps[:, i % 4, d * P:(d + 1) * P], xT[:, d, i * P:(i + 1) * P], ident[:, :])
                        if i == d == 0:
                            last.then_inc(w_used, 1)
                    last.then_inc(f_back, 1)

            def moe(layer, n):
                name = f"ffn{layer}"
                nth, cap, items, tiles = MOE.index(layer), CAP[layer], ITEMS[layer], IR[layer] // P
                pe.wait_ge(in_moe, 16 * 11)

                def router(g):
                    pe.wait_ge(xt_done, NG * n + g + 1)
                    for i in range(g * GROUP, (g + 1) * GROUP):
                        for k in range(KD):
                            last = mm(ps[:, 4, i * E:(i + 1) * E], xT[:, k, i * P:(i + 1) * P], wr[:, layer, k, :], k == 0, k == KD - 1)
                    if g == NG - 1:
                        last.then_inc(r_logits, 1)
                turn_norm(n, after=router)
                pe.wait_ge(r_mask, nth + 1)
                if layer == 0:
                    for i in range(NT):
                        pe.matmul(ps[:, 6, 0:E], ones_b[:, :], mask_b[:, i, :], start=(i == 0), stop=(i == NT - 1))
                rank = ps[:, 5, 0:NT * E].rearrange("p (t e) -> p t e", t=NT)
                pe.matmul(rank, tri[:, :], mask_b[:, :, :], start=True, stop=False, skip_group_check=True)
                for i in range(NT - 1):
                    last = pe.matmul(rank[:, i + 1:NT, :], ones_b[:, :], mask_b[:, i:i + 1, :].to_broadcast([P, NT - 1 - i, E]),
                                     start=False, stop=(i == NT - 2), skip_group_check=True)
                last.then_inc(r_rank, 1)

                def turn_rows(e, s):
                    pe.wait_ge(x_in[s], 16 * (ROW_LOADS[layer][s] + 1) + 8 * (e - s))
                    for k in range(KD):
                        for j in range(tiles):
                            last = pe.transpose(ps[:, 6 + k, j * P:(j + 1) * P], x_row[:, s, j, k * P:(k + 1) * P], ident[:, :])
                    last.then_inc(x_tr, 1)

                def up(e, s, f, start=False):
                    c = CHUNKS[name] + e * FC + f
                    if f == 0:
                        pe.wait_ge(w_lo, PRIMED + PIECES[name] + 4 * e + 2)
                        pe.wait_ge(x_lo, EXPERTS[name] + e + 1)
                    if not start or f >= 2:
                        pe.wait_ge(m_act, MC[name] + e * FC + f - 1)
                    w = slice(f * P, (f + 1) * P)
                    tok = slice(s * GT * 2, s * GT * 2 + cap)
                    o = ps[:, f % 2, 0:cap]
                    for k in range(KD):
                        mm(o, whi[:, s, k, w], xTh[:, k, tok], k == 0, False)
                        mm(o, whi[:, s, k, w], xTl[:, k, tok], False, False)
                        last = mm(o, wlo[:, s, k, w], xTh[:, k, tok], False, k == KD - 1)
                    last.then_inc(f_up, 1)

                def down(e, s, f):
                    c = CHUNKS[name] + e * FC + f
                    if f % 4 == 0:
                        pe.wait_ge(w_lo, PRIMED + PIECES[name] + 4 * e + 3 + f // 4)
                    pe.wait_ge(f_lo, c + 1)
                    if f == 0:
                        pe.wait_ge(y_out, PRIMED + EXPERTS[name] + e - 1)
                    for d in range(KD):
                        w = slice((f % 4) * D + d * P, (f % 4) * D + (d + 1) * P)
                        q = 2 + f // 4
                        o = ps[:, 2 + 2 * s + d, 0:cap]
                        mm(o, whi[:, s, q, w], h_hi[:, f % 4, 0:cap], f == 0, False)
                        mm(o, whi[:, s, q, w], h_lo[:, f % 4, 0:cap], False, False)
                        last = mm(o, wlo[:, s, q, w], h_hi[:, f % 4, 0:cap], False, f == FC - 1)
                    last.then_inc(f_used, 1)

                def turn_back(e, s):
                    pe.wait_ge(y_out, PRIMED + EXPERTS[name] + e + 1)
                    for j in range(tiles):
                        for k in range(KD):
                            o = ps[:, 6 + j // 2, (j % 2) * D + k * P:(j % 2) * D + (k + 1) * P]
                            last = pe.transpose(o, y_t[:, k, j * P:(j + 1) * P], ident[:, :])
                    last.then_inc(y_tr, 1)

                def expert(e, s, start=False, end=False):
                    for f in range(FC):
                        up(e, s, f, start)
                        if f >= LAG:
                            down(e, s, f - LAG)
                        elif not start:
                            down(e - 1, 1 - s, f + FC - LAG)
                        if f == 1 and not end:
                            turn_rows(e + 1, 1 - s)
                        if f == LAG + 2 and not start:
                            if not end:
                                pe.wait_ge(x_lo, EXPERTS[name] + e + 2)
                            turn_back(e - 1, 1 - s)

                turn_rows(0, 0)
                expert(0, 0, start=True)
                pairs_end = items - 1 - items % 2 * 2
                with pe.Fori(1, pairs_end, 2) as e:
                    expert(e, 1)
                    expert(e + 1, 0)
                for e in range(pairs_end + items % 2, items):
                    expert(e, e % 2, end=e == items - 1)
                last_slot = (items - 1) % 2
                for f in range(FC - LAG, FC):
                    down(items - 1, last_slot, f)
                turn_back(items - 1, last_slot)

            if "ffn0" in N:
                moe(0, N["ffn0"])
            if "attn1" in N:
                mha(1, 0, N["attn1"])
            if "ffn1" in N:
                ffn1(N["ffn1"])

            def attn2(n):
                turn_norm(n)
                pe.wait_ge(in_wat, 64 * WAT[2])
                pe.wait_ge(in_a2, 48)
                for i in range(3):
                    for c in range(KD):
                        for k in range(KD):
                            last = mm(ps[:, 4, (i * KD + c) * HD:(i * KD + c + 1) * HD], wat[:, i, k, c * P:(c + 1) * P],
                                      wh[:, i, k, :], k == 0, k == KD - 1)
                last.then_inc(a2_pe, 1)
                pe.wait_ge(a2_dve, 2)
                pe.wait_ge(a2_pool, 2)
                for k in range(KD):
                    mm(ps[0:HD, 5, 0:P], wqkv[:, 1, k, :], ctxT[:, k, :], k == 0, k == KD - 1)
                for b in range(B):
                    for k in range(KD):
                        last = mm(ps[:, 6, b * HD:(b + 1) * HD], ctxD[:, k, b, :, :], wqkv[:, 2, k, :], k == 0, k == KD - 1)
                last.then_inc(a2_pe, 1)
                pe.wait_ge(xt_done, NG * (n + 1))
                for g in range(NG):
                    for k in range(KD):
                        last = mm(ps[0:HD, g, :], wqkv[:, 0, k, :], xT[:, k, g * GT:(g + 1) * GT], k == 0, k == KD - 1)
                    last.then_inc(a2_pe, 1)
                pe.wait_ge(a2_act, 1 + NG)
                pe.wait_ge(a2_dve, 5)
                for i in range(NT):
                    last = mm(ps[:, 4 + i // TB, (i % TB) * S2:(i % TB + 1) * S2], qhT[:, i * P:(i + 1) * P], khT[:, i // TB, :], True, True)
                last.then_inc(a2_pe, 1)
                pe.wait_ge(a2_act, 2 + NG)
                for q in range(PAIRS):
                    last = pe.transpose(ps[:, 6 + q // 4, (q % 4) * P:(q % 4 + 1) * P], sc[:, 0, 2 * q:2 * q + 2, :], ident[:, :])
                last.then_inc(a2_pe, 1)
                pe.wait_ge(a2_act, 3 + NG)
                pe.wait_ge(a2_dve, 10)
                for q in range(PAIRS):
                    for r in range(2):
                        h = slice(r * S2, (r + 1) * S2)
                        last = mm(ps[:, r, q * (HD + 1):(q + 1) * (HD + 1)], pt[h, q, :], vh[h, 2 * q // TB, :], True, True)
                last.then_inc(a2_pe, 1)
                pe.wait_ge(a2_dve, 13)
                for i in range(NT + 1):
                    if i < NT:
                        if i >= 2:
                            pe.wait_ge(a2_act, 3 + NG + i - 1)
                        pe.transpose(ps[:, 2 + i % 2, 0:P], oh8[:, i, :, :], ident[:, :]).then_inc(a2_pe, 1)
                    if i > 0:
                        pe.wait_ge(a2_act, 3 + NG + i)
                        if i > 2:
                            pe.wait_ge(x_done, NT * n + i - 2)
                        mm(ps[:, 4 + (i - 1) % 2, 0:D], ot8[:, (i - 1) % 2, :], wo8[:, :], True, True).then_inc(a2_pe, 1)

            if "attn2" in N:
                attn2(N["attn2"])
            if "ffn2" in N:
                moe(2, N["ffn2"])
            if "attn3" in N:
                mha(3, 1, N["attn3"])
            if "ffn3" in N:
                moe(3, N["ffn3"])

        @block.scalar
        def _(act):
            act.wait_ge(in_gate, 32)
            act.activation(gates[:, :], gates_raw[:, :], ACT.Tanh).then_inc(gates_done, 1)
            act.wait_ge(ctx_tr, 1)
            act.activation(ctxT[:, :, :], ps[:, 7, 0:D].rearrange("p (k s) -> p k s", k=KD), ACT.Copy).then_inc(ctxT_done, 1)

            def std(n):
                act.wait_ge(var_done, n + 1)
                act.activation(st_std[:, :], st_var[:, :], ACT.Sqrt, bias=eps[:, :]).then_inc(std_done, 1)

            def copy_turned(n, dst, wide=False):
                for g in range(NG):
                    act.wait_ge(tr_done, NG * n + g + 1)
                    act.activation(dst[:, :, g * GT:(g + 1) * GT], ps[:, (g if wide else g % 2) * 2:(g if wide else g % 2) * 2 + 2, :],
                                   ACT.Copy).then_inc(xt_done, 1)

            act.wait_ge(const_done, 8)
            std(0)
            copy_turned(0, xT)
            act.wait_ge(a0_kmin, 1)
            act.activation(k0_min[:, :], k0_min[:, :], ACT.Exp).then_inc(a0_kexp, 1)
            with act.Fori(0, NG // B) as j:
                for b in range(B):
                    s = j * B + b
                    act.wait_ge(a0_q, s + 1)
                    act.wait_ge(a0_num, s + 1)
                    for c in range(KD):
                        act.wait_ge(a0_qmin, 2 * s + c + 1)
                        act.activation(q_relu[:, c, :], ps[:, c, :], ACT.Relu, bias=bcol0[:, c:c + 1]).then_inc(a0_qexp, 1)
                    act.activation(q_min[:, :, :], q_min[:, :, :], ACT.Exp).then_inc(a0_qexp, 1)
            std(1)

            def mha(layer, m, n):
                std(n + 1)
                act.wait_ge(m_kv, m + 1)
                act.wait_ge(in_bias, bias_at[layer])
                for c in range(KD):
                    act.activation(kt[:, c, :], ps[:, 4, c * P:(c + 1) * P], ACT.Identity, bias=bcol[:, KD + c:KD + c + 1]).then_inc(m_kt, 1)
                copy_turned(n, xT)
                base = NT * m

                def query(i):
                    act.wait_ge(m_q, base + i + 1)
                    for c in range(KD):
                        act.activation(qt[:, 0, c, :], ps[:, 0, c * P:(c + 1) * P], ACT.Identity, bias=bcol[:, c:c + 1]).then_inc(m_qt, 1)

                def exps(i, j):
                    act.wait_ge(m_sub, base + i + 1)
                    act.activation(sc[:, j, :, :], sc[:, j, :, :], ACT.Exp).then_inc(m_exp, 1)

                def probs(i):
                    act.wait_ge(m_ptr, base + i + 1)
                    act.activation(pt[:, 0:4, :], ps[:, 3, :].rearrange("p (q t) -> p q t", q=4), ACT.Copy).then_inc(m_pta, 1)

                def heads(i):
                    act.wait_ge(m_otr, base + i + 1)
                    act.activation(ot[:, :, :], ps[:, 6, 0:D].rearrange("p (c t) -> p c t", c=KD), ACT.Copy).then_inc(m_ot, 1)

                def step(i, j, first=False, queries=True, more=True):
                    if queries:
                        query(i + 2)
                    probs(i)
                    if not first:
                        heads(i - 1)
                    if more:
                        exps(i + 1, 1 - j)
                query(0)
                query(1)
                exps(0, 0)
                step(0, 0, first=True)
                with act.Fori(1, NT - 4, 2) as i:
                    step(i, 1)
                    step(i + 1, 0)
                step(NT - 3, 1)
                step(NT - 2, 0, queries=False)
                step(NT - 1, 1, queries=False, more=False)
                heads(NT - 1)

            def ffn1(n):
                shared = CHUNKS["ffn1"]
                std(n + 1)
                copy_turned(n, xTh, wide=True)

                def silu(c, f):
                    act.wait_ge(f_up, shared + c + 1)
                    act.activation(h_act[:, f % 2, :], ps[:, (f % 2) * 2, :], ACT.Silu).then_inc(f_act, 1)

                def upper(c, f):
                    act.wait_ge(f_h, c + 1)
                    act.wait_ge(f_used, shared + c - FH + 2)
                    act.activation(h_hi[:, f, :], h_32[:, f % 2, :], ACT.Copy).then_inc(f_hi, 1)

                for f in range(FH):
                    silu(f, f)
                    if f > 0:
                        act.wait_ge(f_h, f)
                        act.activation(h_hi[:, f - 1, :], h_32[:, (f - 1) % 2, :], ACT.Copy).then_inc(f_hi, 1)
                with act.Fori(1, UNITS * NG) as blk:
                    for f in range(FH):
                        silu(blk * FH + f, f)
                        upper(blk * FH + f - 1, (f - 1) % FH)
                upper(UNITS * NG * FH - 1, FH - 1)

            def moe(layer, n):
                name = f"ffn{layer}"
                nth, cap, items, tiles = MOE.index(layer), CAP[layer], ITEMS[layer], IR[layer] // P
                func = {0: ACT.Relu, 2: ACT.Gelu, 3: ACT.Relu}[layer]

                def weights_upper(u, s, q):
                    act.wait_ge(w_in[q], 16 * (LOADS[name][q] + u + 1))
                    act.activation(whi[:, s, q, :], wraw[:, q, :], ACT.Copy).then_inc(w_hi, 1)
                for q in range(4):
                    weights_upper(0, 0, q)
                std(n + 1)
                copy_turned(n, xT)
                act.wait_ge(r_sub, nth + 1)
                act.activation(r_e[:, :, :], r_p[:, :, :], ACT.Exp).then_inc(r_exp, 1)

                def rows_upper(e, s):
                    act.wait_ge(x_tr, EXPERTS[name] + e + 1)
                    act.activation(xTh[:, :, s * GT * 2:s * GT * 2 + cap], ps[:, 6:8, 0:cap], ACT.Copy).then_inc(x_hi, 1)

                def hidden(e, f, ex, start=False):
                    c = CHUNKS[name] + e * FC + f
                    act.wait_ge(f_up, c + 1)
                    if not start or f >= 2:
                        act.wait_ge(f_hi, c - 1)
                        act.wait_ge(f_lo, c - 1)
                    act.activation(h_32[:, f % 2, 0:cap], ps[:, f % 2, 0:cap], func, bias=b1c[:, layer, bass.ds(ex * FC + f, 1)]).then_inc(m_act, 1)

                def upper(e, f, start=False):
                    c = CHUNKS[name] + e * FC + f
                    act.wait_ge(m_act, MC[name] + e * FC + f + 1)
                    if not (start and f < 3):
                        act.wait_ge(f_used, c - FH + 2)
                    act.activation(h_hi[:, f % 4, 0:cap], h_32[:, f % 2, 0:cap], ACT.Copy).then_inc(f_hi, 1)

                def expert(e, s, start=False, end=False):
                    ex = act.value_load(item_expert[0:1, bass.ds(e, 1)], min_val=0, max_val=E - 1) if layer == 0 else e
                    for f in range(FC):
                        hidden(e, f, ex, start)
                        if f > 0:
                            upper(e, f - 1, start)
                        elif not start:
                            upper(e - 1, FC - 1)
                        if f % 2 == 0 and not end:
                            if f == 4 and not start:
                                act.wait_ge(f_used, CHUNKS[name] + e * FC + 1)
                            weights_upper(e + 1, 1 - s, f // 2)
                        if f == 1 and not end:
                            rows_upper(e + 1, 1 - s)
                if layer == 0:
                    act.wait_ge(r_idx, 1)
                rows_upper(0, 0)
                expert(0, 0, start=True)
                pairs_end = items - 1 - items % 2 * 2
                with act.Fori(1, pairs_end, 2) as e:
                    expert(e, 1)
                    expert(e + 1, 0)
                for e in range(pairs_end + items % 2, items):
                    expert(e, e % 2, end=e == items - 1)
                last_slot = (items - 1) % 2
                upper(items - 1, FC - 1)

            if "ffn0" in N:
                moe(0, N["ffn0"])
            if "attn1" in N:
                mha(1, 0, N["attn1"])
            if "ffn1" in N:
                ffn1(N["ffn1"])

            def attn2(n):
                std(n + 1)
                copy_turned(n, xT)
                act.wait_ge(a2_pe, 1)
                act.activation(wqkv[:, :, :, :], ps[:, 4, 0:3 * KD * HD].rearrange("p (i k j) -> p i k j", i=3, k=KD), ACT.Copy).then_inc(a2_act, 1)
                for g in range(NG):
                    act.wait_ge(a2_pe, 3 + g)
                    act.activation(qhT[:, g * GT:(g + 1) * GT], ps[0:HD, g, :], ACT.Identity, bias=bh[:, 0:1]).then_inc(a2_act, 1)
                act.wait_ge(a2_dve, 9)
                act.activation(sc[:, 0, :, :], sc[:, 0, :, :], ACT.Exp).then_inc(a2_act, 1)
                act.wait_ge(a2_pe, 8)
                act.activation(pt[:, 0:4, :], ps[:, 6, :].rearrange("p (q t) -> p q t", q=4), ACT.Copy).then_inc(a2_act, 1)
                for i in range(NT):
                    act.wait_ge(a2_pe, 9 + (2 * i if i else 1))
                    act.activation(ot8[:, i % 2, :], ps[:, 2 + i % 2, 0:P], ACT.Copy).then_inc(a2_act, 1)

            if "attn2" in N:
                attn2(N["attn2"])
            if "ffn2" in N:
                moe(2, N["ffn2"])
            if "attn3" in N:
                mha(3, 1, N["attn3"])
            if "ffn3" in N:
                moe(3, N["ffn3"])

        @block.vector
        def _(dve):
            links = [0]

            def link(ins):
                links[0] += 1
                ins.then_inc(link_s, 1)
                dve.wait_ge(link_s, links[0])

            def stats(n):
                dve.wait_ge(bn_done, NT * (n + 1))
                dve.tensor_tensor(st_sum[:, :], bn[:, :, 1], bn[:, :, 4], ALU.add).then_inc(link_s, 1)
                dve.tensor_tensor(st_dif[:, :], bn[:, :, 1], bn[:, :, 4], ALU.subtract).then_inc(link_s, 1)
                links[0] += 2
                link(dve.tensor_tensor(st_m2[:, :], bn[:, :, 2], bn[:, :, 5], ALU.add))
                dve.tensor_scalar(st_mean[:, :], st_sum[:, :], 0.5, None, ALU.mult).then_inc(link_s, 1)
                links[0] += 1
                link(dve.scalar_tensor_tensor(out=st_sq[:, :], in0=st_dif[:, :], scalar=0.25, in1=st_dif[:, :], op0=ALU.mult, op1=ALU.mult))
                dve.scalar_tensor_tensor(out=st_var[:, :], in0=st_m2[:, :], scalar=1.0 / D, in1=st_sq[:, :],
                                         op0=ALU.mult, op1=ALU.add).then_inc(var_done, 1)
                dve.wait_ge(std_done, n + 1)
                link(dve.reciprocal(st_rstd[:, :], st_std[:, :]))

            def norm(n):
                stats(n + (n > 0))
                for i in range(NT):
                    dve.tensor_scalar(lnx[:, i, :], xs[:, i, :], st_mean[:, i:i + 1], st_rstd[:, i:i + 1],
                                      ALU.subtract, ALU.mult).then_inc(ln_done, 1)

            def next_stats(n, i):
                if n + 1 < len(subs):
                    dve.wait_ge(x_done, NT * n + i + 1)
                    dve.bn_stats(bn[:, i, :], xs[:, i, :]).then_inc(bn_done, 1)

            for i in range(NT):
                if i % GROUP == 0:
                    dve.wait_ge(in_x[i // GROUP], 16)
                dve.bn_stats(bn[:, i, :], xs[:, i, :]).then_inc(bn_done, 1)
            norm(0)
            dve.wait_ge(a0_kv, 1)
            dve.wait_ge(in_bias, bias_at[0])
            link(dve.tensor_tensor(k0[:, :], ps[:, 4, 0:D], brow0[:, 0, :], ALU.add))
            dve.tensor_scalar(k0_min[:, :], k0[:, :], 0.0, None, ALU.min).then_inc(a0_kmin, 1)
            dve.tensor_tensor(v0[:, :], ps[:, 5, 0:D], brow0[:, 1, :], ALU.add).then_inc(a0_k, 1)
            dve.wait_ge(a0_kexp, 1)
            dve.scalar_tensor_tensor(out=k0[:, :], in0=k0[:, :], scalar=0.0, in1=k0_min[:, :], op0=ALU.max, op1=ALU.add).then_inc(a0_k, 1)
            dve.wait_ge(a0_num, 1)
            dve.tensor_copy(kv0[:, :, :, :], ps[:, 6:8, :].rearrange("p b (k e) -> p b k e", k=KD)).then_inc(a0_kvcopy, 1)
            dve.tensor_copy(ksum0[:, :, :], ps[:, 4:6, 0:KD]).then_inc(a0_den, 1)
            dve.wait_ge(a0_den, 1)
            dve.wait_ge(a0_bo, NT)
            def tiles_of(s):
                j, b = divmod(s, B)
                return range((j + b * (NG // B)) * GROUP, (j + b * (NG // B) + 1) * GROUP)

            def residual(s):
                dve.wait_ge(a0_proj, s + 1)
                for t, tile in enumerate(tiles_of(s)):
                    dve.tensor_tensor(lnx[:, tile, :], lnx[:, tile, :], ps[:, 4 + t // 2, (t % 2) * D:(t % 2 + 1) * D],
                                      ALU.add).then_inc(a0_res, 2 if t == GROUP - 1 else 1)

            def sums(s):
                dve.wait_ge(a0_res, 8 * (s + 1))
                for tile in tiles_of(s):
                    dve.bn_stats(bn[:, tile, :], lnx[:, tile, :]).then_inc(bn_done, 1)

            for s in range(NG):
                dve.wait_ge(a0_q, s + 1)
                for c in range(KD):
                    dve.tensor_scalar(q_min[:, c, :], ps[:, c, :], bcol0[:, c:c + 1], 0.0, ALU.add, ALU.min).then_inc(a0_qmin, 1)
                dve.wait_ge(a0_qexp, 3 * s + 3)
                dve.tensor_tensor(q_relu[:, :, :], q_relu[:, :, :], q_min[:, :, :], ALU.add).then_inc(a0_den, 1)
                if s > 0:
                    residual(s - 1)
                dve.wait_ge(a0_den, s + 2)
                for c in range(KD):
                    dve.tensor_scalar(q_den[:, c, :], q_relu[:, c, :], ksum0[:, s % B, c:c + 1], 1e-6, ALU.mult, ALU.add).then_inc(a0_res, 1)
                dve.wait_ge(a0_res, 8 * s + 2)
                dve.reciprocal(q_den[:, :, :], q_den[:, :, :]).then_inc(a0_res, 1)
                dve.wait_ge(a0_res, 8 * s + 3)
                dve.wait_ge(a0_num, s + 2)
                dve.tensor_tensor(q_o[:, :, :], ps[:, 2:4, :], q_den[:, :, :], ALU.mult).then_inc(a0_o, 1)
                if s > 0:
                    sums(s - 1)
            residual(NG - 1)
            sums(NG - 1)
            stats(1)
            for i in range(NT):
                dve.tensor_scalar(lnx[:, i, :], lnx[:, i, :], st_mean[:, i:i + 1], st_rstd[:, i:i + 1],
                                  ALU.subtract, ALU.mult).then_inc(a0_nrm, 1)
            dve.wait_ge(a0_bo, 2 * NT)
            for i in range(NT):
                dve.wait_ge(a0_gam, i + 1)
                dve.tensor_tensor(xs[:, i, :], xs[:, i, :], lnx[:, i, :], ALU.add).then_inc(x_done, 1)
                if i > 0:
                    next_stats(0, i - 1)
            next_stats(0, NT - 1)

            def mha(layer, m, n):
                norm(n)
                dve.wait_ge(m_kt, KD * (m + 1))
                for b in range(B):
                    for c in range(KD):
                        dve.tensor_tensor(kblk[:, b, c, :, :], kt[:, c, b * S2:(b + 1) * S2].unsqueeze(1).to_broadcast([P, HC, S2]),
                                          hmask[:, :].unsqueeze(2).to_broadcast([P, HC, S2]), ALU.mult).then_inc(m_kblk, 1)
                dve.wait_ge(m_kv, m + 1)
                dve.wait_ge(m_tab, 5 * m + 3)
                dve.wait_ge(in_bias, bias_at[layer])
                for b in range(B):
                    for r in range(2):
                        h = slice(r * S2, (r + 1) * S2)
                        dve.tensor_tensor(vblk[h, b, :, r * HD:(r + 1) * HD],
                                          ps[h, 5, b * D:(b + 1) * D].rearrange("p (q r d) -> p q r d", r=2, d=HD)[:, :, r, :],
                                          brow[h, 0, :].rearrange("p (q r d) -> p q r d", r=2, d=HD)[:, :, r, :],
                                          ALU.add).then_inc(m_kblk, 1)
                dve.wait_ge(in_mask, 16 * MASKS[layer])
                if layer == 1:
                    nb = B
                    src = mask8[:, 0:B, :]
                else:
                    nb = NT
                    src = mask32[:, :, :]
                link(dve.tensor_scalar(bmask[:, 0:nb, :], src, 0.0, BIG, ALU.not_equal, ALU.mult))
                link(dve.tensor_scalar(bmask[:, 0:nb, :], bmask[:, 0:nb, :], MASKED[layer], None, ALU.add))
                base = NT * m

                def bound(i, j):
                    dve.wait_ge(m_s, base + i + 1)
                    row_ = i // TB if layer == 1 else i
                    dve.tensor_tensor(sc[:, j, :, :], ps[:, 1:3, :].rearrange("p c (h s) -> p (c h) s", h=HC),
                                      bmask[:, bass.ds(row_, 1), :].to_broadcast([P, H, S2]), ALU.min).then_inc(m_min, 1)

                def maxima(i, j):
                    dve.wait_ge(m_min, base + i + 1)
                    dve.tensor_reduce(smax[:, j, :], sc[:, j, :, :], AX.X, ALU.max).then_inc(m_max, 1)

                def probs(i):
                    dve.wait_ge(m_ptr, base + i + 1)
                    dve.tensor_copy(pt[:, 4:8, :], ps[:, 4, :].rearrange("p (q t) -> p q t", q=4)).then_inc(m_ptd, 1)

                def heads(i):
                    av = ps[:, 5, 0:PAIRS * VC].rearrange("p (q v) -> p q v", q=PAIRS)
                    dve.wait_ge(m_av, base + i + 1)
                    dve.reciprocal(rsum[:, :, :], av[:, :, 2 * HD:VC]).then_inc(m_rs, 1)
                    dve.wait_ge(m_rs, base + i + 1)
                    dve.tensor_tensor(oh[:, :].rearrange("p (q r d) -> p q r d", r=2, d=HD),
                                      av[:, :, 0:2 * HD].rearrange("p q (r d) -> p q r d", r=2),
                                      rsum[:, :, :].unsqueeze(3).to_broadcast([P, PAIRS, 2, HD]), ALU.mult).then_inc(m_oh, 1)

                def residual(i):
                    dve.wait_ge(m_proj, base + i + 1)
                    dve.scalar_tensor_tensor(out=xs[:, i, :], in0=ps[:, 7, 0:D], scalar=gates[:, layer:layer + 1], in1=xs[:, i, :],
                                             op0=ALU.mult, op1=ALU.add).then_inc(x_done, 1)

                def step(i, j, first=False, ahead=True):
                    probs(i)
                    if ahead:
                        bound(i + 2, j)
                    if not first:
                        residual(i - 1)
                    heads(i)
                    if not first:
                        next_stats(n, i - 1)
                    if ahead:
                        maxima(i + 2, j)
                for j in range(2):
                    bound(j, j)
                    maxima(j, j)
                dve.wait_ge(m_bo, (NT + 1) * (m + 1))
                step(0, 0, first=True)
                with dve.Fori(1, NT - 4, 2) as i:
                    step(i, 1)
                    step(i + 1, 0)
                step(NT - 3, 1)
                step(NT - 2, 0, ahead=False)
                step(NT - 1, 1, ahead=False)
                residual(NT - 1)
                next_stats(n, NT - 1)

            def ffn1(n):
                shared = CHUNKS["ffn1"]
                norm(n)
                for g in range(NG):
                    dve.wait_ge(xt_done, NG * n + g + 1)
                    tok = slice(g * GT, (g + 1) * GT)
                    dve.tensor_tensor(xTl[:, :, tok], ps[:, 2 * g:2 * g + 2, :], xTh[:, :, tok].bitcast(F32),
                                      ALU.subtract).then_inc(xl_done, 1)

                def product(c, f, start=False):
                    dve.wait_ge(f_act, c + 1)
                    if not start:
                        dve.wait_ge(f_hi, shared + c - 1)
                        dve.wait_ge(f_lo, shared + c - 1)
                    dve.tensor_tensor(h_32[:, f % 2, :], h_act[:, f % 2, :], ps[:, (f % 2) * 2 + 1, :], ALU.mult).then_inc(f_h, 1)

                def lower(c, f):
                    dve.wait_ge(f_hi, shared + c + 1)
                    dve.tensor_tensor(h_lo[:, f, :], h_32[:, f % 2, :], h_hi[:, f, :].bitcast(F32), ALU.subtract).then_inc(f_lo, 1)

                def add_up(blk, first=False):
                    dve.wait_ge(f_used, shared + blk * FH + FH + 1)
                    dve.wait_ge(f_yevac, blk + 1)
                    tok = bass.ts(blk % NG, GT)
                    if first:
                        dve.tensor_copy(xT[:, :, tok], ps[:, 4:6, :]).then_inc(f_yevac, 1)
                        return
                    dve.tensor_tensor(xT[:, :, tok], xT[:, :, tok], ps[:, 4:6, :], ALU.add).then_inc(f_yevac, 1)

                for f in range(FH):
                    product(f, f, start=f < 2)
                    if f > 0:
                        lower(f - 1, f - 1)
                def block_steps(blk, first=False):
                    for f in range(FH):
                        product(blk * FH + f, f)
                        lower(blk * FH + f - 1, (f - 1) % FH)
                        if f == 1:
                            add_up(blk - 1, first)
                for blk in range(1, NG + 1):
                    block_steps(blk, first=True)
                with dve.Fori(NG + 1, UNITS * NG) as blk:
                    block_steps(blk)
                lower(UNITS * NG * FH - 1, FH - 1)
                add_up(UNITS * NG - 1)
                for i in range(NT):
                    dve.wait_ge(f_back, i + 1)
                    dve.scalar_tensor_tensor(out=xs[:, i, :], in0=ps[:, i % 4, 0:D], scalar=gates[:, 5:6], in1=xs[:, i, :],
                                             op0=ALU.mult, op1=ALU.add).then_inc(x_done, 1)
                    if i > 0:
                        next_stats(n, i - 1)
                next_stats(n, NT - 1)

            def per_token(v, k=E):
                return v.unsqueeze(2).to_broadcast([P, NT, k])

            def per_expert(v):
                return v.unsqueeze(1).to_broadcast([P, NT, E])

            def choose(top, oh):
                link(dve.tensor_reduce(top, r_p[:, :, :], AX.X, ALU.max))
                link(dve.tensor_tensor(r_key[:, :, :], r_p[:, :, :], per_token(top), ALU.is_equal))
                link(dve.tensor_tensor(r_key[:, :, :], r_key[:, :, :], per_expert(desc[:, :]), ALU.mult))
                link(dve.tensor_reduce(r_k[:, :], r_key[:, :, :], AX.X, ALU.max))
                link(dve.tensor_tensor(oh, r_key[:, :, :], per_token(r_k[:, :]), ALU.is_equal))

            def first_rows_of_items():
                def pair(u, v, op):
                    return dve.tensor_tensor(r_grid[:, :, :], u.unsqueeze(2).to_broadcast([P, NT, E]), v.unsqueeze(1).to_broadcast([P, NT, E]), op)

                def square(u, v, op):
                    return dve.tensor_tensor(r_grid[:, 0:E, :], u.unsqueeze(2).to_broadcast([P, E, E]), v.unsqueeze(1).to_broadcast([P, E, E]), op)
                link(dve.tensor_copy(r_count[:, :], ps[:, 6, 0:E]))
                link(square(r_count[:, :], steps[:, :], ALU.is_gt))
                link(dve.tensor_reduce(r_items[:, :], r_grid[:, 0:E, :], AX.X, ALU.add))
                link(square(desc[:, :], desc[:, :], ALU.is_le))
                link(dve.tensor_tensor(r_grid[:, 0:E, :], r_grid[:, 0:E, :], r_items[:, :].unsqueeze(1).to_broadcast([P, E, E]), ALU.mult))
                link(dve.tensor_reduce(r_upto[:, :], r_grid[:, 0:E, :], AX.X, ALU.add))
                link(pair(item_no[:, :], r_upto[:, :], ALU.is_ge))
                link(dve.tensor_reduce(r_m[:, :], r_grid[:, :, :], AX.X, ALU.add))
                link(dve.tensor_scalar(item_expert[:, :], r_m[:, :], float(E - 1), None, ALU.min))
                link(dve.tensor_tensor(r_count[:, :], r_upto[:, :], r_items[:, :], ALU.subtract))
                link(dve.tensor_scalar(r_count[:, :], r_count[:, :], float(IR[0]), -1.0, ALU.mult, ALU.add))
                return r_count[:, :]

            def route(layer, nth):
                logits = ps[:, 4, 0:NT * E].rearrange("p (t e) -> p t e", t=NT)
                dve.wait_ge(r_logits, nth + 1)
                if layer == 2:
                    link(dve.tensor_copy(r_p[:, :, :], logits))
                else:
                    link(dve.tensor_tensor(r_p[:, :, :], logits, per_expert(rb[:, layer, :]), ALU.add))
                link(dve.tensor_reduce(r_m[:, :], r_p[:, :, :], AX.X, ALU.max))
                dve.tensor_tensor(r_p[:, :, :], r_p[:, :, :], per_token(r_m[:, :]), ALU.subtract).then_inc(r_sub, 1)
                dve.wait_ge(r_exp, nth + 1)
                link(dve.tensor_reduce(r_s[:, :], r_e[:, :, :], AX.X, ALU.add))
                link(dve.reciprocal(r_s[:, :], r_s[:, :]))
                link(dve.tensor_tensor(r_p[:, :, :], r_e[:, :, :], per_token(r_s[:, :]), ALU.mult))
                choose(r_top[:, 0, :], r_oh1[:, :, :])
                if TOPK[layer] == 2:
                    link(dve.scalar_tensor_tensor(out=r_p[:, :, :], in0=r_oh1[:, :, :], scalar=-2.0, in1=r_p[:, :, :], op0=ALU.mult, op1=ALU.add))
                    choose(r_top[:, 1, :], r_oh2[:, :, :])
                    dve.tensor_tensor(mask_b[:, :, :], r_oh1[:, :, :], r_oh2[:, :, :], ALU.add).then_inc(r_mask, 1)
                    link(dve.tensor_tensor(r_s[:, :], r_top[:, 0, :], r_top[:, 1, :], ALU.add))
                    link(dve.reciprocal(r_s[:, :], r_s[:, :]))
                    link(dve.tensor_tensor(r_top[:, :, :], r_top[:, :, :], r_s[:, :].unsqueeze(1).to_broadcast([P, 2, NT]), ALU.mult))
                else:
                    dve.tensor_copy(mask_b[:, :, :], r_oh1[:, :, :]).then_inc(r_mask, 1)
                rank = ps[:, 5, 0:NT * E].rearrange("p (t e) -> p t e", t=NT)
                dve.wait_ge(r_rank, nth + 1)
                first = first_row[:, 0:E]
                if layer == 0:
                    first = first_rows_of_items()
                link(dve.tensor_tensor(r_pos[:, :, :], rank, per_expert(first), ALU.add))
                link(dve.tensor_scalar(r_keep[:, :, :], rank, float(CAP[layer] if layer else T), None, ALU.is_le))
                for c, oh in enumerate((r_oh1, r_oh2)[:TOPK[layer]]):
                    link(dve.tensor_tensor(oh[:, :, :], oh[:, :, :], r_keep[:, :, :], ALU.mult))
                    link(dve.tensor_reduce(r_kept[:, c, :], oh[:, :, :], AX.X, ALU.add))
                    link(dve.tensor_tensor(oh[:, :, :], oh[:, :, :], r_pos[:, :, :], ALU.mult))
                    link(dve.tensor_reduce(r_slot[:, c, :], oh[:, :, :], AX.X, ALU.add))
                k = slice(0, TOPK[layer])
                dve.tensor_copy(gidx[:, k, :], r_slot[:, k, :]).then_inc(link_s, 1)
                links[0] += 1
                link(dve.scalar_tensor_tensor(out=r_slot[:, k, :], in0=r_kept[:, k, :], scalar=-FAR, in1=r_slot[:, k, :], op0=ALU.mult, op1=ALU.add))
                dve.tensor_scalar(sidx[:, k, :], r_slot[:, k, :], FAR, None, ALU.add).then_inc(r_idx, 1)
                link(dve.scalar_tensor_tensor(out=r_w[:, k, :], in0=r_top[:, k, :], scalar=gates[:, 4 + layer:5 + layer],
                                              in1=r_kept[:, k, :], op0=ALU.mult, op1=ALU.mult))

            def moe(layer, n):
                name = f"ffn{layer}"
                nth, cap, items, tiles = MOE.index(layer), CAP[layer], ITEMS[layer], IR[layer] // P
                norm(n)
                route(layer, nth)
                if cap < IR[layer]:
                    link(dve.memset(y_t[:, :, cap:SLOTS], 0.0))

                def rows_lower(e, s):
                    dve.wait_ge(x_hi, EXPERTS[name] + e + 1)
                    tok = slice(s * GT * 2, s * GT * 2 + cap)
                    dve.tensor_tensor(xTl[:, :, tok], ps[:, 6:8, 0:cap], xTh[:, :, tok].bitcast(F32), ALU.subtract).then_inc(x_lo, 1)

                def lower(e, f):
                    dve.wait_ge(f_hi, CHUNKS[name] + e * FC + f + 1)
                    dve.tensor_tensor(h_lo[:, f % 4, 0:cap], h_32[:, f % 2, 0:cap], h_hi[:, f % 4, 0:cap].bitcast(F32), ALU.subtract).then_inc(f_lo, 1)

                def output(e, s):
                    ex = dve.value_load(item_expert[0:1, bass.ds(e, 1)], min_val=0, max_val=E - 1) if layer == 0 else e
                    dve.wait_ge(f_used, CHUNKS[name] + (e + 1) * FC + 1)
                    dve.tensor_tensor(y_t[:, :, 0:cap], ps[:, 2 + 2 * s:4 + 2 * s, 0:cap],
                                      b2c[:, layer, bass.ds(ex * KD, KD)].unsqueeze(2).to_broadcast([P, KD, cap]), ALU.add).then_inc(y_out, 1)

                def output_rows(e, s):
                    dve.wait_ge(y_tr, EXPERTS[name] + e + 1)
                    dve.wait_ge(y_st[s], 16 * (ROW_LOADS[layer][s] + 1) + 8 * (e - s))
                    two = ps[:, 6, :].rearrange("p (j d) -> p j d", j=2)
                    dve.tensor_copy(y_row[:, s, 0:tiles - 1, :], two[:, 0:tiles - 1, :]).then_inc(y_half, 1)
                    dve.wait_ge(y_half, EXPERTS[name] + e + 1)
                    dve.tensor_copy(y_row[:, s, tiles - 1, :], ps[:, 7, 0:D] if tiles == 3 else two[:, 1, :]).then_inc(y_copied, 1)

                def expert(e, s, start=False, end=False):
                    for f in range(FC):
                        if f > 0:
                            lower(e, f - 1)
                        elif not start:
                            lower(e - 1, FC - 1)
                        if f == LAG and not start:
                            output(e - 1, 1 - s)
                        if f == LAG + 3 and not start:
                            output_rows(e - 1, 1 - s)
                        if f == 2 and not end:
                            rows_lower(e + 1, 1 - s)
                rows_lower(0, 0)
                expert(0, 0, start=True)
                pairs_end = items - 1 - items % 2 * 2
                with dve.Fori(1, pairs_end, 2) as e:
                    expert(e, 1)
                    expert(e + 1, 0)
                for e in range(pairs_end + items % 2, items):
                    expert(e, e % 2, end=e == items - 1)
                last_slot = (items - 1) % 2
                lower(items - 1, FC - 1)
                output(items - 1, last_slot)
                output_rows(items - 1, last_slot)
                for g in range(NG):
                    dve.wait_ge(fetched[g], 16 * FETCHED[layer])
                    for i in range(g * GROUP, (g + 1) * GROUP):
                        ins = dve.scalar_tensor_tensor(out=xs[:, i, :], in0=lnx[:, i, :], scalar=r_w[:, 0, i:i + 1], in1=xs[:, i, :],
                                                       op0=ALU.mult, op1=ALU.add)
                        if TOPK[layer] == 2:
                            link(ins)
                            ins = dve.scalar_tensor_tensor(out=xs[:, i, :], in0=y_second[:, i, :], scalar=r_w[:, 1, i:i + 1], in1=xs[:, i, :],
                                                           op0=ALU.mult, op1=ALU.add)
                        ins.then_inc(x_done, 1)
                        if i > 0:
                            next_stats(n, i - 1)
                next_stats(n, NT - 1)

            if "ffn0" in N:
                moe(0, N["ffn0"])
            if "attn1" in N:
                mha(1, 0, N["attn1"])
            if "ffn1" in N:
                ffn1(N["ffn1"])

            def attn2(n):
                norm(n)
                dve.wait_ge(in_wat, 64 * WAT[2])
                dve.wait_ge(in_mask, 16 * MASKS[2])
                dve.tensor_tensor(wo8[:, :], wat[:, 3, 0, :], wat[:, 3, 1, :], ALU.add).then_inc(a2_dve, 1)
                link(dve.tensor_scalar(bmask[:, 0:TB, :], mask8[:, :, :], 0.0, BIG, ALU.is_equal, ALU.mult))
                dve.wait_ge(a2_act, 1)
                dve.tensor_scalar(bmask[:, 0:TB, :], bmask[:, 0:TB, :], MASKED[2], None, ALU.add).then_inc(a2_dve, 1)
                dve.wait_ge(in_a2, 48)
                dve.wait_ge(a2_pool, 3)
                dve.wait_ge(a2_pe, 2)
                dve.tensor_scalar(khT[:, :, :], ps[0:HD, 5, 0:P].rearrange("p (b s) -> p b s", b=B), bh[:, 1:2], 0.25, ALU.add, ALU.mult).then_inc(a2_dve, 1)
                for b in range(B):
                    dve.tensor_tensor(vh[:, b, 0:HD], ps[:, 6, b * HD:(b + 1) * HD], bvh[:, :], ALU.add).then_inc(a2_dve, 1)
                dve.wait_ge(a2_pe, 7)
                dve.wait_ge(a2_dve, 2)
                for b in range(B):
                    dve.tensor_tensor(sc[:, 0, b * TB:(b + 1) * TB, :], ps[:, 4 + b, :].rearrange("p (t s) -> p t s", t=TB),
                                      bmask[:, 0:TB, :], ALU.min).then_inc(a2_dve, 1)
                dve.wait_ge(a2_dve, 7)
                dve.tensor_reduce(smax[:, 0, :], sc[:, 0, :, :], AX.X, ALU.max).then_inc(a2_dve, 1)
                dve.wait_ge(a2_dve, 8)
                dve.tensor_tensor(sc[:, 0, :, :], sc[:, 0, :, :], smax[:, 0, :].unsqueeze(2).to_broadcast([P, H, S2]), ALU.subtract).then_inc(a2_dve, 1)
                dve.wait_ge(a2_pe, 8)
                dve.tensor_copy(pt[:, 4:8, :], ps[:, 7, :].rearrange("p (q t) -> p q t", q=4)).then_inc(a2_dve, 1)
                dve.wait_ge(a2_pe, 9)
                av = ps[:, 0:2, 0:PAIRS * (HD + 1)].rearrange("p r (q v) -> p r q v", q=PAIRS)
                dve.reciprocal(rs2[:, :, :], av[:, :, :, HD]).then_inc(a2_dve, 1)
                dve.wait_ge(a2_dve, 11)
                for r in range(2):
                    dve.tensor_tensor(oh8[:, :, :, :].rearrange("p (q r) h j -> p q r h j", r=2)[:, :, r, :, :],
                                      av[:, r, :, 0:HD].unsqueeze(2).to_broadcast([P, PAIRS, HC, HD]),
                                      rs2[:, r, :].unsqueeze(2).unsqueeze(3).to_broadcast([P, PAIRS, HC, HD]), ALU.mult).then_inc(a2_dve, 1)
                for i in range(NT):
                    dve.wait_ge(a2_pe, 9 + (2 * i + 3 if i < NT - 1 else 2 * NT))
                    dve.scalar_tensor_tensor(out=xs[:, i, :], in0=ps[:, 4 + i % 2, 0:D], scalar=gates[:, 2:3], in1=xs[:, i, :],
                                             op0=ALU.mult, op1=ALU.add).then_inc(x_done, 1)
                    if i > 0:
                        next_stats(n, i - 1)
                next_stats(n, NT - 1)

            if "attn2" in N:
                attn2(N["attn2"])
            if "ffn2" in N:
                moe(2, N["ffn2"])
            if "attn3" in N:
                mha(3, 1, N["attn3"])
            if "ffn3" in N:
                moe(3, N["ffn3"])


ATTN = {0: [f"L0_xattn_W{n}" for n in "qkvo"], 1: [f"L1_xattn_W{n}" for n in "qkvo"], 3: [f"L3_xattn_w{n}_kernel" for n in "qkvo"]}
INS = ["x", "ctx_1024", "mask_BxS2_bf1", "mask_SxS2_bk1", "mask_BxSxS2_ik1", "g_xattn", "g_ffn",
       "L0_xattn_bk", "L0_xattn_bv", "L0_xattn_bo", "L0_xattn_gamma", "L0_xattn_beta",
       "L2_xattn_bv_h", "L0_ffn_br", "L3_ffn_gate_b", "L1_ffn_Wg", "L1_ffn_Wu", "L1_ffn_Wd"]
SUBS = ["attn0", "ffn0", "attn1", "ffn1", "attn2", "ffn2", "attn3", "ffn3"]


def kernel(**inputs):
    import concourse.bacc as bacc
    from concourse.bass_utils import run_bass_kernel_spmd as run

    def arr(n):
        return np.ascontiguousarray(inputs[n])

    def cols(n):
        return np.ascontiguousarray(arr(n).reshape(-1, P).T)

    arrays = {n: arr(n) for n in INS}
    arrays["L0_xattn_bq"] = cols("L0_xattn_bq")
    for layer, names in ((1, "L1_xattn_b{}"), (3, "L3_xattn_w{}_bias")):
        for n in "vo":
            arrays[f"L{layer}_b{n}"] = arr(names.format(n))
        for n in "qk":
            arrays[f"L{layer}_b{n}"] = cols(names.format(n))
    for layer in (0, 1):
        arrays[f"attn{layer}"] = np.stack([arr(n).T for n in ATTN[layer]])
    arrays["attn2"] = np.stack([arr(f"L2_xattn_W{n}").T for n in "qkv"] + [arr("L2_xattn_Wo")])
    arrays["attn2_heads"] = np.stack([arr(f"L2_xattn_w{n}_h") for n in "qkv"])
    arrays["attn2_bias"] = np.stack([arr(f"L2_xattn_b{n}_h") for n in "qk"], axis=1)
    for layer, (router, w, b) in {0: ("L0_ffn_Wr", "W", "b"), 2: ("L2_ffn_router_w", "w", "b"), 3: ("L3_ffn_gate_w", "w", "b")}.items():
        arrays[f"router{layer}"] = arr(router).T if layer == 2 else arr(router)
        arrays[f"router{layer}"] = np.ascontiguousarray(arrays[f"router{layer}"])
        for i in "12":
            arrays[f"L{layer}_w{i}"] = arr(f"L{layer}_ffn_{w}{i}")
            arrays[f"b{i}_{layer}"] = cols(f"L{layer}_ffn_b{i}")
    arrays["attn3"] = np.stack([arr(n) for n in ATTN[3]])
    nc = bacc.Bacc("TRN2", target_bir_lowering=False, num_devices=1)
    a = {n: nc.dram_tensor(f"in_{n}", v.shape, mybir.dt.from_np(v.dtype), kind="ExternalInput").ap() for n, v in arrays.items()}
    arrays = {f"in_{n}": v for n, v in arrays.items()}
    out = nc.dram_tensor("out", (B, SEQ, D), F32, kind="ExternalOutput").ap()
    build(nc, a, out, SUBS)
    r = run(nc, [arrays], core_ids=[0])
    return r.results[0]["out"]
```
